# Optimizing a Trainium2 kernel written in Bass

```python
import numpy as np
import jax
import jax.numpy as jnp

def _softmax(x, axis=-1):
    return jax.nn.softmax(x, axis=axis)

def _gelu(x):
    return jax.nn.gelu(x, approximate=True)

def _silu(x):
    return jax.nn.silu(x)

def _sigmoid(x):
    return jax.nn.sigmoid(x)

def _layernorm(x, axis=-1, eps=1e-05):
    m = jnp.mean(x, axis=axis, keepdims=True)
    v = jnp.var(x, axis=axis, keepdims=True)
    return (x - m) / jnp.sqrt(v + eps)

def _scatter_add(tgt, idx, src, axis=0):
    return tgt.at[idx].add(src)

def _segment_sum(src, seg, n):
    return jax.ops.segment_sum(src, seg, n)
kernel_name = 'mk_macaron_d1_jaxref_r8_c7bf56'

def setup_inputs(seed: int=0):
    np.random.seed(seed)
    _w = jnp.asarray

    def _L0_attn_setup():
        import jax, jax.numpy as jnp
        import numpy as np
        D_MODEL = 128
        D_STATE = 64
        HEADDIM = 64
        EXPAND = 2
        D_INNER = D_MODEL * EXPAND
        NHEADS = D_INNER // HEADDIM
        D_IN_PROJ = 2 * D_INNER + 2 * D_STATE + NHEADS
        BATCH, SEQLEN = (4, 512)

        def layernorm(x, w, b, eps=1e-05):
            mu = jnp.mean(x, axis=-1, keepdims=True)
            var = jnp.mean(jnp.square(x - mu), axis=-1, keepdims=True)
            return (x - mu) * jax.lax.rsqrt(var + eps) * w + b

        def _selective_scan(x_multi, A, Bm, Cm, dt):
            Bb, L, H, P = x_multi.shape
            N = Bm.shape[-1]
            dA = jnp.minimum(jnp.exp(dt * A[None, None, :]), 0.99)

            def step(h, inp):
                x_t, B_t, C_t, dA_t = inp
                dBx = jnp.einsum('bhp,bn->bhpn', x_t, B_t)
                h = jnp.clip(dA_t[:, :, None, None] * h + dBx, -10.0, 10.0)
                y_t = jnp.einsum('bn,bhpn->bhp', C_t, h)
                return (h, y_t)
            h0 = jnp.zeros((Bb, H, P, N), dtype=x_multi.dtype)
            xs = (jnp.moveaxis(x_multi, 1, 0), jnp.moveaxis(Bm, 1, 0), jnp.moveaxis(Cm, 1, 0), jnp.moveaxis(dA, 1, 0))
            _, y = jax.lax.scan(step, h0, xs)
            return jnp.moveaxis(y, 0, 1)
        key = jax.random.key(seed)
        ks = jax.random.split(key, 5)
        x = jax.random.normal(ks[0], (BATCH, SEQLEN, D_MODEL), dtype=jnp.float32)
        in_proj_w = jax.random.normal(ks[1], (D_IN_PROJ, D_MODEL), dtype=jnp.float32) * 0.5 * np.sqrt(2.0 / (D_IN_PROJ + D_MODEL))
        out_proj_w = jax.random.normal(ks[2], (D_MODEL, D_INNER), dtype=jnp.float32) * 0.5 * np.sqrt(2.0 / (D_MODEL + D_INNER))
        A_log = jnp.log(jnp.arange(1, NHEADS + 1, dtype=jnp.float32))
        dt_bias = jax.random.normal(ks[3], (NHEADS,), dtype=jnp.float32) * 0.01 + 0.1
        Dparam = jnp.ones((NHEADS,), dtype=jnp.float32)
        return {'x': x, 'in_proj_w': in_proj_w, 'out_proj_w': out_proj_w, 'A_log': A_log, 'dt_bias': dt_bias, 'Dparam': Dparam, 'ln_w': jnp.ones((D_INNER,), jnp.float32), 'ln_b': jnp.zeros((D_INNER,), jnp.float32), 'ni_w': jnp.ones((D_MODEL,), jnp.float32), 'ni_b': jnp.zeros((D_MODEL,), jnp.float32), 'no_w': jnp.ones((D_MODEL,), jnp.float32), 'no_b': jnp.zeros((D_MODEL,), jnp.float32)}
    _L0_attn_in = _L0_attn_setup()

    def _L0_ffn_setup():
        import jax, jax.numpy as jnp
        import numpy as np
        E, K, H, F, R = (8, 2, 128, 256, 64)
        B, S = (2, 256)
        key = jax.random.key(seed)
        k0, k1, k2, k3, k4 = jax.random.split(key, 5)
        return {'hidden_states': jax.random.normal(k0, (B, S, H), dtype=jnp.float32), 'W_A': jax.random.normal(k1, (E, R, H), dtype=jnp.float32) * 0.02, 'W_B': jax.random.normal(k2, (E, F, R), dtype=jnp.float32) * 0.02, 'W_up': jax.random.normal(k3, (E, F, H), dtype=jnp.float32) * 0.02, 'W_down': jax.random.normal(k4, (E, H, F), dtype=jnp.float32) * 0.02}
    _L0_ffn_in = _L0_ffn_setup()
    _d = {'L0_attn_x': _L0_attn_in['x'], 'L0_attn_in_proj_w': _L0_attn_in['in_proj_w'], 'L0_attn_out_proj_w': _L0_attn_in['out_proj_w'], 'L0_attn_A_log': _L0_attn_in['A_log'], 'L0_attn_dt_bias': _L0_attn_in['dt_bias'], 'L0_attn_Dparam': _L0_attn_in['Dparam'], 'L0_attn_ln_w': _L0_attn_in['ln_w'], 'L0_attn_ln_b': _L0_attn_in['ln_b'], 'L0_attn_ni_w': _L0_attn_in['ni_w'], 'L0_attn_ni_b': _L0_attn_in['ni_b'], 'L0_attn_no_w': _L0_attn_in['no_w'], 'L0_attn_no_b': _L0_attn_in['no_b'], 'L0_ffn_W_A': _L0_ffn_in['W_A'], 'L0_ffn_W_B': _L0_ffn_in['W_B'], 'L0_ffn_W_up': _L0_ffn_in['W_up'], 'L0_ffn_W_down': _L0_ffn_in['W_down']}
    _x0 = _d['L0_attn_x']
    _d['L0_attn_x'] = jax.random.normal(jax.random.fold_in(jax.random.key(seed), 1), (16, 512, 128), dtype=_x0.dtype)
    del _x0
    return _d

def reference(L0_attn_x, L0_attn_in_proj_w, L0_attn_out_proj_w, L0_attn_A_log, L0_attn_dt_bias, L0_attn_Dparam, L0_attn_ln_w, L0_attn_ln_b, L0_attn_ni_w, L0_attn_ni_b, L0_attn_no_w, L0_attn_no_b, L0_ffn_W_A, L0_ffn_W_B, L0_ffn_W_up, L0_ffn_W_down):

    def _L0_attn_ref(x, in_proj_w, out_proj_w, A_log, dt_bias, Dparam, ln_w, ln_b, ni_w, ni_b, no_w, no_b):
        import jax, jax.numpy as jnp
        import numpy as np
        D_MODEL = 128
        D_STATE = 64
        HEADDIM = 64
        EXPAND = 2
        D_INNER = D_MODEL * EXPAND
        NHEADS = D_INNER // HEADDIM
        D_IN_PROJ = 2 * D_INNER + 2 * D_STATE + NHEADS
        BATCH, SEQLEN = (4, 512)

        def layernorm(x, w, b, eps=1e-05):
            mu = jnp.mean(x, axis=-1, keepdims=True)
            var = jnp.mean(jnp.square(x - mu), axis=-1, keepdims=True)
            return (x - mu) * jax.lax.rsqrt(var + eps) * w + b

        def _selective_scan(x_multi, A, Bm, Cm, dt):
            Bb, L, H, P = x_multi.shape
            N = Bm.shape[-1]
            dA = jnp.minimum(jnp.exp(dt * A[None, None, :]), 0.99)

            def step(h, inp):
                x_t, B_t, C_t, dA_t = inp
                dBx = jnp.einsum('bhp,bn->bhpn', x_t, B_t)
                h = jnp.clip(dA_t[:, :, None, None] * h + dBx, -10.0, 10.0)
                y_t = jnp.einsum('bn,bhpn->bhp', C_t, h)
                return (h, y_t)
            h0 = jnp.zeros((Bb, H, P, N), dtype=x_multi.dtype)
            xs = (jnp.moveaxis(x_multi, 1, 0), jnp.moveaxis(Bm, 1, 0), jnp.moveaxis(Cm, 1, 0), jnp.moveaxis(dA, 1, 0))
            _, y = jax.lax.scan(step, h0, xs)
            return jnp.moveaxis(y, 0, 1)
        Bb, L, Dm = x.shape
        x_norm = layernorm(x, ni_w, ni_b)
        zxbcdt = jnp.einsum('bld,ed->ble', x_norm, in_proj_w)
        z = zxbcdt[..., :D_INNER]
        x_ssm = zxbcdt[..., D_INNER:2 * D_INNER]
        Bm = zxbcdt[..., 2 * D_INNER:2 * D_INNER + D_STATE]
        Cm = zxbcdt[..., 2 * D_INNER + D_STATE:2 * D_INNER + 2 * D_STATE]
        dt = zxbcdt[..., 2 * D_INNER + 2 * D_STATE:]
        dt = jnp.clip(jax.nn.softplus(dt + dt_bias[None, None, :]), 0.001, 0.1)
        A = -jnp.exp(A_log)
        x_multi = x_ssm.reshape(Bb, L, NHEADS, HEADDIM)
        y = _selective_scan(x_multi, A, Bm, Cm, dt)
        y = y + x_multi * Dparam[None, None, :, None]
        y = y.reshape(Bb, L, D_INNER)
        y = y * jax.nn.silu(z)
        y = layernorm(y, ln_w, ln_b)
        y = jnp.einsum('ble,de->bld', y, out_proj_w)
        y = jnp.clip(y, -10.0, 10.0)
        y = layernorm(y, no_w, no_b)
        return y

    def _L0_ffn_ref(hidden_states, W_A, W_B, W_up, W_down):
        import jax, jax.numpy as jnp
        import numpy as np
        E, K, H, F, R = (8, 2, 128, 256, 64)
        B, S = (2, 256)
        orig_shape = hidden_states.shape
        x = hidden_states.reshape(-1, orig_shape[-1])
        num_experts = W_A.shape[0]
        gate_hidden = jnp.einsum('nh,erh->ner', x, W_A)
        scores = jnp.sqrt(jnp.sum(gate_hidden * gate_hidden, axis=-1))
        topk_scores, topk_idx = jax.lax.top_k(scores, K)
        topk_w = jax.nn.softmax(topk_scores, axis=-1)
        w_full = jnp.sum(jax.nn.one_hot(topk_idx, num_experts, dtype=topk_w.dtype) * topk_w[..., None], axis=1)
        g = jnp.einsum('ner,efr->nef', gate_hidden, W_B)
        up = jnp.einsum('nh,efh->nef', x, W_up)
        y = jnp.einsum('nef,ehf->neh', jax.nn.silu(g) * up, W_down)
        out = jnp.einsum('neh,ne->nh', y, w_full)
        return out.reshape(orig_shape)
    x = L0_attn_x
    x = x + 0.5 * _L0_ffn_ref(_layernorm(x, axis=-1), L0_ffn_W_A, L0_ffn_W_B, L0_ffn_W_up, L0_ffn_W_down)
    x = x + _L0_attn_ref(_layernorm(x, axis=-1), L0_attn_in_proj_w, L0_attn_out_proj_w, L0_attn_A_log, L0_attn_dt_bias, L0_attn_Dparam, L0_attn_ln_w, L0_attn_ln_b, L0_attn_ni_w, L0_attn_ni_b, L0_attn_no_w, L0_attn_no_b)
    x = x + 0.5 * _L0_ffn_ref(_layernorm(x, axis=-1), L0_ffn_W_A, L0_ffn_W_B, L0_ffn_W_up, L0_ffn_W_down)
    return x

_drawn_inputs = setup_inputs


def setup_inputs(seed=0):
    import zlib

    import numpy as np

    out = dict(_drawn_inputs(seed))
    spreads = {'L0_attn_Dparam': (1.0, 0.2),
     'L0_attn_ln_w': (1.0, 0.2),
     'L0_attn_ln_b': (0.0, 0.1),
     'L0_attn_ni_w': (1.0, 0.2),
     'L0_attn_ni_b': (0.0, 0.1),
     'L0_attn_no_w': (1.0, 0.2),
     'L0_attn_no_b': (0.0, 0.1)}
    factors = {'L0_ffn_W_A': 8.0, 'L0_ffn_W_B': 8.0, 'L0_ffn_W_up': 8.0, 'L0_ffn_W_down': 8.0}
    for name, (base, spread) in spreads.items():
        noise = np.random.default_rng([zlib.crc32(name.encode()), seed]).standard_normal(out[name].shape)
        drawn = base * np.exp(spread * noise) if base else spread * noise
        out[name] = jnp.asarray(drawn.astype(out[name].dtype))
    for name, factor in factors.items():
        out[name] = (out[name] * factor).astype(out[name].dtype)
    return out
```

```python
import numpy as np
import concourse.bass as bass
from concourse import mybir
from contextlib import ExitStack

F32 = mybir.dt.float32
BF16 = mybir.dt.bfloat16
I32 = mybir.dt.int32
U32 = mybir.dt.uint32
ALU = mybir.AluOpType
ACT = mybir.ActivationFunctionType
AX = mybir.AxisListType

P = 128
BATCH, SEQ, D = 16, 512, 128
TOK = BATCH * SEQ
TILES = TOK // P
GT = SEQ // P
GROUPS = TILES // GT
E, K2, R, F = 8, 2, 64, 256
INNER, STATE, HEADS, HD = 256, 64, 4, 64
REG = TOK + P
ETILES = TOK * K2 // P + E
SPARE = E * P
EPS = 1e-5
MAGIC = float(0x5F3759DF)
NZX = 2 * INNER
NBD = STATE + HEADS

CUM = GT * NBD
CARRY = 256
BLOCK = 16
STATE_MAX = 9.8
DECAY_MIN = -0.5
LOADS = 14
LOG_CAP = float(np.log(0.99))

C_ID, C_TRI, C_STRICT, C_LAST = 0, P, 2 * P, 3 * P
C_IOTA = 4 * P
C_REG = C_IOTA + E
C_PART = C_REG + E
C_ROW = C_PART + 1
C_N = C_ROW + ETILES


class Chain:

    def __init__(self, eng, sem):
        self.eng, self.sem, self.n = eng, sem, 0

    def __call__(self, ins):
        self.n += 1
        return ins.then_inc(self.sem, 1)

    def sync(self):
        self.eng.wait_ge(self.sem, self.n)

    def restart(self):
        self.sync()
        self.eng.sem_clear(self.sem)
        self.n = 0


def macaron(nc, x, consts, wA_T, wA, wB_T, wUp_T, wDn_T, in_T, out_T, vecs, dt_bias, A_log, Dparam,
            no_w, no_b, out, debug=None):
    ctx = ExitStack()
    with ctx:
        def sb(name, shape, dt=F32):
            return ctx.enter_context(nc.sbuf_tensor(name, shape, dt))

        def ps(name, shape=(P, 512), dt=F32):
            return ctx.enter_context(nc.psum_tensor(name, list(shape), dt))

        def sem(name):
            return ctx.enter_context(nc.semaphore(name))

        xg = [nc.dram_tensor(f"rows_by_expert{n}", (E * REG + SPARE, D), F32).ap() for n in range(2)]
        yg = [nc.dram_tensor(f"expert_results{n}", (ETILES * P, D), F32).ap() for n in range(2)]

        X = sb("X", [P, TILES, D])
        X2 = sb("X2", [P, TILES, D])
        cst = sb("cst", [P, C_N])
        WAT = sb("WAT", [P, E * R])
        work = sb("work", [P, 5, GT, INNER])
        wide = work[:, :, :, :].rearrange("p k t n -> p (k t n)")
        WBT, WA = wide[0:R, 0:E * F], wide[0:R, E * F:E * (F + D)]
        WUG = sb("WUG", [P, E, 2 * F])
        WDT = sb("WDT", [P, E, 2, D])
        WIN = sb("WIN", [P, NZX + NBD + STATE])
        WOUT = sb("WOUT", [P, 2, D])
        ident, tri = cst[:, C_ID:C_ID + P], cst[:, C_TRI:C_TRI + P]
        lastrow = cst[:, C_LAST:C_LAST + P]
        strict_bf = sb("strict_bf", [P, P], BF16)
        tri_bf = sb("tri_bf", [P, P], BF16)
        ones_bf = sb("ones_bf", [P, P], BF16)
        ones = sb("ones", [P, P])
        zeros = sb("zeros", [P, SPARE // P, D])
        vec = sb("vec", [P, 6])
        nAb = sb("nAb", [P, HEADS])
        dtb = sb("dtb", [P, HEADS])
        Dh = sb("Dh", [P, HEADS])
        Dbc = sb("Dbc", [P, INNER])
        now, nob = sb("now", [P, D]), sb("nob", [P, D])

        OH = sb("OH", [P, TILES * K2, E], BF16)
        SLOT = sb("SLOT", [P, TILES * K2])
        W12s = [sb(f"W12_{n}", [P, TILES, K2]) for n in range(2)]
        base = sb("base", [P, GT + 1, E])
        xn = sb("xn", [P, 4, GT, D])
        xT = sb("xT", [P, GT, P])
        sq = sb("sq", [P, GT, E * R])
        ss, sc = sb("ss", [P, GT, E]), sb("sc", [P, GT, E])
        nt1, nt2 = sb("nt1", [P, GT * E]), sb("nt2", [P, GT * E])
        mx, mi = sb("mx", [P, GT, 8]), sb("mi", [P, GT, 8], U32)
        mif = sb("mif", [P, GT, K2])
        pre = sb("pre", [P, GT, E])
        pick = sb("pick", [P, GT * K2, E])
        slot_u = [sb(f"slot_u{q}", [P, GT * K2], U32) for q in range(4)]
        slot_g = [sb(f"slot_g{n}", [P, GT * K2], U32) for n in range(2)]
        ediff, eexp, den = sb("ediff", [P, GT]), sb("eexp", [P, GT]), sb("den", [P, GT])
        st = sb("st", [P, GT, 6])
        mv = sb("mv", [P, GT, 2])
        lnv, lnr = sb("lnv", [P, GT]), sb("lnr", [P, GT])
        cnt, cnt_i, ntl, tend = sb("cnt", [P, E]), sb("cnt_i", [P, E], I32), sb("ntl", [P, E]), sb("tend", [P, E])
        toff, tadj = sb("toff", [P, E]), sb("tadj", [P, E])
        below = sb("below", [P, ETILES, E])
        row_f, exp_f = sb("row_f", [P, ETILES]), sb("exp_f", [P, ETILES])
        tab_row = sb("tab_row", [P, ETILES], I32)
        tab_up, tab_down = sb("tab_up", [P, ETILES + 4], I32), sb("tab_down", [P, ETILES + 4], I32)
        zidx = sb("zidx", [P, E], U32)
        xr = sb("xr", [P, 4, D])
        xrT = sb("xrT", [P, 2, P])
        sg = sb("sg", [P, 2, F])
        hh = sb("hh", [P, 2, F])
        hT = sb("hT", [P, 2, 2, P])
        yo = sb("yo", [P, 4, D])
        G = sb("G", [P, 2, GT * K2, D])
        SLOTU = sb("SLOTU", [P, TILES * K2], U32)
        fin = sb("fin", [P, 2, GT, D])
        x1g, xh = sb("x1g", [P, GT, D]), sb("xh", [P, GT, D])
        xhT = sb("xhT", [P, GT, P])
        BTs, CTs = sb("BTs", [STATE, GT, P]), sb("CTs", [STATE, GT, P])
        Bt, Binf = sb("Bt", [P, GT, STATE]), sb("Binf", [P, GT])
        dt_e, dt_z, dt_q, dt_p, decay = [sb(n, [P, GT, HEADS]) for n in ("dt_e", "dt_z", "dt_q", "dt_p", "decay")]
        e_cum, e_neg, e_end, h_cum = [sb(n, [P, GT, HEADS]) for n in ("e_cum", "e_neg", "e_end", "h_cum")]
        Gm = sb("Gm", [P, GT, P])
        th, zs, xd, xw, yb = [work[:, k] for k in range(5)]
        Wb = sb("Wb", [P, GT, INNER], BF16)
        S = sb("S", [STATE, 2, INNER])
        kmax, bnd = sb("kmax", [P, HEADS]), sb("bnd", [P, GT, HEADS])
        ok_state, ok_decay = sb("ok_state", [P, GT, HEADS]), sb("ok_decay", [P, GT, HEADS])
        yT = sb("yT", [P, 2, GT, P])
        ob = sb("ob", [P, GT, D])
        state_u = sb("state_u", [P, 2, 2, STATE])
        state, step_u = state_u[:, 0], state_u[:, 1]
        ok_all, flag = sb("ok_all", [P, 1]), sb("flag", [P, 1], I32)
        X_, X2_ = X[:, :, :].rearrange("p n d -> p (n d)"), X2[:, :, :].rearrange("p n d -> p (n d)")
        OH_ = OH[:, :, :].rearrange("p n e -> p (n e)")
        W12_ = [w[:, :, :].rearrange("p n c -> p (n c)") for w in W12s]
        WUG_ = WUG[:, :, :].rearrange("p e f -> p (e f)")
        WDT_ = WDT[:, :, :, :].rearrange("p e c d -> p (e c d)")

        B = [ps(f"bank{n}") for n in range(8)]

        v, pe, act, pool, sp = nc.vector, nc.tensor, nc.scalar, nc.gpsimd, nc.sync

        loaded, loaded_x = sem("loaded"), [sem(f"loaded_x{k}") for k in range(4)]
        prepared, wab_ready, wab_kept = sem("prepared"), sem("wab_ready"), sem("wab_kept")
        zeroed, swept = [sem(f"zeroed{n}") for n in range(2)], [sem(f"swept{n}") for n in range(2)]
        A_exp = sem("A_exp")
        dve_own, pool_own = sem("dve_own"), sem("pool_own")

        block = ctx.enter_context(nc.Block())

        passed = sem("passed")

        def wait_on(eng, semaphore, value):
            eng.wait_ge(semaphore, value)
            eng.sem_inc(passed, 1)

        def rsqrt(ch, dst, src, tmp):
            ch(v.tensor_scalar(dst.bitcast(I32), src.bitcast(I32), -0.5, MAGIC, ALU.mult, ALU.add))
            for _ in range(3):
                ch.sync()
                ch(v.tensor_tensor(tmp, dst, dst, ALU.mult))
                ch.sync()
                ch(v.scalar_tensor_tensor(out=tmp, in0=tmp, scalar=-0.5, in1=src, op0=ALU.mult, op1=ALU.mult))
                ch.sync()
                ch(v.scalar_tensor_tensor(out=dst, in0=tmp, scalar=1.5, in1=dst, op0=ALU.add, op1=ALU.mult))
            ch.sync()

        def norm_stats(ch, srcs, scale=1.0, eps=EPS):
            for t, s in enumerate(srcs):
                ch(v.bn_stats(st[:, t, :], s))
            ch.sync()
            for t in range(len(srcs)):
                ch(v.bn_aggr(mv[:, t, :], st[:, t, :]))
            ch.sync()
            ch(v.tensor_scalar(lnv[:, :], mv[:, :, 1], scale, eps, ALU.mult, ALU.add))
            ch.sync()
            rsqrt(ch, lnr[:, :], lnv[:, :], nt1[:, 0:GT])

        def norm_apply(t, dst, src):
            return v.tensor_scalar(dst, src, mv[:, t, 0:1], lnr[:, t:t + 1], ALU.subtract, ALU.mult)

        def tiles_of(arr, g):
            return [arr[:, bass.ds((g * GT + t) * D, D)] for t in range(GT)]

        def route_sems(n, slots):
            names = ("rows_ready", "rowsT_made", "rowsT_ready", "gate_made", "squared", "squares_used",
                     "chosen", "ranked", "diff_ready", "diff_exp", "placed")
            sems = {k: sem(f"gate{n}_{k}") for k in names}
            sems["n"] = min(n, 2) - 1
            sems["scattered"] = [sem(f"gate{n}_scattered{q}") for q in range(slots)]
            return sems

        def route_credits(r):
            v.sem_inc(r["squared"], 2)
            v.sem_inc(r["squares_used"], GT)

        def route_norm(ch, r, g, q, turn, srcs):
            norm_stats(ch, srcs)
            v.wait_ge(r["scattered"][q], turn * (16 * GT * K2))
            for t in range(GT):
                norm_apply(t, xn[:, q, t, :], srcs[t]).then_inc(r["rows_ready"], 1)
            wait_on(v, r["rows_ready"], g * GT + GT)

        def route_choose(ch, r, g, q, bank):
            for t in range(GT):
                v.wait_ge(r["squared"], g * GT + (t + 3))
                v.tensor_reduce(ss[:, t, :], sq[:, t, :].rearrange("p (e r) -> p e r", r=R), AX.X, ALU.add)\
                    .then_inc(r["squares_used"], 1)
            v.wait_ge(r["squares_used"], g * GT + 2 * GT)
            s_, c_ = ss[:, :, :].rearrange("p t e -> p (t e)"), sc[:, :, :].rearrange("p t e -> p (t e)")
            ch(v.tensor_scalar(nt2[:, :], s_, 1e-30, None, ALU.add))
            ch.sync()
            rsqrt(ch, c_, nt2[:, :], nt1[:, :])
            ch(v.tensor_tensor(c_, c_, s_, ALU.mult))
            ch.sync()
            for t in range(GT):
                ch(v.max(mx[:, t, :], sc[:, t, :]))
            ch.sync()
            v.tensor_tensor(ediff[:, :], mx[:, :, 1], mx[:, :, 0], ALU.subtract).then_inc(r["diff_ready"], 1)
            for t in range(GT):
                ch(v.max_index(mi[:, t, :], mx[:, t, :], sc[:, t, :]))
            ch.sync()
            ch(v.tensor_copy(mif[:, :, :], mi[:, :, 0:K2]))
            ch.sync()
            iota = cst[:, C_IOTA:C_IOTA + E].unsqueeze(1).broadcast_to([P, GT * K2, E])
            v.tensor_tensor(OH_[:, bass.ds(g * (GT * K2 * E), GT * K2 * E)].rearrange("p (n e) -> p n e", e=E), iota,
                            mif[:, :, :].rearrange("p t c -> p (t c)").unsqueeze(2).broadcast_to([P, GT * K2, E]),
                            ALU.is_equal).then_inc(r["chosen"], 1)
            v.wait_ge(r["diff_exp"], g + 1)
            ch(v.tensor_scalar(den[:, :], eexp[:, :], 2.0, 2.0, ALU.mult, ALU.add))
            ch.sync()
            ch(v.reciprocal(den[:, :], den[:, :]))
            ch.sync()
            w = W12_[r["n"]][:, bass.ds(g * (GT * K2), GT * K2)].rearrange("p (t c) -> p t c", c=K2)
            ch(v.tensor_copy(w[:, :, 0], den[:, :]))
            ch(v.tensor_tensor(w[:, :, 1], den[:, :], eexp[:, :], ALU.mult))
            v.wait_ge(r["ranked"], g + 1)
            for t in range(GT):
                ch(v.tensor_tensor(base[:, t + 1, :], base[:, t, :], bank[:, (GT + t) * E:(GT + t + 1) * E], ALU.add))
                ch.sync()
            ch(v.tensor_tensor(pre[:, :, :], bank[:, 0:GT * E].rearrange("p (t e) -> p t e", e=E),
                               base[:, 0:GT, :], ALU.add))
            ch.sync()
            ch(v.tensor_copy(base[:, 0, :], base[:, GT, :]))
            for c in range(K2):
                oh = OH_[:, bass.ds(g * (GT * K2 * E), GT * K2 * E)].rearrange("p (t c e) -> p t c e", c=K2, e=E)
                ch(v.tensor_tensor(pick[:, :, :].rearrange("p (t c) e -> p t c e", c=K2)[:, :, c, :], oh[:, :, c, :],
                                   pre[:, :, :], ALU.mult))
            ch.sync()
            slots = SLOT[:, bass.ds(g * (GT * K2), GT * K2)]
            ch(v.tensor_reduce(slots, pick[:, :, :], AX.X, ALU.add))
            ch.sync()
            v.tensor_copy(slot_u[q][:, :], slots).then_inc(r["placed"], 1)

        def route_pe_gate(r, g, q):
            pe.wait_ge(r["rowsT_ready"], g)
            for t in range(GT):
                pe.wait_ge(r["rows_ready"], g * GT + (t + 1))
                last = pe.transpose(B[0][:, t * P:(t + 1) * P], xn[:, q, t, :], ident)
            last.then_inc(r["rowsT_made"], 1)
            pe.wait_ge(r["rowsT_ready"], g + 1)
            for t in range(GT):
                pe.wait_ge(r["squared"], g * GT + (t + 1))
                pe.matmul(B[1 + t % 2][:, :], xT[:, t, :], WAT[:, :], start=True, stop=True)\
                    .then_inc(r["gate_made"], 1)

        def route_pe_rank(r, g, bank):
            pe.wait_ge(r["chosen"], g + 1)
            pe.wait_ge(r["placed"], g)
            oh = OH_[:, bass.ds(g * (GT * K2 * E), GT * K2 * E)].rearrange("p (t c e) -> p t c e", c=K2, e=E)
            for at, w in ((0, strict_bf), (GT * E, ones_bf)):
                for c in range(K2):
                    last = pe.matmul(bank[:, at:at + GT * E], w[:, :], oh[:, :, c, :], start=c == 0, stop=c == K2 - 1)
            last.then_inc(r["ranked"], 1)

        def route_act(r, g):
            act.wait_ge(r["rowsT_made"], g + 1)
            act.wait_ge(r["gate_made"], g * GT)
            act.activation(xT[:, :, :].rearrange("p t k -> p (t k)"), B[0][:, :], ACT.Copy).then_inc(r["rowsT_ready"], 1)
            for t in range(GT):
                act.wait_ge(r["gate_made"], g * GT + (t + 1))
                act.wait_ge(r["squares_used"], g * GT + (t + 1))
                act.activation(sq[:, t, :], B[1 + t % 2][:, :], ACT.Square).then_inc(r["squared"], 1)

        def route_act_exp(r, g):
            act.wait_ge(r["diff_ready"], g + 1)
            act.activation(eexp[:, :], ediff[:, :], ACT.Exp).then_inc(r["diff_exp"], 1)

        def route_pool(r, n, g, q):
            wait_on(pool, r["placed"], g + 1)
            for t in range(GT):
                for c in range(K2):
                    i = t * K2 + c
                    pool.indirect_dma_start(xg[n], bass.IndirectOffsetOnAxis(ap=slot_u[q][:, i:i + 1], axis=0),
                                            xn[:, q, t, :], None).then_inc(r["scattered"][q], 16)

        def tables(ch, tab_ready, zidx_ready, slots_ready):
            reg = cst[:, C_REG:C_REG + E]
            ch(v.tensor_scalar(zidx[:, :], base[:, 0, :], cst[:, C_PART:C_PART + 1], None, ALU.add))
            ch(v.tensor_tensor(cnt[:, :], base[:, 0, :], reg, ALU.subtract))
            ch.sync()
            v.sem_inc(zidx_ready, 1)
            ch(v.tensor_scalar(cnt_i[:, :], cnt[:, :], float(P - 1), None, ALU.add))
            ch.sync()
            ch(v.tensor_scalar(cnt_i[:, :], cnt_i[:, :], 7, None, ALU.arith_shift_right))
            ch.sync()
            ch(v.tensor_copy(ntl[:, :], cnt_i[:, :]))
            ch.sync()
            ch(v.tensor_copy(tend[:, 0:1], ntl[:, 0:1]))
            ch.sync()
            for e in range(1, E):
                ch(v.tensor_tensor(tend[:, e:e + 1], tend[:, e - 1:e], ntl[:, e:e + 1], ALU.add))
                ch.sync()
            ch(v.tensor_tensor(toff[:, :], tend[:, :], ntl[:, :], ALU.subtract))
            ch(v.tensor_scalar(tadj[:, :], ntl[:, :], -float(P), float(REG), ALU.mult, ALU.add))
            ch.sync()
            ch(v.scalar_tensor_tensor(out=toff[:, :], in0=toff[:, :], scalar=float(P), in1=reg, op0=ALU.mult, op1=ALU.subtract))
            rows = cst[:, C_ROW:C_ROW + ETILES]
            ch(v.tensor_scalar(row_f[:, :], rows, 1.0 / P, None, ALU.mult))
            ch.sync()
            ch(v.tensor_tensor(below[:, :, :], row_f[:, :].unsqueeze(2).broadcast_to([P, ETILES, E]),
                               tend[:, :].unsqueeze(1).broadcast_to([P, ETILES, E]), ALU.is_ge))
            ch.sync()
            ch(v.tensor_reduce(exp_f[:, :], below[:, :, :], AX.X, ALU.add))
            ch.sync()
            ch(v.tensor_tensor(below[:, :, :], below[:, :, :], tadj[:, :].unsqueeze(1).broadcast_to([P, ETILES, E]), ALU.mult))
            ch.sync()
            ch(v.tensor_reduce(row_f[:, :], below[:, :, :], AX.X, ALU.add))
            ch(v.tensor_scalar(tab_up[:, 3:3 + ETILES], exp_f[:, :], float(E - 1), None, ALU.min))
            ch(v.tensor_scalar(tab_down[:, 1:1 + ETILES], exp_f[:, :], float(E - 1), None, ALU.min))
            ch.sync()
            ch(v.tensor_tensor(tab_row[:, :], row_f[:, :], rows, ALU.add))
            ch.sync()
            v.sem_inc(tab_ready, 1)
            n = TILES * K2
            ch(v.tensor_tensor(below[:, 0:n, :], OH[:, :, :], toff[:, :].unsqueeze(1).broadcast_to([P, n, E]), ALU.mult))
            ch.sync()
            ch(v.tensor_reduce(row_f[:, 0:n], below[:, 0:n, :], AX.X, ALU.add))
            ch.sync()
            ch(v.tensor_tensor(SLOTU[:, :], SLOT[:, :], row_f[:, 0:n], ALU.add))
            ch.sync()
            v.sem_inc(slots_ready, 1)

        def sweep(n, zidx_ready, swept):
            pool.wait_ge(zidx_ready, 1)
            for e in range(E):
                pool.indirect_dma_start(xg[n], bass.IndirectOffsetOnAxis(ap=zidx[:, e:e + 1], axis=0),
                                        zeros[:, 0, :], None).then_inc(swept, 16)

        def expert_sems(n):
            names = ("rowsT_made", "rowsT_ready", "ug_made", "silu_ready", "h_ready", "hT_made", "hT_ready",
                     "y_made", "y_ready")
            sems = {k: sem(f"ex{n}_{k}") for k in names}
            sems["n"] = n
            sems["in"] = [sem(f"ex{n}_in{u}") for u in range(4)]
            sems["stored"] = [sem(f"ex{n}_stored{u}") for u in range(4)]
            return sems

        def turns_of_tiles(eng, step):
            turns = ETILES // 4
            for u in range(4):
                step(u, u, 0)
            with eng.Fori(1, turns - 1) as turn:
                for u in range(4):
                    step(turn * 4 + u, u, turn)
            for u in range(4):
                step((turns - 1) * 4 + u, u, turns - 1)

        def exists(j, ahead):
            return not isinstance(j, int) or 0 <= j + ahead < ETILES

        def used(eng, semaphore, j, ahead):
            if not isinstance(j, int) or j + ahead >= 2:
                eng.wait_ge(semaphore, j + (ahead - 1))

        def experts_pe(s, tab_ready):
            regs = {k: [pe.alloc_register(f"expert{s['n']}_{k}{w}") for w in range(4)] for k in ("up", "down")}

            def rows_T(j, u, turn, ahead):
                at = (u + ahead) % 4
                pe.wait_ge(s["in"][at], (turn + (u + ahead) // 4) * 16 + 16)
                used(pe, s["rowsT_ready"], j, ahead)
                pe.transpose(B[at % 2][:, 0:P], xr[:, at, :], ident).then_inc(s["rowsT_made"], 1)

            def up(j, u, ahead, expert):
                at = (u + ahead) % 2
                pe.wait_ge(s["rowsT_ready"], j + (ahead + 1))
                used(pe, s["h_ready"], j, ahead)
                pe.matmul(B[2 + at][:, :], xrT[:, at, :], WUG_[:, bass.ds(expert * (2 * F), 2 * F)], start=True, stop=True)\
                    .then_inc(s["ug_made"], 1)

            def hidden_T(j, u):
                pe.wait_ge(s["h_ready"], j + 1)
                used(pe, s["hT_ready"], j, 0)
                for k in range(2):
                    last = pe.transpose(B[4 + u % 2][:, k * P:(k + 1) * P], hh[:, u % 2, k * P:(k + 1) * P], ident)
                last.then_inc(s["hT_made"], 1)

            def down(j, u, behind, expert):
                at = (u - behind) % 2
                pe.wait_ge(s["hT_ready"], j + (1 - behind))
                used(pe, s["y_ready"], j, -behind)
                for k in range(2):
                    last = pe.matmul(B[6 + at][:, 0:D], hT[:, at, k, :],
                                     WDT_[:, bass.ds(expert * (2 * D) + k * D, D)], start=k == 0, stop=k == 1)
                last.then_inc(s["y_made"], 1)

            def expert_of(k, u):
                return pe.snap(regs[k][u], min_val=0, max_val=E - 1)

            def step(j, u, turn):
                if isinstance(j, int) and j == 0:
                    pe.reg_load(regs["up"][3], tab_up[0:1, 3:4])
                    rows_T(0, 0, 0, 0)
                    rows_T(0, 0, 0, 1)
                    up(0, 0, 0, expert_of("up", 3))
                if u == 0:
                    pe.reg_load(regs["up"], tab_up[0:1, bass.ds(j + 4, 4)])
                    pe.reg_load(regs["down"], tab_down[0:1, bass.ds(j, 4)])
                if exists(j, 2):
                    rows_T(j, u, turn, 2)
                if exists(j, 1):
                    up(j, u, 1, expert_of("up", u))
                hidden_T(j, u)
                if exists(j, -1):
                    down(j, u, 1, expert_of("down", u))
                if isinstance(j, int) and j == ETILES - 1:
                    pe.reg_load(regs["down"][0], tab_down[0:1, ETILES:ETILES + 1])
                    down(j, u, 0, expert_of("down", 0))
            pe.wait_ge(tab_ready, 1)
            turns_of_tiles(pe, step)

        def experts_act(s):
            def silu(j, u, ahead):
                at = (u + ahead) % 2
                act.wait_ge(s["ug_made"], j + (ahead + 1))
                used(act, s["h_ready"], j, ahead)
                act.activation(sg[:, at, :], B[2 + at][:, F:2 * F], ACT.Silu).then_inc(s["silu_ready"], 1)

            def keep_y(j, u, turn, behind):
                at = (u - behind) % 4
                act.wait_ge(s["y_made"], j + (1 - behind))
                if not isinstance(turn, int) or (turn > 0 and not (turn == 1 and u < behind)):
                    act.wait_ge(s["stored"][at], (turn + (u - behind) // 4) * 16)
                act.activation(yo[:, at, :], B[6 + at % 2][:, 0:D], ACT.Copy).then_inc(s["y_ready"], 1)

            def step(j, u, turn):
                if isinstance(j, int) and j == 0:
                    silu(0, 0, 0)
                if exists(j, 1):
                    silu(j, u, 1)
                if exists(j, -1):
                    keep_y(j, u, turn, 1)
                if isinstance(j, int) and j == ETILES - 1:
                    keep_y(j, u, turn, 0)
            turns_of_tiles(act, step)

        def experts_dve(s):
            def keep_rows_T(j, u, ahead):
                at = (u + ahead) % 2
                v.wait_ge(s["rowsT_made"], j + (ahead + 1))
                used(v, s["ug_made"], j, ahead)
                v.tensor_copy(xrT[:, at, :], B[at][:, 0:P]).then_inc(s["rowsT_ready"], 1)

            def hidden(j, u, ahead):
                at = (u + ahead) % 2
                v.wait_ge(s["silu_ready"], j + (ahead + 1))
                used(v, s["hT_made"], j, ahead)
                v.tensor_tensor(hh[:, at, :], sg[:, at, :], B[2 + at][:, 0:F], ALU.mult).then_inc(s["h_ready"], 1)

            def step(j, u, turn):
                if isinstance(j, int) and j == 0:
                    keep_rows_T(0, 0, 0)
                    keep_rows_T(0, 0, 1)
                    hidden(0, 0, 0)
                if exists(j, 2):
                    keep_rows_T(j, u, 2)
                if exists(j, 1):
                    hidden(j, u, 1)
                v.wait_ge(s["hT_made"], j + 1)
                used(v, s["y_made"], j, 0)
                v.tensor_copy(hT[:, u % 2, :, :].rearrange("p c k -> p (c k)"), B[4 + u % 2][:, 0:2 * P])\
                    .then_inc(s["hT_ready"], 1)
            turns_of_tiles(v, step)

        def experts_sp(s, n, r, tab_ready, swept, slots):
            for q in range(slots):
                sp.wait_ge(r["scattered"][q], 16 * GT * K2 * (GROUPS // slots))
            sp.wait_ge(swept, 16 * E)
            sp.wait_ge(zeroed[n], 16)
            sp.wait_ge(tab_ready, 1)

            def step(j, u, turn):
                row = sp.value_load(tab_row[0:1, bass.ds(j, 1)], min_val=0, max_val=E * REG + SPARE - P)
                if not (isinstance(turn, int) and turn == 0):
                    sp.wait_ge(s["rowsT_made"], j - 3)
                sp.dma_start(xr[:, u, :], xg[n][bass.ds(row, P), :]).then_inc(s["in"][u], 16)
            turns_of_tiles(sp, step)

        def experts_pool(s, n):
            def step(j, u, turn):
                pool.wait_ge(s["y_ready"], j + 1)
                pool.dma_start(yg[n][bass.ds(j * P, P), :], yo[:, u, :]).then_inc(s["stored"][u], 16)
            turns_of_tiles(pool, step)

        def all_stored(eng, s):
            for u in range(4):
                eng.wait_ge(s["stored"][u], 16 * (ETILES // 4))

        def gather(n, g, q, own, gathered, own_sem=None):
            pool.tensor_copy(slot_g[q][:, :], SLOTU[:, bass.ds(g * (GT * K2), GT * K2)]).then_inc(own_sem or pool_own, 1)
            wait_on(pool, own_sem or pool_own, own)
            for i in range(GT * K2):
                pool.indirect_dma_start(G[:, q, i, :], None, yg[n],
                                        bass.IndirectOffsetOnAxis(ap=slot_g[q][:, i:i + 1], axis=0)).then_inc(gathered, 16)

        def combine(ch, n, g, q, srcs, dst):
            for c in range(K2):
                for t in range(GT):
                    w = W12_[n][:, bass.ds(g * (GT * K2) + (t * K2 + c), 1)]
                    ch(v.scalar_tensor_tensor(out=dst[t], in0=G[:, q, t * K2 + c, :], scalar=w,
                                              in1=srcs[t] if c == 0 else dst[t], op0=ALU.mult, op1=ALU.add))
                ch.sync()

        def per_head(a):
            return a.unsqueeze(2).broadcast_to([a.shape[0], HEADS, HD])

        def heads(a):
            return a.rearrange("p (h c) -> p h c", c=HD)

        m = {k: sem(f"mix_{k}") for k in (
            "combined", "xh_ready", "xhT_made", "xhT_ready", "bd_made", "bcT_made", "bcT_ready", "dt_in", "dt_exp",
            "decay_ready", "cum_made", "exps_ready", "zx_made", "tanh_ready", "xw_ready", "cb_made", "Gm_ready",
            "Binf_ready", "wb_ready", "state_made", "S_ready", "y_made", "y_used", "bound_ready", "carry_made",
            "yn_ready", "ynT_made", "yT_ready", "o_made", "o_used")}
        gathered_m = sem("gathered_m")

        def mix_dve(ch, g, c, before, general=False):
            v.wait_ge(gathered_m, (c + 1) * (16 * GT * K2))
            combine(ch, 0, g, 0, tiles_of(X_, g), [x1g[:, t, :] for t in range(GT)])
            v.sem_inc(m["combined"], 1)
            norm_stats(ch, [x1g[:, t, :] for t in range(GT)], 1.0 + EPS, EPS * EPS)
            for t in range(GT):
                norm_apply(t, xh[:, t, :], x1g[:, t, :]).then_inc(m["xh_ready"], 1)
            v.wait_ge(m["xh_ready"], c * GT + GT)
            before()
            v.wait_ge(m["bd_made"], c + 1)
            bd = B[7][:, 0:GT * NBD].rearrange("p (t n) -> p t n", n=NBD)
            dtr = bd[:, :, STATE:NBD]
            ch(v.tensor_tensor(dt_e[:, :, :], dtr, dtb[:, :].unsqueeze(1).broadcast_to([P, GT, HEADS]), ALU.add))
            ch.sync()
            ch(v.tensor_scalar(dt_e[:, :, :], dt_e[:, :, :], 20.0, None, ALU.min))
            ch.sync()
            v.sem_inc(m["dt_in"], 1)
            ch(v.tensor_copy(Bt[:, :, :], bd[:, :, 0:STATE]))
            ch.sync()
            ch(v.tensor_reduce(Binf[:, :], Bt[:, :, :], AX.X, ALU.max, apply_absolute_value=True))
            ch.sync()
            v.sem_inc(m["Binf_ready"], 1)
            v.wait_ge(m["dt_exp"], c + 1)
            ch(v.tensor_scalar(dt_e[:, :, :], dt_p[:, :, :], 0.12, None, ALU.min))
            ch.sync()
            ch(v.tensor_scalar(dt_q[:, :, :], dt_e[:, :, :], 2.0, None, ALU.add))
            ch.sync()
            ch(v.reciprocal(dt_q[:, :, :], dt_q[:, :, :]))
            ch.sync()
            ch(v.tensor_tensor(dt_z[:, :, :], dt_e[:, :, :], dt_q[:, :, :], ALU.mult))
            ch.sync()
            ch(v.tensor_tensor(dt_q[:, :, :], dt_z[:, :, :], dt_z[:, :, :], ALU.mult))
            ch.sync()
            ch(v.tensor_scalar(dt_p[:, :, :], dt_q[:, :, :], 2 / 7, 2 / 5, ALU.mult, ALU.add))
            ch.sync()
            ch(v.tensor_tensor(dt_p[:, :, :], dt_p[:, :, :], dt_q[:, :, :], ALU.mult))
            ch.sync()
            ch(v.scalar_tensor_tensor(out=dt_p[:, :, :], in0=dt_p[:, :, :], scalar=2 / 3, in1=dt_q[:, :, :], op0=ALU.add, op1=ALU.mult))
            ch.sync()
            ch(v.scalar_tensor_tensor(out=dt_p[:, :, :], in0=dt_p[:, :, :], scalar=2.0, in1=dt_z[:, :, :], op0=ALU.add, op1=ALU.mult))
            ch.sync()
            ch(v.tensor_scalar(dt_p[:, :, :], dt_p[:, :, :], 0.001, 0.1, ALU.max, ALU.min))
            ch.sync()
            ch(v.tensor_tensor(dt_p[:, :, :], dt_p[:, :, :], nAb[:, :].unsqueeze(1).broadcast_to([P, GT, HEADS]), ALU.mult))
            ch.sync()
            if general:
                general_dve(ch, g, c)
            else:
                chunks_dve(ch, c)
            norm_stats(ch, [yb[:, t, :] for t in range(GT)])
            for t in range(GT):
                norm_apply(t, yb[:, t, :], yb[:, t, :]).then_inc(m["yn_ready"], 1)
            v.wait_ge(m["yn_ready"], c * GT + GT)
            v.wait_ge(m["o_made"], c + 1)
            ch(v.tensor_scalar(ob[:, :, :].rearrange("p t d -> p (t d)"), B[6][:, :], 10.0, -10.0, ALU.min, ALU.max))
            ch.sync()
            v.sem_inc(m["o_used"], 1)
            norm_stats(ch, [ob[:, t, :] for t in range(GT)])
            for t in range(GT):
                ch(norm_apply(t, ob[:, t, :], ob[:, t, :]))
            ch.sync()
            ch(v.tensor_tensor(ob[:, :, :], ob[:, :, :], now[:, :].unsqueeze(1).broadcast_to([P, GT, D]), ALU.mult))
            ch.sync()
            ch(v.tensor_tensor(ob[:, :, :], ob[:, :, :], nob[:, :].unsqueeze(1).broadcast_to([P, GT, D]), ALU.add))
            ch.sync()
            ch(v.tensor_tensor(X2_[:, bass.ds(g * (GT * D), GT * D)], ob[:, :, :].rearrange("p t d -> p (t d)"),
                               x1g[:, :, :].rearrange("p t d -> p (t d)"), ALU.add))
            ch.sync()

        def chunks_dve(ch, c):
            ch(v.scalar_tensor_tensor(out=ok_decay[:, :, :], in0=dt_p[:, :, :], scalar=DECAY_MIN, in1=ok_decay[:, :, :], op0=ALU.is_ge, op1=ALU.mult))
            ch(v.tensor_scalar(decay[:, :, :], dt_p[:, :, :], LOG_CAP, DECAY_MIN, ALU.min, ALU.max))
            ch.sync()
            v.sem_inc(m["decay_ready"], 1)
            for t in range(2):
                gate_and_skip(ch, c, t)
            v.wait_ge(m["cb_made"], c + 1)
            v.tensor_tensor(Gm[:, :, :], B[6][:, :].rearrange("p (t k) -> p t k", k=P),
                            tri.unsqueeze(1).broadcast_to([P, GT, P]), ALU.mult).then_inc(m["Gm_ready"], 1)
            v.wait_ge(m["exps_ready"], c + 1)
            ch(v.tensor_scalar(h_cum[:, :, :], e_cum[:, :, :], 0.5, None, ALU.mult))
            for t in range(2):
                weigh(t)
            for t in range(GT):
                if t < GT - 2:
                    gate_and_skip(ch, c, t + 2)
                    weigh(t + 2)
                chunk(ch, c, t)
            ch(v.tensor_tensor(ok_state[:, :, :], ok_state[:, :, :], bnd[:, :, :], ALU.mult))

        def gate_and_skip(ch, c, t):
            bank = B[2 + t % 2]
            v.wait_ge(m["tanh_ready"], c * GT + (t + 1))
            ch(v.scalar_tensor_tensor(out=zs[:, t, :], in0=th[:, t, :], scalar=1.0, in1=bank[:, 0:INNER], op0=ALU.add, op1=ALU.mult))
            ch(v.tensor_tensor(xd[:, t, :], bank[:, INNER:NZX], Dbc[:, :], ALU.mult))

        def weigh(t):
            bank = B[2 + t % 2]
            v.tensor_tensor(heads(xw[:, t, :]), heads(bank[:, INNER:NZX]), per_head(e_neg[:, t, :]), ALU.mult)\
                .then_inc(m["xw_ready"], 1)

        def chunk(ch, c, t):
            n = c * GT + (t + 1)
            bank = B[4 + t % 2]
            if t < GT - 1:
                v.wait_ge(m["state_made"], c * (GT - 1) + (t + 1))
                new = B[0][0:STATE, (t % 2) * INNER:(t % 2 + 1) * INNER]
                if t > 0:
                    ch(v.tensor_tensor(S[:, t % 2, :], S[:, (t + 1) % 2, :], new, ALU.add))
                    ch.sync()
                    new = S[:, t % 2, :]
                ch(v.tensor_tensor(heads(S[:, t % 2, :]), heads(new), per_head(e_end[0:STATE, t, :]), ALU.mult))
                ch.sync()
                v.sem_inc(m["S_ready"], 1)
            v.wait_ge(m["y_made"], n)
            ch(v.tensor_reduce(kmax[:, :], heads(bank[:, INNER:2 * INNER]), AX.X, ALU.max))
            ch(v.tensor_tensor(heads(yb[:, t, :]), heads(bank[:, 0:INNER]), per_head(h_cum[:, t, :]), ALU.mult))
            ch.sync()
            v.sem_inc(m["y_used"], 1)
            if t > 0:
                v.wait_ge(m["carry_made"], c * (GT - 1) + t)
                ch(v.tensor_tensor(kmax[:, :], kmax[:, :], B[1][:, CARRY:CARRY + HEADS], ALU.add))
            ch(v.tensor_tensor(yb[:, t, :], yb[:, t, :], xd[:, t, :], ALU.add))
            ch.sync()
            ch(v.tensor_tensor(decay[:, t, :], kmax[:, :], e_cum[:, t, :], ALU.mult))
            ch(v.tensor_tensor(yb[:, t, :], yb[:, t, :], zs[:, t, :], ALU.mult))
            ch.sync()
            v.sem_inc(m["bound_ready"], 1)
            ch(v.tensor_scalar(bnd[:, t, :], decay[:, t, :], STATE_MAX, None, ALU.is_le))
            if t == GT - 1:
                ch.sync()

        def mix_pe(r, g, c, rank_before, general=False):
            pe.wait_ge(r["rowsT_ready"], g)
            for t in range(GT):
                pe.wait_ge(m["xh_ready"], c * GT + (t + 1))
                last = pe.transpose(B[0][:, t * P:(t + 1) * P], xh[:, t, :], ident)
            last.then_inc(m["xhT_made"], 1)
            pe.wait_ge(m["xhT_ready"], c + 1)
            for t in range(GT):
                last = pe.matmul(B[7][:, t * NBD:(t + 1) * NBD], xhT[:, t, :], WIN[:, NZX:NZX + NBD], start=True, stop=True)
            last.then_inc(m["bd_made"], 1)
            wide = xhT[:, :, :].rearrange("p t k -> p (t k)")
            pe.matmul(B[4][0:STATE, :], WIN[:, NZX:NZX + STATE], wide, start=True, stop=True)
            pe.matmul(B[5][0:STATE, :], WIN[:, NZX + NBD:NZX + NBD + STATE], wide, start=True, stop=True)\
                .then_inc(m["bcT_made"], 1)
            pe.wait_ge(r["squared"], g * GT + 2)
            for t in range(2):
                project(t)
            rank_before()
            if general:
                general_pe(c)
            else:
                chunks_pe(c)
            for t in range(GT):
                pe.wait_ge(m["yn_ready"], c * GT + (t + 1))
                for k in range(2):
                    last = pe.transpose(B[2 + k][:, t * P:(t + 1) * P], yb[:, t, k * P:(k + 1) * P], ident)
            last.then_inc(m["ynT_made"], 1)
            pe.wait_ge(m["yT_ready"], c + 1)
            for t in range(GT):
                for k in range(2):
                    last = pe.matmul(B[6][:, t * P:(t + 1) * P], yT[:, k, t, :], WOUT[:, k, :], start=k == 0, stop=k == 1)
            last.then_inc(m["o_made"], 1)

        def chunks_pe(c):
            pe.wait_ge(m["decay_ready"], c + 1)
            a = decay[:, :, :].rearrange("p t h -> p (t h)")
            pe.matmul(B[7][:, CUM:CUM + GT * HEADS], tri, a, start=True, stop=True)
            pe.matmul(B[7][:, CUM + GT * HEADS:CUM + 2 * GT * HEADS], ones[:, :], a, start=True, stop=True)\
                .then_inc(m["cum_made"], 1)
            pe.wait_ge(m["bcT_ready"], c + 1)
            pe.wait_ge(m["o_used"], c)
            for t in range(GT):
                last = pe.matmul(B[6][:, t * P:(t + 1) * P], BTs[:, t, :], CTs[:, t, :], start=True, stop=True)
            last.then_inc(m["cb_made"], 1)
            pe.wait_ge(m["Gm_ready"], c + 1)
            for t in range(GT):
                n = c * GT + (t + 1)
                bank = B[4 + t % 2]
                pe.wait_ge(m["xw_ready"], n)
                if t < GT - 2:
                    project(t + 2)
                if t < GT - 1:
                    if t == 2:
                        pe.wait_ge(m["S_ready"], c * (GT - 1) + 1)
                    pe.matmul(B[0][0:STATE, (t % 2) * INNER:(t % 2 + 1) * INNER], Bt[:, t, :], xw[:, t, :], start=True, stop=True)\
                        .then_inc(m["state_made"], 1)
                if t >= 2:
                    pe.wait_ge(m["y_used"], n - 2)
                pe.wait_ge(m["wb_ready"], n)
                pe.matmul(bank[:, INNER:2 * INNER], tri_bf[:, :], Wb[:, t, :], start=True, stop=True)
                last = pe.matmul(bank[:, 0:INNER], Gm[:, t, :], xw[:, t, :], start=True, stop=t == 0)
                if t > 0:
                    pe.wait_ge(m["S_ready"], c * (GT - 1) + t)
                    last = pe.matmul(bank[:, 0:INNER], CTs[:, t, :], S[:, (t - 1) % 2, :], start=False, stop=True)
                last.then_inc(m["y_made"], 1)
                if t < GT - 1:
                    pe.wait_ge(m["bound_ready"], n)
                    pe.matmul(B[1][:, CARRY:CARRY + HEADS], lastrow, decay[:, t, :], start=True, stop=True)\
                        .then_inc(m["carry_made"], 1)

        def project(t):
            pe.matmul(B[2 + t % 2][:, :], xhT[:, t, :], WIN[:, 0:NZX], start=True, stop=True).then_inc(m["zx_made"], 1)

        def mix_act(c, exp_before, general=False):
            act.wait_ge(m["xhT_made"], c + 1)
            act.activation(xhT[:, :, :].rearrange("p t k -> p (t k)"), B[0][:, :], ACT.Identity,
                           scale=vec[:, 0:1], bias=vec[:, 1:2]).then_inc(m["xhT_ready"], 1)
            exp_before()
            act.wait_ge(m["bcT_made"], c + 1)
            act.activation(BTs[:, :, :].rearrange("p t k -> p (t k)"), B[4][0:STATE, :], ACT.Copy)
            act.activation(CTs[:, :, :].rearrange("p t k -> p (t k)"), B[5][0:STATE, :], ACT.Copy).then_inc(m["bcT_ready"], 1)
            act.wait_ge(m["dt_in"], c + 1)
            act.activation(dt_p[:, :, :], dt_e[:, :, :], ACT.Exp).then_inc(m["dt_exp"], 1)
            if general:
                general_act(c)
            else:
                chunks_act(c)
            act.wait_ge(m["ynT_made"], c + 1)
            for k in range(2):
                last = act.activation(yT[:, k, :, :].rearrange("p t j -> p (t j)"), B[2 + k][:, :], ACT.Identity,
                                      scale=vec[:, 2 + k:3 + k], bias=vec[:, 4 + k:5 + k])
            last.then_inc(m["yT_ready"], 1)

        def chunks_act(c):
            for t in range(2):
                tanh_z(c, t)
            act.wait_ge(m["cum_made"], c + 1)
            cum = B[7][:, CUM:CUM + 2 * GT * HEADS].rearrange("p (k t h) -> p k t h", k=2, h=HEADS)
            act.activation(e_neg[:, :, :], cum[:, 0], ACT.Exp, scale=-1.0)
            act.activation(e_cum[:, :, :], cum[:, 0], ACT.Exp)
            act.activation(e_end[:, :, :], cum[:, 1], ACT.Exp).then_inc(m["exps_ready"], 1)
            act.wait_ge(m["Binf_ready"], c + 1)
            for t in range(GT):
                n = c * GT + (t + 1)
                act.wait_ge(m["xw_ready"], n)
                act.activation(Wb[:, t, :], xw[:, t, :], ACT.Abs, scale=Binf[:, t:t + 1]).then_inc(m["wb_ready"], 1)
                if t < GT - 2:
                    tanh_z(c, t + 2)

        def tanh_z(c, t):
            act.wait_ge(m["zx_made"], c * GT + (t + 1))
            act.activation(th[:, t, :], B[2 + t % 2][:, 0:INNER], ACT.Tanh, scale=0.5).then_inc(m["tanh_ready"], 1)

        gen = {k: sem(f"general_{k}") for k in (
            "log_ready", "decay_made", "tile_ready", "T_made", "c_made", "bc_ready", "bc_stored", "block_in", "block_used",
            "scanned", "y_made", "flag_sum", "flag_ready", "own")}
        bc_rows = nc.dram_tensor("bc_rows", (1, SEQ * 2 * STATE), F32).ap()
        xs_T = G[:, 1].rearrange("p (c a) d -> p c (a d)", c=2)
        da_T = fin[:, :, :, :].rearrange("p c t d -> p c (t d)")
        ys_T = xn[:, 1:3].rearrange("p c t d -> p c (t d)")
        bc = ob
        bc_all = sq[:, :, :].rearrange("p t n -> p (t n)")

        def general_dve(ch, g, c):
            ch(v.tensor_scalar(decay[:, :, :], dt_p[:, :, :], LOG_CAP, None, ALU.min))
            ch.sync()
            v.sem_inc(gen["log_ready"], 1)
            v.wait_ge(gen["c_made"], g + 1)
            ch(v.tensor_copy(bc[:, :, 0:STATE], Bt[:, :, :]))
            ch(v.tensor_copy(bc[:, :, STATE:2 * STATE], B[6][:, 0:GT * STATE].rearrange("p (t n) -> p t n", n=STATE)))
            ch.sync()
            v.sem_inc(gen["bc_ready"], 1)
            v.wait_ge(gen["decay_made"], g + 1)
            for t in range(GT):
                gate_and_skip(ch, c, t)
                ch.sync()
                ch(v.tensor_copy(heads(th[:, t, :]), per_head(e_cum[:, t, :])))
                ch(v.tensor_copy(xw[:, t, :], B[2 + t % 2][:, INNER:NZX]))
                ch.sync()
                v.sem_inc(m["xw_ready"], 1)
            v.wait_ge(gen["T_made"], g + 1)
            for k in range(2):
                ch(v.tensor_copy(xs_T[:, k, :], B[4 + k][:, :]))
                ch(v.tensor_copy(da_T[:, k, :], B[k][:, :]))
            ch(v.memset(state, 0.0))
            ch.restart()
            with v.Fori(0, SEQ // BLOCK) as blk:
                wait_on(v, gen["block_in"], g * (16 * SEQ // BLOCK) + (blk * 16 + 16))
                with v.Fori(0, BLOCK) as tt:
                    def over_n(a):
                        return a[:, :, bass.ds(blk * BLOCK + tt, 1)].broadcast_to([P, 2, STATE])

                    def over_c(at):
                        return bc_all[:, bass.ds(tt * (2 * STATE) + at, STATE)].unsqueeze(1).broadcast_to([P, 2, STATE])
                    ch(v.tensor_tensor(step_u, over_c(0), over_n(xs_T), ALU.mult))
                    ch(v.tensor_tensor(state, state, over_n(da_T), ALU.mult))
                    ch.sync()
                    ch(v.tensor_tensor(state, state, step_u, ALU.add))
                    ch.sync()
                    ch(v.tensor_scalar(state, state, 10.0, -10.0, ALU.min, ALU.max))
                    ch.sync()
                    ch(v.tensor_tensor(step_u, state, over_c(STATE), ALU.mult))
                    ch.sync()
                    ch(v.tensor_reduce(ys_T[:, :, bass.ds(blk * BLOCK + tt, 1)], step_u, AX.X, ALU.add))
                    ch.restart()
                v.sem_inc(gen["block_used"], 1)
            v.sem_inc(gen["scanned"], 1)
            v.wait_ge(gen["y_made"], g + 1)
            for t in range(GT):
                ch(v.tensor_scalar(yb[:, t, :], B[4 + t // 2][:, (t % 2) * INNER:(t % 2 + 1) * INNER], 0.5, None, ALU.mult))
                ch.sync()
                ch(v.tensor_tensor(yb[:, t, :], yb[:, t, :], xd[:, t, :], ALU.add))
                ch.sync()
                ch(v.tensor_tensor(yb[:, t, :], yb[:, t, :], zs[:, t, :], ALU.mult))
            ch.sync()

        def general_pe(c):
            g = c - GROUPS
            pe.wait_ge(m["o_used"], c)
            for t in range(GT):
                last = pe.matmul(B[6][:, t * STATE:(t + 1) * STATE], xhT[:, t, :],
                                 WIN[:, NZX + NBD:NZX + NBD + STATE], start=True, stop=True)
            last.then_inc(gen["c_made"], 1)
            pe.wait_ge(gen["log_ready"], g + 1)
            pe.wait_ge(m["bcT_ready"], c + 1)
            for t in range(GT):
                pe.wait_ge(m["xw_ready"], c * GT + (t + 1))
                if t < GT - 2:
                    project(t + 2)
                for k in range(2):
                    part = slice(k * P, (k + 1) * P)
                    pe.transpose(B[4 + k][:, t * P:(t + 1) * P], xw[:, t, part], ident)
                    last = pe.transpose(B[k][:, t * P:(t + 1) * P], th[:, t, part], ident)
            last.then_inc(gen["T_made"], 1)
            pe.wait_ge(gen["scanned"], g + 1)
            for t in range(GT):
                for k in range(2):
                    at = (t % 2) * INNER + k * P
                    last = pe.transpose(B[4 + t // 2][:, at:at + P], ys_T[:, k, t * P:(t + 1) * P], ident)
            last.then_inc(gen["y_made"], 1)

        def general_act(c):
            g = c - GROUPS
            act.wait_ge(gen["log_ready"], g + 1)
            act.activation(e_cum[:, :, :], decay[:, :, :], ACT.Exp).then_inc(gen["decay_made"], 1)
            for t in range(GT):
                tanh_z(c, t)

        def general_sp(g):
            wait_on(sp, gen["bc_ready"], g + 1)
            sp.wait_ge(gen["block_used"], g * (SEQ // BLOCK))
            sp.dma_start(bc_rows.rearrange("o (t p n) -> (o p) t n", p=P, n=2 * STATE), bc[:, :, :]).then_inc(gen["bc_stored"], 16)
            wait_on(sp, gen["bc_stored"], g * 16 + 16)
            with sp.Fori(0, SEQ // BLOCK) as blk:
                sp.wait_ge(gen["block_used"], g * (SEQ // BLOCK) + blk)
                sp.dma_start(bc_all, bc_rows[:, bass.ds(blk * (BLOCK * 2 * STATE), BLOCK * 2 * STATE)]
                             .broadcast_to([P, BLOCK * 2 * STATE])).then_inc(gen["block_in"], 16)

        def flagged(eng):
            eng.wait_ge(gen["flag_ready"], 1)
            return eng.value_load(flag[0:1, 0:1], min_val=0, max_val=1) > 0

        r1 = route_sems(1, 4)
        e1 = expert_sems(1)
        tab1, zidx1, slots1 = sem("tab1_ready"), sem("zidx1_ready"), sem("slots1_ready")
        r2, r3, e2 = route_sems(2, 1), route_sems(3, 1), expert_sems(2)
        tab2, zidx2, slots2 = sem("tab2_ready"), sem("zidx2_ready"), sem("slots2_ready")
        gathered_f = [sem(f"gathered_f{q}") for q in range(2)]
        combined_f, stored_f = sem("combined_f"), [sem(f"stored_f{q}") for q in range(2)]

        @block.sync
        def _(_e):
            sp.dma_start(cst[:, :], consts).then_inc(loaded, 16)
            sp.dma_start(WAT[:, :], wA_T).then_inc(loaded, 16)
            sp.dma_start(WA, wA).then_inc(loaded, 16)
            sp.dma_start(WBT, wB_T).then_inc(loaded, 16)
            for k in range(4):
                part = slice(k * TILES // 4, (k + 1) * TILES // 4)
                sp.dma_start(X[:, part, :], x.rearrange("(n p) d -> p n d", p=P)[:, part, :]).then_inc(loaded_x[k], 16)
            sp.dma_start(WUG[:, :, 0:F], wUp_T).then_inc(loaded, 16)
            sp.dma_start(WDT[:, :, :, :], wDn_T).then_inc(loaded, 16)
            sp.dma_start(WIN[:, :], in_T).then_inc(loaded, 16)
            sp.dma_start(WOUT[:, :, :], out_T).then_inc(loaded, 16)
            sp.dma_start(vec[:, :], vecs).then_inc(loaded, 16)
            for dst, src in ((nAb, A_log), (dtb, dt_bias), (Dh, Dparam), (now, no_w), (nob, no_b)):
                sp.dma_start(dst[:, :], src.broadcast_to([P, src.shape[1]])).then_inc(loaded, 16)
            sp.wait_ge(prepared, 1)
            for n in range(2):
                sp.dma_start(xg[n][E * REG:E * REG + SPARE, :].rearrange("(p n) d -> p n d", p=P), zeros[:, :, :])\
                    .then_inc(zeroed[n], 16)
            experts_sp(e1, 0, r1, tab1, swept[0], 4)
            with sp.If(flagged(sp)):
                with sp.Fori(0, GROUPS) as g:
                    general_sp(g)
            experts_sp(e2, 1, r2, tab2, swept[1], 1)
            with sp.Fori(0, GROUPS // 2) as turn:
                for q in range(2):
                    g = turn * 2 + q
                    sp.wait_ge(combined_f, g + 3)
                    sp.dma_start(out[bass.ds(g * SEQ, SEQ), :].rearrange("(t p) d -> p t d", p=P), fin[:, q, :, :])\
                        .then_inc(stored_f[q], 16)
            for q in range(2):
                sp.wait_ge(stored_f[q], 16 * (GROUPS // 2))

        @block.vector
        def _(_e):
            ch = Chain(v, dve_own)
            ch(v.memset(zeros[:, :, :], 0.0))
            ch(v.memset(ones_bf[:, :], 1.0))
            ch(v.memset(ones[:, :], 1.0))
            for tab in (tab_up, tab_down):
                ch(v.memset(tab[:, :], 0))
            v.wait_ge(loaded, 16 * LOADS)
            v.wait_ge(A_exp, 1)
            ch(v.tensor_copy(strict_bf[:, :], cst[:, C_STRICT:C_STRICT + P]))
            ch(v.tensor_copy(tri_bf[:, :], tri))
            ch(v.tensor_copy(base[:, 0, :], cst[:, C_REG:C_REG + E]))
            ch.sync()
            ch(v.tensor_scalar(nAb[:, :], nAb[:, :], -1.0, None, ALU.mult))
            ch(v.tensor_scalar(Dh[:, :], Dh[:, :], 0.5, None, ALU.mult))
            ch(v.memset(ok_state[:, :, :], 1.0))
            ch(v.memset(ok_decay[:, :, :], 1.0))
            ch.sync()
            ch(v.tensor_copy(heads(Dbc[:, :]), per_head(Dh[:, :])))
            route_credits(r1)
            route_credits(r2)
            route_credits(r3)
            ch.restart()
            v.sem_inc(prepared, 1)
            for e in range(E):
                v.wait_ge(wab_ready, e + 1)
                v.tensor_copy(WUG[:, e, F:2 * F], B[4 + e % 4][:, 0:F]).then_inc(wab_kept, 1)
            for k in range(4):
                v.wait_ge(loaded_x[k], 16)
            route_norm(ch, r1, 0, 0, 0, tiles_of(X_, 0))

            def turn_of_groups(turn, last):
                for q in range(4):
                    g = turn * 4 + q
                    if not (last and q == 3):
                        route_norm(ch, r1, g + 1, (q + 1) % 4, turn + (q == 3), tiles_of(X_, g + 1))
                    route_choose(ch, r1, g, q, B[3])
                    ch.restart()
            ch.restart()
            with v.Fori(0, GROUPS // 4 - 1) as turn:
                turn_of_groups(turn, False)
            turn_of_groups(GROUPS // 4 - 1, True)
            tables(ch, tab1, zidx1, slots1)
            ch.restart()
            experts_dve(e1)
            ch(v.tensor_copy(base[:, 0, :], cst[:, C_REG:C_REG + E]))
            ch.sync()
            mix_dve(ch, 0, 0, lambda: None)
            route_norm(ch, r2, 0, 0, 0, tiles_of(X2_, 0))
            ch.restart()
            with v.Fori(1, GROUPS) as g:
                mix_dve(ch, g, g, lambda: route_choose(ch, r2, g - 1, 0, B[1]))
                route_norm(ch, r2, g, 0, g, tiles_of(X2_, g))
                ch.restart()
            route_choose(ch, r2, GROUPS - 1, 0, B[1])
            ch(v.tensor_tensor(bnd[:, :, :], ok_state[:, :, :], ok_decay[:, :, :], ALU.mult))
            ch.sync()
            ch(v.tensor_reduce(ok_all[:, :], bnd[:, :, :].rearrange("p t h -> p (t h)"), AX.X, ALU.min))
            ch.sync()
            v.sem_inc(gen["flag_sum"], 1)
            v.wait_ge(gen["flag_sum"], 2)
            ch(v.tensor_scalar(flag[:, :], B[7][:, 0:1], P - 0.5, None, ALU.is_lt))
            ch.restart()
            v.sem_inc(gen["flag_ready"], 1)
            with v.If(flagged(v)):
                v.tensor_copy(base[:, 0, :], cst[:, C_REG:C_REG + E]).then_inc(dve_own, 1)
                v.wait_ge(dve_own, 1)
                v.sem_clear(dve_own)
                again = Chain(v, dve_own)
                mix_dve(again, 0, GROUPS, lambda: None, True)
                route_norm(again, r3, 0, 0, 0, tiles_of(X2_, 0))
                again.restart()
                with v.Fori(1, GROUPS) as g:
                    mix_dve(again, g, g + GROUPS, lambda: route_choose(again, r3, g - 1, 0, B[1]), True)
                    route_norm(again, r3, g, 0, g, tiles_of(X2_, g))
                    again.restart()
                route_choose(again, r3, GROUPS - 1, 0, B[1])
                again.restart()
            tables(ch, tab2, zidx2, slots2)
            ch.restart()
            experts_dve(e2)
            v.sem_inc(combined_f, 2)
            with v.Fori(0, GROUPS // 2) as turn:
                for q in range(2):
                    g = turn * 2 + q
                    v.wait_ge(gathered_f[q], (turn + 1) * (16 * GT * K2))
                    v.wait_ge(stored_f[q], turn * 16)
                    combine(ch, 1, g, q, tiles_of(X2_, g), [fin[:, q, t, :] for t in range(GT)])
                    v.sem_inc(combined_f, 1)
                ch.restart()

        @block.tensor
        def _(_e):
            pe.wait_ge(loaded, 16 * LOADS)
            for e in range(E):
                if e >= 4:
                    pe.wait_ge(wab_kept, e - 3)
                pe.matmul(B[4 + e % 4][:, 0:F], WA[:, e * D:(e + 1) * D], WBT[:, e * F:(e + 1) * F], start=True, stop=True)\
                    .then_inc(wab_ready, 1)
            pe.wait_ge(prepared, 1)
            with pe.Fori(0, GROUPS // 4) as turn:
                for q in range(4):
                    g = turn * 4 + q
                    route_pe_gate(r1, g, q)
                    route_pe_rank(r1, g, B[3])
            experts_pe(e1, tab1)
            mix_pe(r2, 0, 0, lambda: None)
            route_pe_gate(r2, 0, 0)
            with pe.Fori(1, GROUPS) as g:
                mix_pe(r2, g, g, lambda: route_pe_rank(r2, g - 1, B[1]))
                route_pe_gate(r2, g, 0)
            route_pe_rank(r2, GROUPS - 1, B[1])
            pe.wait_ge(gen["flag_sum"], 1)
            pe.matmul(B[7][:, 0:1], ones[:, :], ok_all[:, :], start=True, stop=True).then_inc(gen["flag_sum"], 1)
            with pe.If(flagged(pe)):
                mix_pe(r3, 0, GROUPS, lambda: None, True)
                route_pe_gate(r3, 0, 0)
                with pe.Fori(1, GROUPS) as g:
                    mix_pe(r3, g, g + GROUPS, lambda: route_pe_rank(r3, g - 1, B[1]), True)
                    route_pe_gate(r3, g, 0)
                route_pe_rank(r3, GROUPS - 1, B[1])
            experts_pe(e2, tab2)

        @block.scalar
        def _(_e):
            act.wait_ge(loaded, 16 * LOADS)
            act.activation(nAb[:, :], nAb[:, :], ACT.Exp).then_inc(A_exp, 1)
            with act.Fori(0, GROUPS) as g:
                route_act(r1, g)
                route_act_exp(r1, g)
            experts_act(e1)
            mix_act(0, lambda: None)
            route_act(r2, 0)
            with act.Fori(1, GROUPS) as g:
                mix_act(g, lambda: route_act_exp(r2, g - 1))
                route_act(r2, g)
            route_act_exp(r2, GROUPS - 1)
            with act.If(flagged(act)):
                mix_act(GROUPS, lambda: None, True)
                route_act(r3, 0)
                with act.Fori(1, GROUPS) as g:
                    mix_act(g + GROUPS, lambda: route_act_exp(r3, g - 1), True)
                    route_act(r3, g)
                route_act_exp(r3, GROUPS - 1)
            experts_act(e2)

        @block.gpsimd
        def _(_e):
            with pool.Fori(0, GROUPS // 4) as turn:
                for q in range(4):
                    route_pool(r1, 0, turn * 4 + q, q)
            sweep(0, zidx1, swept[0])
            experts_pool(e1, 0)
            all_stored(pool, e1)
            pool.wait_ge(slots1, 1)
            gather(0, 0, 0, 1, gathered_m)
            with pool.Fori(0, GROUPS - 1) as g:
                pool.wait_ge(m["combined"], g + 1)
                gather(0, g + 1, 0, g + 2, gathered_m)
                route_pool(r2, 1, g, 0)
            route_pool(r2, 1, GROUPS - 1, 0)
            with pool.If(flagged(pool)):
                gather(0, 0, 0, 1, gathered_m, gen["own"])
                with pool.Fori(0, GROUPS - 1) as g:
                    pool.wait_ge(m["combined"], g + (GROUPS + 1))
                    gather(0, g + 1, 0, g + 2, gathered_m, gen["own"])
                    route_pool(r3, 1, g, 0)
                route_pool(r3, 1, GROUPS - 1, 0)
                pool.wait_ge(r3["scattered"][0], 16 * GT * K2 * GROUPS)
            sweep(1, zidx2, swept[1])
            experts_pool(e2, 1)
            all_stored(pool, e2)
            pool.wait_ge(slots2, 1)
            with pool.Fori(0, GROUPS // 2) as turn:
                for q in range(2):
                    g = turn * 2 + q
                    pool.wait_ge(combined_f, g + 1)
                    gather(1, g, q, g + (GROUPS + 1), gathered_f[q])


def kernel(**inputs):
    import numpy as np
    import concourse.bacc as bacc
    from concourse.bass_utils import run_bass_kernel_spmd

    a = {k.replace("L0_", ""): np.asarray(i) for k, i in inputs.items()}
    cc = np.ascontiguousarray
    k, m = np.arange(P)[:, None], np.arange(P)[None, :]
    consts = np.zeros((P, C_N), np.float32)
    consts[:, C_ID:C_ID + P] = k == m
    consts[:, C_TRI:C_TRI + P] = k <= m
    consts[:, C_STRICT:C_STRICT + P] = k < m
    consts[P - 1, C_LAST:C_LAST + P] = 1
    consts[:, C_IOTA:C_IOTA + E] = np.arange(E)
    consts[:, C_REG:C_REG + E] = np.arange(E) * REG
    consts[:, C_PART] = np.arange(P)
    consts[:, C_ROW:C_ROW + ETILES] = np.arange(ETILES) * P
    win = a["attn_in_proj_w"].T
    o = 2 * INNER
    win = np.concatenate([win[:, 0:o + STATE], win[:, o + 2 * STATE:], win[:, o + STATE:o + 2 * STATE]], axis=1)
    halves = lambda w: w.reshape(2, P).T
    arrays = {
        "x": cc(a["attn_x"].reshape(TOK, D)),
        "consts": consts,
        "wA_T": cc(a["ffn_W_A"].transpose(2, 0, 1).reshape(D, E * R)),
        "wA": cc(a["ffn_W_A"].transpose(1, 0, 2).reshape(R, E * D)),
        "wB_T": cc(a["ffn_W_B"].transpose(2, 0, 1).reshape(R, E * F)),
        "wUp_T": cc(a["ffn_W_up"].transpose(2, 0, 1)),
        "wDn_T": cc(a["ffn_W_down"].transpose(2, 0, 1).reshape(2, P, E, D).transpose(1, 2, 0, 3)),
        "in_T": cc(win),
        "out_T": cc(a["attn_out_proj_w"].T.reshape(2, P, D).transpose(1, 0, 2)),
        "vecs": cc(np.concatenate([a["attn_ni_w"][:, None], a["attn_ni_b"][:, None],
                                   halves(a["attn_ln_w"]), halves(a["attn_ln_b"])], axis=1)),
        "dt_bias": cc(a["attn_dt_bias"].reshape(1, HEADS)),
        "A_log": cc(a["attn_A_log"].reshape(1, HEADS)),
        "Dparam": cc(a["attn_Dparam"].reshape(1, HEADS)),
        "no_w": cc(a["attn_no_w"].reshape(1, D)),
        "no_b": cc(a["attn_no_b"].reshape(1, D)),
    }
    nc = bacc.Bacc("TRN2", target_bir_lowering=False, num_devices=1)
    args = [nc.dram_tensor(n, v.shape, F32, kind="ExternalInput").ap() for n, v in arrays.items()]
    args.append(nc.dram_tensor("out", (TOK, D), F32, kind="ExternalOutput").ap())
    macaron(nc, *args)
    res = run_bass_kernel_spmd(nc, [arrays], core_ids=[0])
    return res.results[0]["out"].reshape(BATCH, SEQ, D)
```

```python
import numpy as np
import concourse.bass as bass
from concourse import mybir
from contextlib import ExitStack

F32 = mybir.dt.float32
BF16 = mybir.dt.bfloat16
I32 = mybir.dt.int32
U32 = mybir.dt.uint32
ALU = mybir.AluOpType
ACT = mybir.ActivationFunctionType
AX = mybir.AxisListType

P = 128
BATCH, SEQ, D = 16, 512, 128
TOK = BATCH * SEQ
TILES = TOK // P
SQ = 2
CHUNKS = SEQ // P
GT = SQ * CHUNKS
GROUPS = TILES // GT
SLOTS = 2
E, K2, R, F = 8, 2, 64, 256
INNER, STATE, HEADS, HD = 256, 64, 4, 64
REG = TOK + P
ETILES = TOK * K2 // P + E
SPARE = E * P
EPS = 1e-5
MAGIC = float(0x5F3759DF)
NZX = 2 * INNER
C_DT, C_BC = NZX, NZX + HEADS
ITEMS = [(t, q) for t in range(CHUNKS) for q in range(SQ)]
TILE = [q * CHUNKS + t for t, q in ITEMS]
CARRIED = (CHUNKS - 1) * SQ
CARRY = INNER
M_DT, M_CUM, M_TOT = 0, GT * HEADS, 2 * GT * HEADS
BLOCK = 16
STATE_MAX = 9.8
DECAY_MIN = -0.5
LOADS = 12
LOG_CAP = float(np.log(0.99))

C_ID, C_TRI, C_STRICT, C_LAST = 0, P, 2 * P, 3 * P
C_IOTA = 4 * P
C_REG = C_IOTA + E
C_PART = C_REG + E
C_ROW = C_PART + 1
C_BLK = C_ROW + ETILES
C_N = C_BLK + E * E // 2


class Chain:

    def __init__(self, eng, sem):
        self.eng, self.sem, self.n = eng, sem, 0

    def __call__(self, ins):
        self.n += 1
        return ins.then_inc(self.sem, 1)

    def sync(self):
        self.eng.wait_ge(self.sem, self.n)

    def restart(self):
        self.sync()
        self.eng.sem_clear(self.sem)
        self.n = 0


def macaron(nc, x, consts, wA_T, wA, wB_T, wUp_T, wDn_T, in_T, out_T, vecs, dt_bias, A_log, Dparam,
            no_w, no_b, out, debug=None):
    ctx = ExitStack()
    with ctx:
        def sb(name, shape, dt=F32):
            return ctx.enter_context(nc.sbuf_tensor(name, shape, dt))

        def ps(name, shape=(P, 512), dt=F32):
            return ctx.enter_context(nc.psum_tensor(name, list(shape), dt))

        def sem(name):
            return ctx.enter_context(nc.semaphore(name))

        xg = [nc.dram_tensor(f"rows_by_expert{n}", (E * REG + SPARE, D), F32).ap() for n in range(2)]
        yg = [nc.dram_tensor(f"expert_results{n}", (ETILES * P, D), F32).ap() for n in range(2)]

        X = sb("X", [P, TILES, D])
        X2 = sb("X2", [P, TILES, D])
        cst = sb("cst", [P, C_N])
        WAT = sb("WAT", [P, E * R])
        work = sb("work", [P, 3, GT, INNER])
        wide = work[:, :, :, :].rearrange("p k t n -> p (k t n)")
        WBT, WA = wide[0:R, 0:E * F], wide[0:R, E * F:E * (F + D)]
        WUG = sb("WUG", [P, E, 2 * F])
        WDT = sb("WDT", [P, E, 2, D])
        WIN = sb("WIN", [P, NZX + HEADS + 2 * STATE])
        WOUT = sb("WOUT", [P, 2, D])
        ident, tri = cst[:, C_ID:C_ID + P], cst[:, C_TRI:C_TRI + P]
        lastrow = cst[:, C_LAST:C_LAST + P]
        strict_bf = sb("strict_bf", [P, P], BF16)
        tri_bf = sb("tri_bf", [P, P], BF16)
        ones_bf = sb("ones_bf", [P, P], BF16)
        zeros_bf = sb("zeros_bf", [P, P], BF16)
        ones = sb("ones", [P, P])
        zeros = sb("zeros", [P, SPARE // P, D])
        vec = sb("vec", [P, 6])
        nAb = sb("nAb", [P, HEADS])
        dtb = sb("dtb", [P, HEADS])
        Dh = sb("Dh", [P, HEADS])
        Dbc = sb("Dbc", [P, INNER])
        now, nob = sb("now", [P, D]), sb("nob", [P, D])

        OH = sb("OH", [P, TILES * K2, E], BF16)
        SLOT = sb("SLOT", [P, TILES * K2])
        W12s = [sb(f"W12_{n}", [P, TILES, K2]) for n in range(2)]
        base = sb("base", [P, E])
        xn = sb("xn", [P, SLOTS, GT, D])
        xT = sb("xT", [P, GT * P])
        G_sq = sb("G_sq", [P, 3, GT * K2, D])
        G = G_sq[:, 0:2]
        sq = G_sq[:, 1:3].rearrange("p q (j a) d -> p q j (a d)", j=E // 2)
        sc = sb("sc", [P, GT, E])
        nt1, nt2 = sb("nt1", [P, GT * E]), sb("nt2", [P, GT * E])
        mx, mi = sb("mx", [P, GT, 8]), sb("mi", [P, GT, 8], U32)
        mif = sb("mif", [P, GT, K2])
        pre = sb("pre", [P, GT, E])
        pick = sb("pick", [P, GT * K2, E])
        slot_u = [sb(f"slot_u{q}", [P, GT * K2], U32) for q in range(SLOTS)]
        slot_g = [sb(f"slot_g{n}", [P, GT * K2], U32) for n in range(2)]
        ediff, eexp, den = sb("ediff", [P, GT]), sb("eexp", [P, GT]), sb("den", [P, GT])
        st = sb("st", [P, GT, 6])
        lnv = sb("lnv", [P, GT])
        norms = {n: (sb(f"mv_{n}", [P, GT, 2]), sb(f"rstd_{n}", [P, GT]), sb(f"shift_{n}", [P, GT]))
                 for n in ("x1", "rows", "y", "o")}
        cnt, cnt_i, ntl, tend = sb("cnt", [P, E]), sb("cnt_i", [P, E], I32), sb("ntl", [P, E]), sb("tend", [P, E])
        toff, tadj = sb("toff", [P, E]), sb("tadj", [P, E])
        GW = sb("GW", [P, 2, GT * P])
        below = GW[:, :, :].rearrange("p k n -> p (k n)")[:, 0:ETILES * E].rearrange("p (j e) -> p j e", e=E)
        Gm, Wb = GW[:, 0].rearrange("p (t k) -> p t k", k=P), GW[:, 1].bitcast(BF16).rearrange("p (t n) -> p t n", n=INNER)
        yT = GW[:, :, :].rearrange("p k (t j) -> p k t j", j=P)
        row_f, exp_f = sb("row_f", [P, ETILES]), sb("exp_f", [P, ETILES])
        tab_row = sb("tab_row", [P, ETILES], I32)
        tab_up, tab_down = sb("tab_up", [P, ETILES + 4], I32), sb("tab_down", [P, ETILES + 4], I32)
        zidx = sb("zidx", [P, E], U32)
        ex = wide[:, E * (F + D):]

        def ex_part(at, *shape):
            n = int(np.prod(shape))
            names = "abc"[:len(shape)]
            return ex[:, at:at + n].rearrange(f"p ({' '.join(names)}) -> p {' '.join(names)}", **dict(zip(names, shape)))
        xr, yo = ex_part(0, 4, D), ex_part(4 * D, 4, D)
        xrT, hT = ex_part(8 * D, 2, P), ex_part(10 * D, 2, 2, P)
        sg, hh = ex_part(14 * D, 2, F), ex_part(14 * D + 2 * F, 2, F)
        SLOTU = sb("SLOTU", [P, TILES * K2], U32)
        fin = work[:, 0:2].rearrange("p k t n -> p (k t n)").rearrange("p (q t d) -> p q t d", q=4, d=D)[:, 0:2]
        xh, xhT = sb("xh", [P, GT, D]), sb("xhT", [P, GT, P])
        ob = xh
        BTs, CTs = sb("BTs", [STATE, GT, P]), sb("CTs", [STATE, GT, P])
        Bt, Binf = sb("Bt", [P, GT, STATE]), sb("Binf", [P, GT])
        dt_e, dt_z, dt_q, dt_p, decay = [sb(n, [P, GT, HEADS]) for n in ("dt_e", "dt_z", "dt_q", "dt_p", "decay")]
        e_cum, e_neg, e_end, h_cum = [sb(n, [P, GT, HEADS]) for n in ("e_cum", "e_neg", "e_end", "h_cum")]
        th, xd, xw = [work[:, k] for k in range(3)]
        zs, yb = th, xw
        S = sb("S", [STATE, SQ, 2, INNER])
        kmax, bnd = sb("kmax", [P, HEADS]), sb("bnd", [P, GT, HEADS])
        ok_state, ok_decay = sb("ok_state", [P, GT, HEADS]), sb("ok_decay", [P, GT, HEADS])
        state_u = sb("state_u", [P, 2, 2, STATE])
        state, step_u = state_u[:, 0], state_u[:, 1]
        ok_all, flag = sb("ok_all", [P, 1]), sb("flag", [P, 1], I32)
        X_, X2_ = X[:, :, :].rearrange("p n d -> p (n d)"), X2[:, :, :].rearrange("p n d -> p (n d)")
        OH_ = OH[:, :, :].rearrange("p n e -> p (n e)")
        W12_ = [w[:, :, :].rearrange("p n c -> p (n c)") for w in W12s]
        WUG_ = WUG[:, :, :].rearrange("p e f -> p (e f)")
        WDT_ = WDT[:, :, :, :].rearrange("p e c d -> p (e c d)")

        B = [ps(f"bank{n}") for n in range(8)]

        v, pe, act, pool, sp = nc.vector, nc.tensor, nc.scalar, nc.gpsimd, nc.sync

        loaded, loaded_first = sem("loaded"), sem("loaded_first")
        loaded_x = [sem(f"loaded_x{k}") for k in range(4)]
        wab_ready, wab_kept = sem("wab_ready"), sem("wab_kept")
        zeroed, swept = [sem(f"zeroed{n}") for n in range(2)], [sem(f"swept{n}") for n in range(2)]
        A_exp, zeros_ready = sem("A_exp"), sem("zeros_ready")
        dve_own, pool_own = sem("dve_own"), sem("pool_own")

        block = ctx.enter_context(nc.Block())

        passed = sem("passed")

        def wait_on(eng, semaphore, value):
            eng.wait_ge(semaphore, value)
            eng.sem_inc(passed, 1)

        def after(eng, semaphore, value):
            if not isinstance(value, int) or value > 0:
                eng.wait_ge(semaphore, value)

        def rsqrt(ch, dst, src, tmp):
            k = 3 / 8
            ch(v.tensor_scalar(dst.bitcast(I32), src.bitcast(I32), -0.5, MAGIC, ALU.mult, ALU.add))
            ch.sync()
            ch(v.tensor_tensor(tmp, dst, dst, ALU.mult))
            ch.sync()
            ch(v.tensor_tensor(tmp, tmp, src, ALU.mult))
            ch.sync()
            ch(v.scalar_tensor_tensor(out=tmp, in0=tmp, scalar=-10 / 3, in1=tmp, op0=ALU.add, op1=ALU.mult))
            ch.sync()
            ch(v.scalar_tensor_tensor(out=dst, in0=tmp, scalar=5.0, in1=dst, op0=ALU.add, op1=ALU.mult))
            ch.sync()
            ch(v.tensor_tensor(tmp, dst, dst, ALU.mult))
            ch.sync()
            ch(v.scalar_tensor_tensor(out=tmp, in0=tmp, scalar=-0.5 * k ** 3, in1=src, op0=ALU.mult, op1=ALU.mult))
            ch.sync()
            ch(v.scalar_tensor_tensor(out=dst, in0=tmp, scalar=1.5 * k, in1=dst, op0=ALU.add, op1=ALU.mult))
            ch.sync()

        def norm_stats(ch, name, srcs, scale=1.0, eps=EPS):
            mv, rstd, shift = norms[name]
            for t, src in enumerate(srcs):
                ch(v.bn_stats(st[:, t, :], src))
            ch.sync()
            for t in range(len(srcs)):
                ch(v.bn_aggr(mv[:, t, :], st[:, t, :]))
            ch.sync()
            ch(v.tensor_scalar(lnv[:, :], mv[:, :, 1], scale, eps, ALU.mult, ALU.add))
            ch.sync()
            rsqrt(ch, rstd[:, :], lnv[:, :], nt1[:, 0:GT])
            ch(v.scalar_tensor_tensor(out=shift[:, :], in0=mv[:, :, 0], scalar=-1.0, in1=rstd[:, :], op0=ALU.mult, op1=ALU.mult))
            ch.sync()

        def normalise(name, t, dst, src):
            _, rstd, shift = norms[name]
            return act.activation(dst, src, ACT.Identity, scale=rstd[:, t:t + 1], bias=shift[:, t:t + 1])

        def tiles_of(arr, g):
            return [arr[:, bass.ds((g * GT + t) * D, D)] for t in range(GT)]

        def route_sems(n, slots, T, scores):
            names = ("norm_ready", "rows_ready", "rowsT_made", "rowsT_ready", "gate_made", "squared", "summed",
                     "chosen", "ranked", "diff_ready", "diff_exp", "placed")
            sems = {k: sem(f"gate{n}_{k}") for k in names}
            sems["n"] = min(n, 2) - 1
            sems["T"], sems["scores"] = T, scores
            sems["scattered"] = [sem(f"gate{n}_scattered{q}") for q in range(slots)]
            return sems

        def route_norm(ch, r, g, srcs):
            if not isinstance(g, int) or g > 0:
                wait_on(v, r["rows_ready"], g * GT)
            norm_stats(ch, "rows", srcs)
            v.sem_inc(r["norm_ready"], 1)

        def route_choose(ch, r, g, q, turn):
            scores, ranks = B[r["scores"][q]][:, 0:GT * E], B[1]
            v.wait_ge(r["summed"], g + 1)
            c_ = sc[:, :, :].rearrange("p t e -> p (t e)")
            ch(v.tensor_scalar(nt2[:, :], scores, 1e-30, None, ALU.add))
            ch.sync()
            rsqrt(ch, c_, nt2[:, :], nt1[:, :])
            ch(v.tensor_tensor(c_, c_, scores, ALU.mult))
            ch.sync()
            for t in range(GT):
                ch(v.max(mx[:, t, :], sc[:, t, :]))
            ch.sync()
            v.tensor_tensor(ediff[:, :], mx[:, :, 1], mx[:, :, 0], ALU.subtract).then_inc(r["diff_ready"], 1)
            for t in range(GT):
                ch(v.max_index(mi[:, t, :], mx[:, t, :], sc[:, t, :]))
            ch.sync()
            ch(v.tensor_copy(mif[:, :, :], mi[:, :, 0:K2]))
            ch.sync()
            iota = cst[:, C_IOTA:C_IOTA + E].unsqueeze(1).broadcast_to([P, GT * K2, E])
            v.tensor_tensor(OH_[:, bass.ds(g * (GT * K2 * E), GT * K2 * E)].rearrange("p (n e) -> p n e", e=E), iota,
                            mif[:, :, :].rearrange("p t c -> p (t c)").unsqueeze(2).broadcast_to([P, GT * K2, E]),
                            ALU.is_equal).then_inc(r["chosen"], 1)
            v.wait_ge(r["diff_exp"], g + 1)
            ch(v.tensor_scalar(den[:, :], eexp[:, :], 2.0, 2.0, ALU.mult, ALU.add))
            ch.sync()
            ch(v.reciprocal(den[:, :], den[:, :]))
            ch.sync()
            w = W12_[r["n"]][:, bass.ds(g * (GT * K2), GT * K2)].rearrange("p (t c) -> p t c", c=K2)
            ch(v.tensor_copy(w[:, :, 0], den[:, :]))
            ch(v.tensor_tensor(w[:, :, 1], den[:, :], eexp[:, :], ALU.mult))
            v.wait_ge(r["ranked"], g + 1)
            ch(v.tensor_tensor(pre[:, :, :], ranks[:, 0:GT * E].rearrange("p (t e) -> p t e", e=E),
                               base[:, :].unsqueeze(1).broadcast_to([P, GT, E]), ALU.add))
            ch.sync()
            ch(v.tensor_tensor(base[:, :], ranks[:, GT * E:(GT + 1) * E], base[:, :], ALU.add))
            for c in range(K2):
                oh = OH_[:, bass.ds(g * (GT * K2 * E), GT * K2 * E)].rearrange("p (t c e) -> p t c e", c=K2, e=E)
                ch(v.tensor_tensor(pick[:, :, :].rearrange("p (t c) e -> p t c e", c=K2)[:, :, c, :], oh[:, :, c, :],
                                   pre[:, :, :], ALU.mult))
            ch.sync()
            slots = SLOT[:, bass.ds(g * (GT * K2), GT * K2)]
            ch(v.tensor_reduce(slots, pick[:, :, :], AX.X, ALU.add))
            ch.sync()
            if not isinstance(turn, int) or turn > 0:
                wait_on(v, r["scattered"][q], turn * (16 * GT * K2))
            v.tensor_copy(slot_u[q][:, :], slots).then_inc(r["placed"], 1)

        def route_pe_transpose(r, g, q):
            after(pe, r["rowsT_ready"], g * 2)
            for t in range(GT):
                pe.wait_ge(r["rows_ready"], g * GT + (t + 1))
                at = (t % 4) * P
                last = pe.transpose(B[r["T"][t // 4]][:, at:at + P], xn[:, q, t, :], ident)
                if t % 4 == 3:
                    last.then_inc(r["rowsT_made"], 1)

        def route_pe_gate(r, g, half):
            pe.wait_ge(r["rowsT_ready"], g * 2 + 2)
            for j in range(E // 2):
                after(pe, r["squared"], g * E + (half * (E // 2) + j - 1))
                pe.matmul(B[6 + j % 2][:, :], WAT[:, j * P:(j + 1) * P], xT[:, half * 4 * P:(half + 1) * 4 * P],
                          start=True, stop=True).then_inc(r["gate_made"], 1)

        def route_pe_scores(r, g, q):
            pe.wait_ge(r["squared"], g * E + E)
            for t in range(GT):
                for j in range(E // 2):
                    last = pe.matmul(B[r["scores"][q]][:, t * E:(t + 1) * E], sq[:, t // 4, j, (t % 4) * P:(t % 4 + 1) * P],
                                     cst[:, C_BLK + j * E:C_BLK + (j + 1) * E], start=j == 0, stop=j == E // 2 - 1)
            last.then_inc(r["summed"], 1)

        def route_pe_rank(r, g):
            pe.wait_ge(r["chosen"], g + 1)
            after(pe, r["placed"], g)
            oh = OH_[:, bass.ds(g * (GT * K2 * E), GT * K2 * E)].rearrange("p (t c e) -> p t c e", c=K2, e=E)
            pe.matmul(B[1][:, 0:(GT + 1) * E], zeros_bf[:, :], tri_bf[:, 0:(GT + 1) * E], start=True, stop=False)
            for c in range(K2):
                pe.matmul(B[1][:, 0:GT * E], strict_bf[:, :], oh[:, :, c, :], start=False, stop=False)
            for before in range(1, GT + 1):
                for c in range(K2):
                    last = pe.matmul(B[1][:, before * E:(GT + 1) * E], ones_bf[:, :], oh[:, 0:GT + 1 - before, c, :],
                                     start=False, stop=before == GT and c == K2 - 1)
            last.then_inc(r["ranked"], 1)

        def route_act_rows(r, g, q, turn, srcs):
            act.wait_ge(r["norm_ready"], g + 1)
            after(act, r["scattered"][q], turn * (16 * GT * K2))
            for t in range(GT):
                normalise("rows", t, xn[:, q, t, :], srcs[t]).then_inc(r["rows_ready"], 1)

        def route_act_T(r, g):
            after(act, r["gate_made"], g * E)
            for half in range(2):
                act.wait_ge(r["rowsT_made"], g * 2 + (half + 1))
                act.activation(xT[:, half * 4 * P:(half + 1) * 4 * P], B[r["T"][half]][:, :], ACT.Copy)\
                    .then_inc(r["rowsT_ready"], 1)

        def route_act_squares(r, g, half):
            after(act, r["summed"], g)
            for j in range(E // 2):
                act.wait_ge(r["gate_made"], g * E + (half * (E // 2) + j + 1))
                act.activation(sq[:, half, j, :], B[6 + j % 2][:, :], ACT.Square).then_inc(r["squared"], 1)

        def route_act_exp(r, g):
            act.wait_ge(r["diff_ready"], g + 1)
            act.activation(eexp[:, :], ediff[:, :], ACT.Exp).then_inc(r["diff_exp"], 1)

        def route_pool(r, n, g, q):
            wait_on(pool, r["placed"], g + 1)
            for t in range(GT):
                for c in range(K2):
                    i = t * K2 + c
                    pool.indirect_dma_start(xg[n], bass.IndirectOffsetOnAxis(ap=slot_u[q][:, i:i + 1], axis=0),
                                            xn[:, q, t, :], None).then_inc(r["scattered"][q], 16)

        def tables(ch, tab_ready, zidx_ready, slots_ready):
            reg = cst[:, C_REG:C_REG + E]
            ch(v.tensor_scalar(zidx[:, :], base[:, :], cst[:, C_PART:C_PART + 1], None, ALU.add))
            ch(v.tensor_tensor(cnt[:, :], base[:, :], reg, ALU.subtract))
            ch.sync()
            v.sem_inc(zidx_ready, 1)
            ch(v.tensor_scalar(cnt_i[:, :], cnt[:, :], float(P - 1), None, ALU.add))
            ch.sync()
            ch(v.tensor_scalar(cnt_i[:, :], cnt_i[:, :], 7, None, ALU.arith_shift_right))
            ch.sync()
            ch(v.tensor_copy(ntl[:, :], cnt_i[:, :]))
            ch.sync()
            ch(v.tensor_copy(tend[:, 0:1], ntl[:, 0:1]))
            ch.sync()
            for e in range(1, E):
                ch(v.tensor_tensor(tend[:, e:e + 1], tend[:, e - 1:e], ntl[:, e:e + 1], ALU.add))
                ch.sync()
            ch(v.tensor_tensor(toff[:, :], tend[:, :], ntl[:, :], ALU.subtract))
            ch(v.tensor_scalar(tadj[:, :], ntl[:, :], -float(P), float(REG), ALU.mult, ALU.add))
            ch.sync()
            ch(v.scalar_tensor_tensor(out=toff[:, :], in0=toff[:, :], scalar=float(P), in1=reg, op0=ALU.mult, op1=ALU.subtract))
            rows = cst[:, C_ROW:C_ROW + ETILES]
            ch(v.tensor_scalar(row_f[:, :], rows, 1.0 / P, None, ALU.mult))
            ch.sync()
            ch(v.tensor_tensor(below[:, :, :], row_f[:, :].unsqueeze(2).broadcast_to([P, ETILES, E]),
                               tend[:, :].unsqueeze(1).broadcast_to([P, ETILES, E]), ALU.is_ge))
            ch.sync()
            ch(v.tensor_reduce(exp_f[:, :], below[:, :, :], AX.X, ALU.add))
            ch.sync()
            ch(v.tensor_tensor(below[:, :, :], below[:, :, :], tadj[:, :].unsqueeze(1).broadcast_to([P, ETILES, E]), ALU.mult))
            ch.sync()
            ch(v.tensor_reduce(row_f[:, :], below[:, :, :], AX.X, ALU.add))
            ch(v.tensor_scalar(tab_up[:, 3:3 + ETILES], exp_f[:, :], float(E - 1), None, ALU.min))
            ch(v.tensor_scalar(tab_down[:, 1:1 + ETILES], exp_f[:, :], float(E - 1), None, ALU.min))
            ch.sync()
            ch(v.tensor_tensor(tab_row[:, :], row_f[:, :], rows, ALU.add))
            ch.sync()
            v.sem_inc(tab_ready, 1)
            n = TILES * K2
            ch(v.tensor_tensor(below[:, 0:n, :], OH[:, :, :], toff[:, :].unsqueeze(1).broadcast_to([P, n, E]), ALU.mult))
            ch.sync()
            ch(v.tensor_reduce(row_f[:, 0:n], below[:, 0:n, :], AX.X, ALU.add))
            ch.sync()
            ch(v.tensor_tensor(SLOTU[:, :], SLOT[:, :], row_f[:, 0:n], ALU.add))
            ch.sync()
            v.sem_inc(slots_ready, 1)

        def sweep(n, zidx_ready, swept):
            pool.wait_ge(zidx_ready, 1)
            for e in range(E):
                pool.indirect_dma_start(xg[n], bass.IndirectOffsetOnAxis(ap=zidx[:, e:e + 1], axis=0),
                                        zeros[:, 0, :], None).then_inc(swept, 16)

        def expert_sems(n):
            names = ("rowsT_made", "rowsT_ready", "ug_made", "silu_ready", "h_ready", "hT_made", "hT_ready",
                     "y_made", "y_ready")
            sems = {k: sem(f"ex{n}_{k}") for k in names}
            sems["n"] = n
            sems["in"] = [sem(f"ex{n}_in{u}") for u in range(4)]
            sems["stored"] = [sem(f"ex{n}_stored{u}") for u in range(4)]
            return sems

        def turns_of_tiles(eng, step):
            turns = ETILES // 4
            for u in range(4):
                step(u, u, 0)
            with eng.Fori(1, turns - 1) as turn:
                for u in range(4):
                    step(turn * 4 + u, u, turn)
            for u in range(4):
                step((turns - 1) * 4 + u, u, turns - 1)

        def exists(j, ahead):
            return not isinstance(j, int) or 0 <= j + ahead < ETILES

        def used(eng, semaphore, j, ahead):
            if not isinstance(j, int) or j + ahead >= 2:
                eng.wait_ge(semaphore, j + (ahead - 1))

        def experts_pe(s, tab_ready):
            regs = {k: [pe.alloc_register(f"expert{s['n']}_{k}{w}") for w in range(4)] for k in ("up", "down")}

            def rows_T(j, u, turn, ahead):
                at = (u + ahead) % 4
                pe.wait_ge(s["in"][at], (turn + (u + ahead) // 4) * 16 + 16)
                used(pe, s["rowsT_ready"], j, ahead)
                pe.transpose(B[at % 2][:, 0:P], xr[:, at, :], ident).then_inc(s["rowsT_made"], 1)

            def up(j, u, ahead, expert):
                at = (u + ahead) % 2
                pe.wait_ge(s["rowsT_ready"], j + (ahead + 1))
                used(pe, s["h_ready"], j, ahead)
                pe.matmul(B[2 + at][:, :], xrT[:, at, :], WUG_[:, bass.ds(expert * (2 * F), 2 * F)], start=True, stop=True)\
                    .then_inc(s["ug_made"], 1)

            def hidden_T(j, u):
                pe.wait_ge(s["h_ready"], j + 1)
                used(pe, s["hT_ready"], j, 0)
                for k in range(2):
                    last = pe.transpose(B[4 + u % 2][:, k * P:(k + 1) * P], hh[:, u % 2, k * P:(k + 1) * P], ident)
                last.then_inc(s["hT_made"], 1)

            def down(j, u, behind, expert):
                at = (u - behind) % 2
                pe.wait_ge(s["hT_ready"], j + (1 - behind))
                used(pe, s["y_ready"], j, -behind)
                for k in range(2):
                    last = pe.matmul(B[6 + at][:, 0:D], hT[:, at, k, :],
                                     WDT_[:, bass.ds(expert * (2 * D) + k * D, D)], start=k == 0, stop=k == 1)
                last.then_inc(s["y_made"], 1)

            def expert_of(k, u):
                return pe.snap(regs[k][u], min_val=0, max_val=E - 1)

            def step(j, u, turn):
                if isinstance(j, int) and j == 0:
                    pe.reg_load(regs["up"][3], tab_up[0:1, 3:4])
                    rows_T(0, 0, 0, 0)
                    rows_T(0, 0, 0, 1)
                    up(0, 0, 0, expert_of("up", 3))
                if u == 0:
                    pe.reg_load(regs["up"], tab_up[0:1, bass.ds(j + 4, 4)])
                    pe.reg_load(regs["down"], tab_down[0:1, bass.ds(j, 4)])
                if exists(j, 2):
                    rows_T(j, u, turn, 2)
                if exists(j, 1):
                    up(j, u, 1, expert_of("up", u))
                hidden_T(j, u)
                if exists(j, -1):
                    down(j, u, 1, expert_of("down", u))
                if isinstance(j, int) and j == ETILES - 1:
                    pe.reg_load(regs["down"][0], tab_down[0:1, ETILES:ETILES + 1])
                    down(j, u, 0, expert_of("down", 0))
            pe.wait_ge(tab_ready, 1)
            turns_of_tiles(pe, step)

        def experts_act(s):
            def silu(j, u, ahead):
                at = (u + ahead) % 2
                act.wait_ge(s["ug_made"], j + (ahead + 1))
                used(act, s["h_ready"], j, ahead)
                act.activation(sg[:, at, :], B[2 + at][:, F:2 * F], ACT.Silu).then_inc(s["silu_ready"], 1)

            def keep_y(j, u, turn, behind):
                at = (u - behind) % 4
                act.wait_ge(s["y_made"], j + (1 - behind))
                if not isinstance(turn, int) or (turn > 0 and not (turn == 1 and u < behind)):
                    act.wait_ge(s["stored"][at], (turn + (u - behind) // 4) * 16)
                act.activation(yo[:, at, :], B[6 + at % 2][:, 0:D], ACT.Copy).then_inc(s["y_ready"], 1)

            def step(j, u, turn):
                if isinstance(j, int) and j == 0:
                    silu(0, 0, 0)
                if exists(j, 1):
                    silu(j, u, 1)
                if exists(j, -1):
                    keep_y(j, u, turn, 1)
                if isinstance(j, int) and j == ETILES - 1:
                    keep_y(j, u, turn, 0)
            turns_of_tiles(act, step)

        def experts_dve(s):
            def keep_rows_T(j, u, ahead):
                at = (u + ahead) % 2
                v.wait_ge(s["rowsT_made"], j + (ahead + 1))
                used(v, s["ug_made"], j, ahead)
                v.tensor_copy(xrT[:, at, :], B[at][:, 0:P]).then_inc(s["rowsT_ready"], 1)

            def hidden(j, u, ahead):
                at = (u + ahead) % 2
                v.wait_ge(s["silu_ready"], j + (ahead + 1))
                used(v, s["hT_made"], j, ahead)
                v.tensor_tensor(hh[:, at, :], sg[:, at, :], B[2 + at][:, 0:F], ALU.mult).then_inc(s["h_ready"], 1)

            def step(j, u, turn):
                if isinstance(j, int) and j == 0:
                    keep_rows_T(0, 0, 0)
                    keep_rows_T(0, 0, 1)
                    hidden(0, 0, 0)
                if exists(j, 2):
                    keep_rows_T(j, u, 2)
                if exists(j, 1):
                    hidden(j, u, 1)
                v.wait_ge(s["hT_made"], j + 1)
                used(v, s["y_made"], j, 0)
                v.tensor_copy(hT[:, u % 2, :, :].rearrange("p c k -> p (c k)"), B[4 + u % 2][:, 0:2 * P])\
                    .then_inc(s["hT_ready"], 1)
            turns_of_tiles(v, step)

        def experts_sp(s, n, r, tab_ready, swept, slots):
            for q in range(slots):
                sp.wait_ge(r["scattered"][q], 16 * GT * K2 * (GROUPS // slots))
            sp.wait_ge(swept, 16 * E)
            sp.wait_ge(zeroed[n], 16)
            sp.wait_ge(tab_ready, 1)

            def step(j, u, turn):
                row = sp.value_load(tab_row[0:1, bass.ds(j, 1)], min_val=0, max_val=E * REG + SPARE - P)
                if not (isinstance(turn, int) and turn == 0):
                    sp.wait_ge(s["rowsT_made"], j - 3)
                sp.dma_start(xr[:, u, :], xg[n][bass.ds(row, P), :]).then_inc(s["in"][u], 16)
            turns_of_tiles(sp, step)

        def experts_pool(s, n):
            def step(j, u, turn):
                pool.wait_ge(s["y_ready"], j + 1)
                pool.dma_start(yg[n][bass.ds(j * P, P), :], yo[:, u, :]).then_inc(s["stored"][u], 16)
            turns_of_tiles(pool, step)

        def all_stored(eng, s):
            for u in range(4):
                eng.wait_ge(s["stored"][u], 16 * (ETILES // 4))

        def gather(n, g, q, own, gathered):
            pool.tensor_copy(slot_g[q][:, :], SLOTU[:, bass.ds(g * (GT * K2), GT * K2)]).then_inc(pool_own, 1)
            wait_on(pool, pool_own, own)
            for i in range(GT * K2):
                pool.indirect_dma_start(G[:, q, i, :], None, yg[n],
                                        bass.IndirectOffsetOnAxis(ap=slot_g[q][:, i:i + 1], axis=0)).then_inc(gathered, 16)

        def combine(ch, n, g, q, srcs, dst):
            for c in range(K2):
                for t in range(GT):
                    w = W12_[n][:, bass.ds(g * (GT * K2) + (t * K2 + c), 1)]
                    ch(v.scalar_tensor_tensor(out=dst[t], in0=G[:, q, t * K2 + c, :], scalar=w,
                                              in1=srcs[t] if c == 0 else dst[t], op0=ALU.mult, op1=ALU.add))
                ch.sync()

        def per_head(a):
            return a.unsqueeze(2).broadcast_to([a.shape[0], HEADS, HD])

        def heads(a):
            return a.rearrange("p (h c) -> p h c", c=HD)

        m = {k: sem(f"mix_{k}") for k in (
            "combined", "norm_ready", "xh_ready", "xhT_made", "xhT_ready", "dt_made", "b_made", "bcT_made", "Bt_ready",
            "bcT_ready", "dt_in", "dt_exp", "decay_ready", "cum_made", "exps_ready", "zx_made", "tanh_ready", "xw_ready",
            "cb_made", "Gm_ready", "Binf_ready", "wb_ready", "state_made", "S_ready", "y_made", "bound_ready",
            "y_norm_ready", "yn_ready", "ynT_made", "yT_ready", "o_made", "o_used", "x1_kept")}
        gathered_m = sem("gathered_m")

        def mix_dve(ch, r, g, c, general=False):
            if not (isinstance(g, int) and g == 0):
                finish_dve(ch, g - 1, c - 1)
            if not general:
                v.wait_ge(gathered_m, (c + 1) * (16 * GT * K2))
                combine(ch, 0, g, 0, tiles_of(X_, g), tiles_of(X_, g))
                v.sem_inc(m["combined"], 1)
            norm_stats(ch, "x1", tiles_of(X_, g), 1.0 + EPS, EPS * EPS)
            v.sem_inc(m["norm_ready"], 1)
            if not (isinstance(g, int) and g == 0):
                route_norm(ch, r, g - 1, tiles_of(X2_, g - 1))
            v.wait_ge(m["dt_made"], c + 1)
            dtr = B[0][:, M_DT:M_DT + GT * HEADS].rearrange("p (t h) -> p t h", h=HEADS)
            ch(v.tensor_tensor(dt_e[:, :, :], dtr, dtb[:, :].unsqueeze(1).broadcast_to([P, GT, HEADS]), ALU.add))
            ch.sync()
            ch(v.tensor_scalar(dt_e[:, :, :], dt_e[:, :, :], 20.0, None, ALU.min))
            ch.sync()
            v.sem_inc(m["dt_in"], 1)
            v.wait_ge(m["dt_exp"], c + 1)
            ch(v.tensor_scalar(dt_e[:, :, :], dt_p[:, :, :], 0.12, None, ALU.min))
            ch.sync()
            ch(v.tensor_scalar(dt_q[:, :, :], dt_e[:, :, :], 2.0, None, ALU.add))
            ch.sync()
            ch(v.reciprocal(dt_q[:, :, :], dt_q[:, :, :]))
            ch.sync()
            ch(v.tensor_tensor(dt_z[:, :, :], dt_e[:, :, :], dt_q[:, :, :], ALU.mult))
            ch.sync()
            ch(v.tensor_tensor(dt_q[:, :, :], dt_z[:, :, :], dt_z[:, :, :], ALU.mult))
            ch.sync()
            ch(v.tensor_scalar(dt_p[:, :, :], dt_q[:, :, :], 2 / 7, 2 / 5, ALU.mult, ALU.add))
            ch.sync()
            ch(v.tensor_tensor(dt_p[:, :, :], dt_p[:, :, :], dt_q[:, :, :], ALU.mult))
            ch.sync()
            ch(v.scalar_tensor_tensor(out=dt_p[:, :, :], in0=dt_p[:, :, :], scalar=2 / 3, in1=dt_q[:, :, :], op0=ALU.add, op1=ALU.mult))
            ch.sync()
            ch(v.scalar_tensor_tensor(out=dt_p[:, :, :], in0=dt_p[:, :, :], scalar=2.0, in1=dt_z[:, :, :], op0=ALU.add, op1=ALU.mult))
            ch.sync()
            ch(v.tensor_scalar(dt_p[:, :, :], dt_p[:, :, :], 0.001, 0.1, ALU.max, ALU.min))
            ch.sync()
            ch(v.tensor_tensor(dt_p[:, :, :], dt_p[:, :, :], nAb[:, :].unsqueeze(1).broadcast_to([P, GT, HEADS]), ALU.mult))
            ch.sync()
            if general:
                general_dve(ch, g, c)
            else:
                chunks_dve(ch, c)
            norm_stats(ch, "y", [yb[:, t, :] for t in range(GT)])
            v.sem_inc(m["y_norm_ready"], 1)
            if not (isinstance(g, int) and g == 0):
                route_choose(ch, r, g - 1, 0, g - 1)

        def finish_dve(ch, g, c):
            mv, rstd, _ = norms["o"]
            v.wait_ge(m["o_made"], c + 1)
            for half in range(2):
                at = slice(half * 4, (half + 1) * 4)
                ch(v.tensor_scalar(ob[:, at, :].rearrange("p t d -> p (t d)"), B[6 + half][:, :], 10.0, -10.0, ALU.min, ALU.max))
            ch.sync()
            v.sem_inc(m["o_used"], 1)
            norm_stats(ch, "o", [ob[:, t, :] for t in range(GT)])
            for t in range(GT):
                ch(v.scalar_tensor_tensor(out=ob[:, t, :], in0=ob[:, t, :], scalar=mv[:, t, 0:1], in1=now[:, :],
                                          op0=ALU.subtract, op1=ALU.mult))
            v.wait_ge(m["x1_kept"], c + 1)
            ch.sync()
            x2 = tiles_of(X2_, g)
            for t in range(GT):
                ch(v.scalar_tensor_tensor(out=x2[t], in0=ob[:, t, :], scalar=rstd[:, t:t + 1], in1=x2[t],
                                          op0=ALU.mult, op1=ALU.add))
            ch.sync()

        def chunks_dve(ch, c):
            ch(v.scalar_tensor_tensor(out=ok_decay[:, :, :], in0=dt_p[:, :, :], scalar=DECAY_MIN, in1=ok_decay[:, :, :], op0=ALU.is_ge, op1=ALU.mult))
            ch(v.tensor_scalar(decay[:, :, :], dt_p[:, :, :], LOG_CAP, DECAY_MIN, ALU.min, ALU.max))
            ch.sync()
            v.sem_inc(m["decay_ready"], 1)
            v.wait_ge(m["Bt_ready"], c + 1)
            ch(v.tensor_reduce(Binf[:, :], Bt[:, :, :], AX.X, ALU.max, apply_absolute_value=True))
            for n in range(2):
                gate_and_skip(ch, c, n, TILE[n])
            ch.sync()
            v.sem_inc(m["Binf_ready"], 1)
            v.wait_ge(m["cb_made"], c + 1)
            for half in range(2):
                at = slice(half * 4, (half + 1) * 4)
                v.tensor_tensor(Gm[:, at, :], B[6 + half][:, :].rearrange("p (t k) -> p t k", k=P),
                                tri.unsqueeze(1).broadcast_to([P, 4, P]), ALU.mult).then_inc(m["Gm_ready"], 1)
            v.wait_ge(m["exps_ready"], c + 1)
            ch(v.tensor_scalar(h_cum[:, :, :], e_cum[:, :, :], 0.5, None, ALU.mult))
            for n in range(2):
                weigh(n)
            for n in range(GT):
                chunk(ch, c, n)
                if n < GT - 2:
                    gate_and_skip(ch, c, n + 2, TILE[n + 2])
                    weigh(n + 2)
            ch.sync()
            ch(v.tensor_tensor(ok_state[:, :, :], ok_state[:, :, :], bnd[:, :, :], ALU.mult))

        def gate_and_skip(ch, c, n, i):
            bank = B[2 + n % 2]
            v.wait_ge(m["tanh_ready"], c * GT + (n + 1))
            ch(v.scalar_tensor_tensor(out=zs[:, i, :], in0=th[:, i, :], scalar=1.0, in1=bank[:, 0:INNER], op0=ALU.add, op1=ALU.mult))
            ch(v.tensor_tensor(xd[:, i, :], bank[:, INNER:NZX], Dbc[:, :], ALU.mult))

        def weigh(n):
            v.tensor_tensor(heads(xw[:, TILE[n], :]), heads(B[2 + n % 2][:, INNER:NZX]), per_head(e_neg[:, TILE[n], :]), ALU.mult)\
                .then_inc(m["xw_ready"], 1)

        def chunk(ch, c, n):
            (t, q), i = ITEMS[n], TILE[n]
            if t < CHUNKS - 1:
                v.wait_ge(m["state_made"], c * CARRIED + (n + 1))
                new = B[q][0:STATE, 0:INNER]
                if t > 0:
                    ch(v.tensor_tensor(S[:, q, t % 2, :], S[:, q, (t + 1) % 2, :], new, ALU.add))
                    ch.sync()
                    new = S[:, q, t % 2, :]
                ch(v.tensor_tensor(heads(S[:, q, t % 2, :]), heads(new), per_head(e_end[0:STATE, i, :]), ALU.mult))
            v.wait_ge(m["y_made"], c * GT + (n + 1))
            ch(v.tensor_reduce(kmax[:, :], heads(B[4 + q][:, INNER:2 * INNER]), AX.X, ALU.max))
            ch(v.tensor_tensor(heads(yb[:, i, :]), heads(B[4 + q][:, 0:INNER]), per_head(h_cum[:, i, :]), ALU.mult))
            ch.sync()
            if t < CHUNKS - 1:
                v.sem_inc(m["S_ready"], 1)
            if t > 0:
                ch(v.tensor_tensor(kmax[:, :], kmax[:, :], B[q][:, CARRY:CARRY + HEADS], ALU.add))
            ch(v.tensor_tensor(yb[:, i, :], yb[:, i, :], xd[:, i, :], ALU.add))
            ch.sync()
            ch(v.tensor_tensor(decay[:, i, :], kmax[:, :], e_cum[:, i, :], ALU.mult))
            ch(v.tensor_tensor(yb[:, i, :], yb[:, i, :], zs[:, i, :], ALU.mult))
            ch.sync()
            v.sem_inc(m["bound_ready"], 1)
            ch(v.tensor_scalar(bnd[:, i, :], decay[:, i, :], STATE_MAX, None, ALU.is_le))

        def mix_pe(r, g, c, general=False):
            first = isinstance(g, int) and g == 0
            for t in range(GT):
                pe.wait_ge(m["xh_ready"], c * GT + (t + 1))
                last = pe.transpose(B[2 + t // 4][:, (t % 4) * P:(t % 4 + 1) * P], xh[:, t, :], ident)
                if t % 4 == 3:
                    last.then_inc(m["xhT_made"], 1)
            pe.wait_ge(m["xhT_ready"], c * 2 + 2)
            for t in range(GT):
                last = pe.matmul(B[0][:, M_DT + t * HEADS:M_DT + (t + 1) * HEADS], xhT[:, t, :], WIN[:, C_DT:C_DT + HEADS], start=True, stop=True)
            last.then_inc(m["dt_made"], 1)
            after(pe, m["o_used"], c)
            for t in range(GT):
                last = pe.matmul(B[7][:, t * STATE:(t + 1) * STATE], xhT[:, t, :], WIN[:, C_BC:C_BC + STATE], start=True, stop=True)
            last.then_inc(m["b_made"], 1)
            for half in range(2):
                pe.matmul(B[4 + half][:, :], WIN[:, C_BC:C_BC + 2 * STATE], xhT[:, half * 4:(half + 1) * 4, :].rearrange("p t k -> p (t k)"),
                          start=True, stop=True).then_inc(m["bcT_made"], 1)
            order = range(GT) if general else TILE
            for n in range(2):
                project(n, order[n])
            if general:
                pe.wait_ge(m["bcT_ready"], c + 1)
                if not first:
                    route_pe_transpose(r, g - 1, 0)
                    for half in range(2):
                        route_pe_gate(r, g - 1, half)
                    route_pe_scores(r, g - 1, 0)
                general_pe(c)
            else:
                pe.wait_ge(m["decay_ready"], c + 1)
                a = decay[:, :, :].rearrange("p t h -> p (t h)")
                pe.matmul(B[0][:, M_CUM:M_CUM + GT * HEADS], tri, a, start=True, stop=True)
                pe.matmul(B[0][:, M_TOT:M_TOT + GT * HEADS], ones[:, :], a, start=True, stop=True).then_inc(m["cum_made"], 1)
                pe.wait_ge(m["bcT_ready"], c + 1)
                for i in range(GT):
                    last = pe.matmul(B[6 + i // 4][:, (i % 4) * P:(i % 4 + 1) * P], BTs[:, i, :], CTs[:, i, :], start=True, stop=True)
                last.then_inc(m["cb_made"], 1)
                pe.wait_ge(m["Gm_ready"], c * 2 + 2)
                for n in range(GT):
                    chunk_pe(c, n)
                    if not first and n == 1:
                        route_pe_transpose(r, g - 1, 0)
                    if not first and n == 4:
                        route_pe_gate(r, g - 1, 0)
                if not first:
                    route_pe_gate(r, g - 1, 1)
                    pe.wait_ge(m["bound_ready"], (c + 1) * GT)
                    route_pe_scores(r, g - 1, 0)
            for i in range(GT):
                pe.wait_ge(m["yn_ready"], c * GT + (i + 1))
                for k in range(2):
                    last = pe.transpose(B[2 + 2 * (i // 4) + k][:, (i % 4) * P:(i % 4 + 1) * P], yb[:, i, k * P:(k + 1) * P], ident)
                if i % 4 == 3:
                    last.then_inc(m["ynT_made"], 1)
            if not first:
                route_pe_rank(r, g - 1)
            for i in range(GT):
                pe.wait_ge(m["yT_ready"], c * 2 + (i // 4 + 1))
                for k in range(2):
                    last = pe.matmul(B[6 + i // 4][:, (i % 4) * P:(i % 4 + 1) * P], yT[:, k, i, :], WOUT[:, k, :], start=k == 0, stop=k == 1)
            last.then_inc(m["o_made"], 1)

        def chunk_pe(c, n):
            (t, q), i = ITEMS[n], TILE[n]
            if n >= 2:
                pe.wait_ge(m["bound_ready"], c * GT + (n - 1))
                pe.matmul(B[q][:, CARRY:CARRY + HEADS], lastrow, decay[:, TILE[n - 2], :], start=True, stop=True)
            pe.wait_ge(m["xw_ready"], c * GT + (n + 1))
            if t < CHUNKS - 1:
                pe.matmul(B[q][0:STATE, 0:INNER], Bt[:, i, :], xw[:, i, :], start=True, stop=True).then_inc(m["state_made"], 1)
            pe.matmul(B[4 + q][:, 0:INNER], Gm[:, i, :], xw[:, i, :], start=True, stop=t == 0)
            if t > 0:
                pe.wait_ge(m["S_ready"], c * CARRIED + (n - 1))
                pe.matmul(B[4 + q][:, 0:INNER], CTs[:, i, :], S[:, q, (t - 1) % 2, :], start=False, stop=True)
            pe.wait_ge(m["wb_ready"], c * GT + (n + 1))
            pe.matmul(B[4 + q][:, INNER:2 * INNER], tri_bf[:, :], Wb[:, i, :], start=True, stop=True).then_inc(m["y_made"], 1)
            if n < GT - 2:
                project(n + 2, TILE[n + 2])

        def project(n, i):
            pe.matmul(B[2 + n % 2][:, :], xhT[:, i, :], WIN[:, 0:NZX], start=True, stop=True).then_inc(m["zx_made"], 1)

        def mix_act(r, g, c, general=False):
            first = isinstance(g, int) and g == 0
            act.wait_ge(m["norm_ready"], c + 1)
            for t in range(GT):
                normalise("x1", t, xh[:, t, :], tiles_of(X_, g)[t]).then_inc(m["xh_ready"], 1)
            for half in range(2):
                act.wait_ge(m["xhT_made"], c * 2 + (half + 1))
                act.activation(xhT[:, half * 4:(half + 1) * 4, :].rearrange("p t k -> p (t k)"), B[2 + half][:, :], ACT.Identity,
                               scale=vec[:, 0:1], bias=vec[:, 1:2]).then_inc(m["xhT_ready"], 1)
            if not first:
                route_act_rows(r, g - 1, 0, g - 1, tiles_of(X2_, g - 1))
            act.wait_ge(m["dt_in"], c + 1)
            act.activation(dt_p[:, :, :], dt_e[:, :, :], ACT.Exp).then_inc(m["dt_exp"], 1)
            act.wait_ge(m["b_made"], c + 1)
            act.activation(Bt[:, :, :].rearrange("p t n -> p (t n)"), B[7][:, 0:GT * STATE], ACT.Copy).then_inc(m["Bt_ready"], 1)
            for half in range(2):
                act.wait_ge(m["bcT_made"], c * 2 + (half + 1))
                at = slice(half * 4, (half + 1) * 4)
                act.activation(BTs[:, at, :].rearrange("p t k -> p (t k)"), B[4 + half][0:STATE, :], ACT.Copy)
                last = act.activation(CTs[:, at, :].rearrange("p t k -> p (t k)"), B[4 + half][STATE:2 * STATE, :], ACT.Copy)
            last.then_inc(m["bcT_ready"], 1)
            if general:
                if not first:
                    route_act_T(r, g - 1)
                    for half in range(2):
                        route_act_squares(r, g - 1, half)
                general_act(c)
            else:
                for n in range(2):
                    tanh_z(c, n, TILE[n])
                act.wait_ge(m["cum_made"], c + 1)
                cum = B[0][:, M_CUM:M_CUM + 2 * GT * HEADS].rearrange("p (k t h) -> p k t h", k=2, h=HEADS)
                act.activation(e_neg[:, :, :], cum[:, 0], ACT.Exp, scale=-1.0)
                act.activation(e_cum[:, :, :], cum[:, 0], ACT.Exp)
                act.activation(e_end[:, :, :], cum[:, 1], ACT.Exp).then_inc(m["exps_ready"], 1)
                act.wait_ge(m["Binf_ready"], c + 1)
                for n in range(GT):
                    act.wait_ge(m["xw_ready"], c * GT + (n + 1))
                    act.activation(Wb[:, TILE[n], :], xw[:, TILE[n], :], ACT.Abs, scale=Binf[:, TILE[n]:TILE[n] + 1])\
                        .then_inc(m["wb_ready"], 1)
                    if n < GT - 2:
                        tanh_z(c, n + 2, TILE[n + 2])
                    if not first and n == 1:
                        route_act_T(r, g - 1)
                    if not first and n == 4:
                        route_act_squares(r, g - 1, 0)
                if not first:
                    route_act_squares(r, g - 1, 1)
            act.wait_ge(m["y_norm_ready"], c + 1)
            for i in range(GT):
                normalise("y", i, yb[:, i, :], yb[:, i, :]).then_inc(m["yn_ready"], 1)
            if not first:
                route_act_exp(r, g - 1)
            for half in range(2):
                act.wait_ge(m["ynT_made"], c * 2 + (half + 1))
                for k in range(2):
                    last = act.activation(yT[:, k, half * 4:(half + 1) * 4, :].rearrange("p t j -> p (t j)"), B[2 + 2 * half + k][:, :],
                                          ACT.Identity, scale=vec[:, 2 + k:3 + k], bias=vec[:, 4 + k:5 + k])
                last.then_inc(m["yT_ready"], 1)

        def tanh_z(c, n, i):
            act.wait_ge(m["zx_made"], c * GT + (n + 1))
            act.activation(th[:, i, :], B[2 + n % 2][:, 0:INNER], ACT.Tanh, scale=0.5).then_inc(m["tanh_ready"], 1)

        def keep_x1(g, c):
            pool.wait_ge(m["xh_ready"], (c + 1) * GT)
            pool.tensor_tensor(X2_[:, bass.ds(g * (GT * D), GT * D)].rearrange("p (t d) -> p t d", d=D),
                               X_[:, bass.ds(g * (GT * D), GT * D)].rearrange("p (t d) -> p t d", d=D),
                               nob[:, :].unsqueeze(1).broadcast_to([P, GT, D]), ALU.add).then_inc(m["x1_kept"], 1)

        def last_pe(r, g):
            route_pe_transpose(r, g, 0)
            for half in range(2):
                route_pe_gate(r, g, half)
            route_pe_scores(r, g, 0)
            route_pe_rank(r, g)

        def last_act(r, g):
            route_act_rows(r, g, 0, g, tiles_of(X2_, g))
            route_act_T(r, g)
            for half in range(2):
                route_act_squares(r, g, half)
            route_act_exp(r, g)

        def last_dve(ch, r, g, c):
            finish_dve(ch, g, c)
            route_norm(ch, r, g, tiles_of(X2_, g))
            route_choose(ch, r, g, 0, g)

        gen = {k: sem(f"general_{k}") for k in (
            "log_ready", "decay_made", "tile_ready", "T_made", "c_made", "bc_ready", "bc_stored", "block_in", "block_used",
            "scanned", "y_made", "flag_sum", "flag_ready")}
        bc_rows = nc.dram_tensor("bc_rows", (1, SQ * SEQ * 2 * STATE), F32).ap()
        xs_T = G[:, 1, 0:GT].rearrange("p (c a) d -> p c (a d)", c=2)
        da_T = G[:, 1, GT:2 * GT].rearrange("p (c a) d -> p c (a d)", c=2)
        ys_T = xT[:, :].rearrange("p (c n) -> p c n", c=2)
        decay_w = G[:, 0].rearrange("p (t a) d -> p t (a d)", a=2)
        bc = ob
        bc_all = sq[:, 1].rearrange("p j n -> p (j n)")

        def general_dve(ch, g, c):
            ch(v.tensor_scalar(decay[:, :, :], dt_p[:, :, :], LOG_CAP, None, ALU.min))
            ch.sync()
            v.sem_inc(gen["log_ready"], 1)
            v.wait_ge(gen["c_made"], g + 1)
            v.wait_ge(m["Bt_ready"], c + 1)
            ch(v.tensor_copy(bc[:, :, 0:STATE], Bt[:, :, :]))
            ch(v.tensor_copy(bc[:, :, STATE:2 * STATE], B[6][:, 0:GT * STATE].rearrange("p (t n) -> p t n", n=STATE)))
            ch.sync()
            v.sem_inc(gen["bc_ready"], 1)
            v.wait_ge(gen["decay_made"], g + 1)
            for q in range(SQ):
                general_sequence(ch, g, c, q)

        def general_sequence(ch, g, c, q):
            seq, blocks = g * SQ + q, SEQ // BLOCK
            for i in range(q * CHUNKS, (q + 1) * CHUNKS):
                gate_and_skip(ch, c, i, i)
                ch.sync()
                ch(v.tensor_copy(heads(decay_w[:, i, :]), per_head(e_cum[:, i, :])))
                ch(v.tensor_copy(xw[:, i, :], B[2 + i % 2][:, INNER:NZX]))
                ch.sync()
                v.sem_inc(m["xw_ready"], 1)
            v.wait_ge(gen["T_made"], seq + 1)
            for k in range(2):
                ch(v.tensor_copy(xs_T[:, k, :], B[4 + k][:, :]))
                ch(v.tensor_copy(da_T[:, k, :], B[7 * k][:, :]))
            ch(v.memset(state, 0.0))
            ch.restart()
            with v.Fori(0, blocks) as blk:
                wait_on(v, gen["block_in"], seq * (16 * blocks) + (blk * 16 + 16))
                with v.Fori(0, BLOCK) as tt:
                    def over_n(a):
                        return a[:, :, bass.ds(blk * BLOCK + tt, 1)].broadcast_to([P, 2, STATE])

                    def over_c(at):
                        return bc_all[:, bass.ds(tt * (2 * STATE) + at, STATE)].unsqueeze(1).broadcast_to([P, 2, STATE])
                    ch(v.tensor_tensor(step_u, over_c(0), over_n(xs_T), ALU.mult))
                    ch(v.tensor_tensor(state, state, over_n(da_T), ALU.mult))
                    ch.sync()
                    ch(v.tensor_tensor(state, state, step_u, ALU.add))
                    ch.sync()
                    ch(v.tensor_scalar(state, state, 10.0, -10.0, ALU.min, ALU.max))
                    ch.sync()
                    ch(v.tensor_tensor(step_u, state, over_c(STATE), ALU.mult))
                    ch.sync()
                    ch(v.tensor_reduce(ys_T[:, :, bass.ds(blk * BLOCK + tt, 1)], step_u, AX.X, ALU.add))
                    ch.restart()
                v.sem_inc(gen["block_used"], 1)
            v.sem_inc(gen["scanned"], 1)
            v.wait_ge(gen["y_made"], seq + 1)
            for t in range(CHUNKS):
                i = q * CHUNKS + t
                ch(v.tensor_scalar(yb[:, i, :], B[4 + t // 2][:, (t % 2) * INNER:(t % 2 + 1) * INNER], 0.5, None, ALU.mult))
                ch.sync()
                ch(v.tensor_tensor(yb[:, i, :], yb[:, i, :], xd[:, i, :], ALU.add))
                ch.sync()
                ch(v.tensor_tensor(yb[:, i, :], yb[:, i, :], zs[:, i, :], ALU.mult))
            ch.sync()

        def general_pe(c):
            g = c - GROUPS
            pe.wait_ge(gen["log_ready"], g + 1)
            for i in range(GT):
                last = pe.matmul(B[6][:, i * STATE:(i + 1) * STATE], xhT[:, i, :],
                                 WIN[:, C_BC + STATE:C_BC + 2 * STATE], start=True, stop=True)
            last.then_inc(gen["c_made"], 1)
            for q in range(SQ):
                seq = g * SQ + q
                if q > 0:
                    pe.wait_ge(m["xw_ready"], c * GT + (q * CHUNKS + 1))
                for t in range(CHUNKS):
                    i = q * CHUNKS + t
                    pe.wait_ge(m["xw_ready"], c * GT + (i + 1))
                    if i < GT - 2:
                        project(i + 2, i + 2)
                    for k in range(2):
                        part = slice(k * P, (k + 1) * P)
                        pe.transpose(B[4 + k][:, t * P:(t + 1) * P], xw[:, i, part], ident)
                        last = pe.transpose(B[7 * k][:, t * P:(t + 1) * P], decay_w[:, i, part], ident)
                last.then_inc(gen["T_made"], 1)
                pe.wait_ge(gen["scanned"], seq + 1)
                for t in range(CHUNKS):
                    for k in range(2):
                        at = (t % 2) * INNER + k * P
                        last = pe.transpose(B[4 + t // 2][:, at:at + P], ys_T[:, k, t * P:(t + 1) * P], ident)
                last.then_inc(gen["y_made"], 1)

        def general_act(c):
            g = c - GROUPS
            act.wait_ge(gen["log_ready"], g + 1)
            act.activation(e_cum[:, :, :], decay[:, :, :], ACT.Exp).then_inc(gen["decay_made"], 1)
            for i in range(GT):
                tanh_z(c, i, i)

        def general_sp(g):
            blocks = SQ * SEQ // BLOCK
            wait_on(sp, gen["bc_ready"], g + 1)
            sp.dma_start(bc_rows.rearrange("o (t p n) -> (o p) t n", p=P, n=2 * STATE), bc[:, :, :]).then_inc(gen["bc_stored"], 16)
            wait_on(sp, gen["bc_stored"], g * 16 + 16)

            def block_in(blk):
                sp.dma_start(bc_all, bc_rows[:, bass.ds(blk * (BLOCK * 2 * STATE), BLOCK * 2 * STATE)]
                             .broadcast_to([P, BLOCK * 2 * STATE])).then_inc(gen["block_in"], 16)
            block_in(0)
            with sp.Fori(1, blocks) as blk:
                sp.wait_ge(gen["block_used"], g * blocks + blk)
                block_in(blk)

        def flagged(eng):
            eng.wait_ge(gen["flag_ready"], 1)
            return eng.value_load(flag[0:1, 0:1], min_val=0, max_val=1) > 0

        r1, e1 = route_sems(1, SLOTS, (4, 5), (0, 2)), expert_sems(1)
        tab1, zidx1, slots1 = sem("tab1_ready"), sem("zidx1_ready"), sem("slots1_ready")
        r2, r3, e2 = route_sems(2, 1, (6, 7), (0,)), route_sems(3, 1, (6, 7), (1,)), expert_sems(2)
        tab2, zidx2, slots2 = sem("tab2_ready"), sem("zidx2_ready"), sem("slots2_ready")
        gathered_f = [sem(f"gathered_f{q}") for q in range(2)]
        combined_f, stored_f = sem("combined_f"), [sem(f"stored_f{q}") for q in range(2)]

        @block.sync
        def _(_e):
            part = [slice(k * TILES // 4, (k + 1) * TILES // 4) for k in range(4)]
            x_tiles = x.rearrange("(n p) d -> p n d", p=P)
            sp.dma_start(cst[:, :], consts).then_inc(loaded_first, 16)
            sp.dma_start(X[:, part[0], :], x_tiles[:, part[0], :]).then_inc(loaded_x[0], 16)
            sp.dma_start(WAT[:, :], wA_T).then_inc(loaded_first, 16)
            for k in range(1, 4):
                sp.dma_start(X[:, part[k], :], x_tiles[:, part[k], :]).then_inc(loaded_x[k], 16)
            sp.dma_start(WA, wA).then_inc(loaded, 16)
            sp.dma_start(WBT, wB_T).then_inc(loaded, 16)
            sp.dma_start(WUG[:, :, 0:F], wUp_T).then_inc(loaded, 16)
            sp.dma_start(WDT[:, :, :, :], wDn_T).then_inc(loaded, 16)
            sp.dma_start(vec[:, :], vecs).then_inc(loaded, 16)
            for dst, src in ((nAb, A_log), (dtb, dt_bias), (Dh, Dparam), (now, no_w), (nob, no_b)):
                sp.dma_start(dst[:, :], src.broadcast_to([P, src.shape[1]])).then_inc(loaded, 16)
            sp.dma_start(WIN[:, :], in_T).then_inc(loaded, 16)
            sp.dma_start(WOUT[:, :, :], out_T).then_inc(loaded, 16)
            sp.wait_ge(zeros_ready, 1)
            for n in range(2):
                sp.dma_start(xg[n][E * REG:E * REG + SPARE, :].rearrange("(p n) d -> p n d", p=P), zeros[:, :, :])\
                    .then_inc(zeroed[n], 16)
            experts_sp(e1, 0, r1, tab1, swept[0], SLOTS)
            with sp.If(flagged(sp)):
                with sp.Fori(0, GROUPS) as g:
                    general_sp(g)
            experts_sp(e2, 1, r2, tab2, swept[1], 1)

            def store(g, q):
                sp.wait_ge(combined_f, g + 1)
                sp.dma_start(out[bass.ds(g * (GT * P), GT * P), :].rearrange("(t p) d -> p t d", p=P), fin[:, q, :, :])\
                    .then_inc(stored_f[q], 16)
            with sp.Fori(0, GROUPS // 2) as turn:
                for q in range(2):
                    store(turn * 2 + q, q)
            for q in range(2):
                sp.wait_ge(stored_f[q], 16 * (GROUPS // 2))

        @block.vector
        def _(_e):
            ch = Chain(v, dve_own)
            ch(v.memset(zeros[:, :, :], 0.0))
            ch(v.memset(ones_bf[:, :], 1.0))
            ch(v.memset(zeros_bf[:, :], 0.0))
            ch(v.memset(ones[:, :], 1.0))
            for tab in (tab_up, tab_down):
                ch(v.memset(tab[:, :], 0))
            ch(v.memset(ok_state[:, :, :], 1.0))
            ch(v.memset(ok_decay[:, :, :], 1.0))
            v.wait_ge(loaded_first, 16 * 2)
            ch(v.tensor_copy(strict_bf[:, :], cst[:, C_STRICT:C_STRICT + P]))
            ch(v.tensor_copy(tri_bf[:, :], tri))
            ch(v.tensor_copy(base[:, :], cst[:, C_REG:C_REG + E]))
            ch.restart()
            v.sem_inc(zeros_ready, 1)

            def turn_of_groups(turn, last):
                for q in range(SLOTS):
                    g = turn * SLOTS + q
                    if not (last and q == SLOTS - 1):
                        route_norm(ch, r1, g + 1, tiles_of(X_, g + 1))
                    route_choose(ch, r1, g, q, turn)
                    ch.restart()
            v.wait_ge(loaded_x[0], 16)
            route_norm(ch, r1, 0, tiles_of(X_, 0))
            for k in range(1, 4):
                v.wait_ge(loaded_x[k], 16)
            turn_of_groups(0, False)
            with v.Fori(1, GROUPS // SLOTS - 1) as turn:
                turn_of_groups(turn, False)
            turn_of_groups(GROUPS // SLOTS - 1, True)
            tables(ch, tab1, zidx1, slots1)
            v.wait_ge(A_exp, 1)
            ch(v.tensor_scalar(nAb[:, :], nAb[:, :], -1.0, None, ALU.mult))
            ch(v.tensor_scalar(Dh[:, :], Dh[:, :], 0.5, None, ALU.mult))
            ch.sync()
            ch(v.tensor_copy(heads(Dbc[:, :]), per_head(Dh[:, :])))
            ch.restart()
            experts_dve(e1)
            ch(v.tensor_copy(base[:, :], cst[:, C_REG:C_REG + E]))
            ch.sync()
            for g in range(2):
                mix_dve(ch, r2, g, g)
                ch.restart()
            with v.Fori(2, GROUPS) as g:
                mix_dve(ch, r2, g, g)
                ch.restart()
            last_dve(ch, r2, GROUPS - 1, GROUPS - 1)
            ch(v.tensor_tensor(bnd[:, :, :], ok_state[:, :, :], ok_decay[:, :, :], ALU.mult))
            ch.sync()
            ch(v.tensor_reduce(ok_all[:, :], bnd[:, :, :].rearrange("p t h -> p (t h)"), AX.X, ALU.min))
            ch.sync()
            v.sem_inc(gen["flag_sum"], 1)
            v.wait_ge(gen["flag_sum"], 2)
            ch(v.tensor_scalar(flag[:, :], B[7][:, 0:1], P - 0.5, None, ALU.is_lt))
            ch.restart()
            v.sem_inc(gen["flag_ready"], 1)
            with v.If(flagged(v)):
                v.wait_ge(r2["scattered"][0], 16 * GT * K2 * GROUPS)
                v.tensor_copy(base[:, :], cst[:, C_REG:C_REG + E]).then_inc(dve_own, 1)
                v.wait_ge(dve_own, 1)
                v.sem_clear(dve_own)
                again = Chain(v, dve_own)
                for g in range(2):
                    mix_dve(again, r3, g, g + GROUPS, True)
                    again.restart()
                with v.Fori(2, GROUPS) as g:
                    mix_dve(again, r3, g, g + GROUPS, True)
                    again.restart()
                last_dve(again, r3, GROUPS - 1, 2 * GROUPS - 1)
                again.restart()
            tables(ch, tab2, zidx2, slots2)
            ch.restart()
            experts_dve(e2)

            def combine_last(turn):
                for q in range(2):
                    g = turn * 2 + q
                    v.wait_ge(gathered_f[q], (turn + 1) * (16 * GT * K2))
                    after(v, stored_f[q], turn * 16)
                    combine(ch, 1, g, q, tiles_of(X2_, g), [fin[:, q, t, :] for t in range(GT)])
                    v.sem_inc(combined_f, 1)
                ch.restart()
            combine_last(0)
            with v.Fori(1, GROUPS // 2) as turn:
                combine_last(turn)

        @block.tensor
        def _(_e):
            pe.wait_ge(loaded_first, 16 * 2)
            pe.wait_ge(zeros_ready, 1)

            def turn_of_groups(turn, last):
                for q in range(SLOTS):
                    g = turn * SLOTS + q
                    if not (last and q == SLOTS - 1):
                        route_pe_transpose(r1, g + 1, (q + 1) % SLOTS)
                    route_pe_rank(r1, g)
                    if not (last and q == SLOTS - 1):
                        for half in range(2):
                            route_pe_gate(r1, g + 1, half)
                        route_pe_scores(r1, g + 1, (q + 1) % SLOTS)
            route_pe_transpose(r1, 0, 0)
            for half in range(2):
                route_pe_gate(r1, 0, half)
            route_pe_scores(r1, 0, 0)
            turn_of_groups(0, False)
            with pe.Fori(1, GROUPS // SLOTS - 1) as turn:
                turn_of_groups(turn, False)
            turn_of_groups(GROUPS // SLOTS - 1, True)
            pe.wait_ge(loaded, 16 * LOADS)
            for e in range(E):
                if e >= 4:
                    pe.wait_ge(wab_kept, e - 3)
                pe.matmul(B[2 + e % 4][:, 0:F], WA[:, e * D:(e + 1) * D], WBT[:, e * F:(e + 1) * F], start=True, stop=True)\
                    .then_inc(wab_ready, 1)
            pe.wait_ge(wab_kept, E)
            experts_pe(e1, tab1)
            for g in range(2):
                mix_pe(r2, g, g)
            with pe.Fori(2, GROUPS) as g:
                mix_pe(r2, g, g)
            last_pe(r2, GROUPS - 1)
            pe.wait_ge(gen["flag_sum"], 1)
            pe.matmul(B[7][:, 0:1], ones[:, :], ok_all[:, :], start=True, stop=True).then_inc(gen["flag_sum"], 1)
            with pe.If(flagged(pe)):
                for g in range(2):
                    mix_pe(r3, g, g + GROUPS, True)
                with pe.Fori(2, GROUPS) as g:
                    mix_pe(r3, g, g + GROUPS, True)
                last_pe(r3, GROUPS - 1)
            experts_pe(e2, tab2)

        @block.scalar
        def _(_e):
            def turn_of_groups(turn, last):
                for q in range(SLOTS):
                    g = turn * SLOTS + q
                    if not (last and q == SLOTS - 1):
                        route_act_rows(r1, g + 1, (q + 1) % SLOTS, turn + (q == SLOTS - 1), tiles_of(X_, g + 1))
                    route_act_exp(r1, g)
                    if not (last and q == SLOTS - 1):
                        route_act_T(r1, g + 1)
                        for half in range(2):
                            route_act_squares(r1, g + 1, half)
            route_act_rows(r1, 0, 0, 0, tiles_of(X_, 0))
            route_act_T(r1, 0)
            for half in range(2):
                route_act_squares(r1, 0, half)
            turn_of_groups(0, False)
            with act.Fori(1, GROUPS // SLOTS - 1) as turn:
                turn_of_groups(turn, False)
            turn_of_groups(GROUPS // SLOTS - 1, True)
            act.wait_ge(loaded, 16 * LOADS)
            act.activation(nAb[:, :], nAb[:, :], ACT.Exp).then_inc(A_exp, 1)
            for e in range(E):
                act.wait_ge(wab_ready, e + 1)
                act.activation(WUG[:, e, F:2 * F], B[2 + e % 4][:, 0:F], ACT.Copy).then_inc(wab_kept, 1)
            experts_act(e1)
            for g in range(2):
                mix_act(r2, g, g)
            with act.Fori(2, GROUPS) as g:
                mix_act(r2, g, g)
            last_act(r2, GROUPS - 1)
            with act.If(flagged(act)):
                act.wait_ge(r2["scattered"][0], 16 * GT * K2 * GROUPS)
                for g in range(2):
                    mix_act(r3, g, g + GROUPS, True)
                with act.Fori(2, GROUPS) as g:
                    mix_act(r3, g, g + GROUPS, True)
                last_act(r3, GROUPS - 1)
            experts_act(e2)

        @block.gpsimd
        def _(_e):
            with pool.Fori(0, GROUPS // SLOTS) as turn:
                for q in range(SLOTS):
                    route_pool(r1, 0, turn * SLOTS + q, q)
            sweep(0, zidx1, swept[0])
            experts_pool(e1, 0)
            all_stored(pool, e1)
            pool.wait_ge(slots1, 1)
            gather(0, 0, 0, 1, gathered_m)
            pool.wait_ge(m["combined"], 1)
            gather(0, 1, 0, 2, gathered_m)
            keep_x1(0, 0)
            with pool.Fori(1, GROUPS - 1) as g:
                pool.wait_ge(m["combined"], g + 1)
                gather(0, g + 1, 0, g + 2, gathered_m)
                keep_x1(g, g)
                route_pool(r2, 1, g - 1, 0)
            keep_x1(GROUPS - 1, GROUPS - 1)
            for g in range(GROUPS - 2, GROUPS):
                route_pool(r2, 1, g, 0)
            with pool.If(flagged(pool)):
                keep_x1(0, GROUPS)
                with pool.Fori(1, GROUPS) as g:
                    keep_x1(g, g + GROUPS)
                    route_pool(r3, 1, g - 1, 0)
                route_pool(r3, 1, GROUPS - 1, 0)
                pool.wait_ge(r3["scattered"][0], 16 * GT * K2 * GROUPS)
            sweep(1, zidx2, swept[1])
            experts_pool(e2, 1)
            all_stored(pool, e2)
            pool.wait_ge(slots2, 1)

            def gather_last(g, q):
                gather(1, g, q, g + (GROUPS + 1), gathered_f[q])
            for q in range(2):
                gather_last(q, q)
            with pool.Fori(1, GROUPS // 2) as turn:
                for q in range(2):
                    g = turn * 2 + q
                    pool.wait_ge(combined_f, g - 1)
                    gather_last(g, q)


def kernel(**inputs):
    import numpy as np
    import concourse.bacc as bacc
    from concourse.bass_utils import run_bass_kernel_spmd

    a = {k.replace("L0_", ""): np.asarray(i) for k, i in inputs.items()}
    cc = np.ascontiguousarray
    k, m = np.arange(P)[:, None], np.arange(P)[None, :]
    consts = np.zeros((P, C_N), np.float32)
    consts[:, C_ID:C_ID + P] = k == m
    consts[:, C_TRI:C_TRI + P] = k <= m
    consts[:, C_STRICT:C_STRICT + P] = k < m
    consts[P - 1, C_LAST:C_LAST + P] = 1
    consts[:, C_IOTA:C_IOTA + E] = np.arange(E)
    consts[:, C_REG:C_REG + E] = np.arange(E) * REG
    consts[:, C_PART] = np.arange(P)
    for j in range(E // 2):
        for e in range(E):
            consts[:, C_BLK + j * E + e] = 2 * j + np.arange(P) // R == e
    consts[:, C_ROW:C_ROW + ETILES] = np.arange(ETILES) * P
    win = a["attn_in_proj_w"].T
    o = 2 * INNER
    win = np.concatenate([win[:, 0:o], win[:, o + 2 * STATE:], win[:, o:o + 2 * STATE]], axis=1)
    halves = lambda w: w.reshape(2, P).T
    arrays = {
        "x": cc(a["attn_x"].reshape(TOK, D)),
        "consts": consts,
        "wA_T": cc(a["ffn_W_A"].transpose(2, 0, 1).reshape(D, E * R)),
        "wA": cc(a["ffn_W_A"].transpose(1, 0, 2).reshape(R, E * D)),
        "wB_T": cc(a["ffn_W_B"].transpose(2, 0, 1).reshape(R, E * F)),
        "wUp_T": cc(a["ffn_W_up"].transpose(2, 0, 1)),
        "wDn_T": cc(a["ffn_W_down"].transpose(2, 0, 1).reshape(2, P, E, D).transpose(1, 2, 0, 3)),
        "in_T": cc(win),
        "out_T": cc(a["attn_out_proj_w"].T.reshape(2, P, D).transpose(1, 0, 2)),
        "vecs": cc(np.concatenate([a["attn_ni_w"][:, None], a["attn_ni_b"][:, None],
                                   halves(a["attn_ln_w"]), halves(a["attn_ln_b"])], axis=1)),
        "dt_bias": cc(a["attn_dt_bias"].reshape(1, HEADS)),
        "A_log": cc(a["attn_A_log"].reshape(1, HEADS)),
        "Dparam": cc(a["attn_Dparam"].reshape(1, HEADS)),
        "no_w": cc(a["attn_no_w"].reshape(1, D)),
        "no_b": cc(a["attn_no_b"].reshape(1, D)),
    }
    nc = bacc.Bacc("TRN2", target_bir_lowering=False, num_devices=1)
    args = [nc.dram_tensor(n, v.shape, F32, kind="ExternalInput").ap() for n, v in arrays.items()]
    args.append(nc.dram_tensor("out", (TOK, D), F32, kind="ExternalOutput").ap())
    macaron(nc, *args)
    res = run_bass_kernel_spmd(nc, [arrays], core_ids=[0])
    return res.results[0]["out"].reshape(BATCH, SEQ, D)
```

```python
import numpy as np
import concourse.bass as bass
from concourse import mybir
from contextlib import ExitStack

F32 = mybir.dt.float32
BF16 = mybir.dt.bfloat16
I32 = mybir.dt.int32
U32 = mybir.dt.uint32
ALU = mybir.AluOpType
ACT = mybir.ActivationFunctionType
AX = mybir.AxisListType

P = 128
BATCH, SEQ, D = 16, 512, 128
TOK = BATCH * SEQ
TILES = TOK // P
SQ = 2
CHUNKS = SEQ // P
GT = SQ * CHUNKS
GROUPS = TILES // GT
SLOTS = 4
E, K2, R, F = 8, 2, 64, 256
INNER, STATE, HEADS, HD = 256, 64, 4, 64
REG = TOK + P
ETILES = TOK * K2 // P + E
SPARE = E * P
ROW = D + 4
C_W, C_DW, C_E2, C_TOKEN = D, D + 1, D + 2, D + 3
EPS = 1e-5
MAGIC = float(0x5F3759DF)
NZX = 2 * INNER
C_DT, C_BC = NZX, NZX + HEADS
NDB = HEADS + STATE
ITEMS = [(t, q) for t in range(CHUNKS) for q in range(SQ)]
TILE = [q * CHUNKS + t for t, q in ITEMS]
ROWS_AT, T_AT = {n: range(2 * n - 2, 2 * n) for n in range(1, 5)}, 5
GATE_AT = [(), (), (), (), (), (), (), (0, 1, 2, 3, 4, 5, 6, 7)]
CARRIED = (CHUNKS - 1) * SQ
CARRY = INNER
M_CUM, M_TOT = 0, GT * HEADS
BLOCK = 16
STATE_MAX = 9.8
DECAY_MIN = -0.5
LOADS = 12
LOG_CAP = float(np.log(0.99))

C_ID, C_TRI, C_STRICT, C_LAST = 0, P, 2 * P, 3 * P
C_IOTA = 4 * P
C_REG = C_IOTA + E
C_ROW = C_REG + E
C_TOK = C_ROW + ETILES
C_N = C_TOK + GT


class Chain:

    def __init__(self, eng, sem):
        self.eng, self.sem, self.n = eng, sem, 0

    def __call__(self, ins):
        self.n += 1
        return ins.then_inc(self.sem, 1)

    def sync(self, upto=None):
        self.eng.wait_ge(self.sem, upto or self.n)

    def restart(self):
        self.sync()
        self.eng.sem_clear(self.sem)
        self.n = 0


def macaron(nc, x, consts, no_rows, wA_T, wA, wB_T, wUp_T, wDn_T, in_T, out_T, vecs, dt_bias, A_log, Dparam,
            no_w, no_b, out):
    ctx = ExitStack()
    with ctx:
        def sb(name, shape, dt=F32):
            return ctx.enter_context(nc.sbuf_tensor(name, shape, dt))

        def ps(name, shape=(P, 512), dt=F32):
            return ctx.enter_context(nc.psum_tensor(name, list(shape), dt))

        def sem(name):
            return ctx.enter_context(nc.semaphore(name))

        xg = [nc.dram_tensor(f"rows_by_expert{n}", (E * REG + SPARE, ROW), F32).ap() for n in range(2)]
        yg = [nc.dram_tensor(f"expert_results{n}", (K2 * TOK + 2 * SPARE, D), F32).ap() for n in range(2)]

        X = sb("X", [P, TILES, D])
        X2 = sb("X2", [P, TILES, D])
        cst = sb("cst", [P, C_N])
        WAT = sb("WAT", [P, E * R])
        work = sb("work", [P, 3, GT, INNER])
        wide = work[:, :, :, :].rearrange("p k t n -> p (k t n)")
        WBT, WA = wide[0:R, 0:E * F], wide[0:R, E * F:E * (F + D)]
        WUG = sb("WUG", [P, E, 2 * F])
        WDT = sb("WDT", [P, E, 2, D])
        WIN = sb("WIN", [P, NZX + HEADS + 2 * STATE])
        WOUT = sb("WOUT", [P, 2, D])
        ident, tri = cst[:, C_ID:C_ID + P], cst[:, C_TRI:C_TRI + P]
        lastrow = cst[:, C_LAST:C_LAST + P]
        strict_bf = sb("strict_bf", [P, P], BF16)
        tri_bf = sb("tri_bf", [P, P], BF16)
        ones_bf = sb("ones_bf", [P, P], BF16)
        zeros_bf = sb("zeros_bf", [P, P], BF16)
        ones = sb("ones", [P, P])
        vec = sb("vec", [P, 6])
        nAb = sb("nAb", [P, HEADS])
        dtb = sb("dtb", [P, HEADS])
        Dh = sb("Dh", [P, HEADS])
        Dbc = sb("Dbc", [P, INNER])
        now, nob = sb("now", [P, D]), sb("nob", [P, D])

        OH = sb("OH", [P, TILES * K2, E], BF16)
        slot_f = sb("slot_f", [P, GT * K2])
        tokens = sb("tokens", [P, GT])
        base = sb("base", [P, E])
        rows_X2 = X2[:, :, :].rearrange("p n d -> p (n d)")[:, 0:(SLOTS - 1) * GT * ROW]\
            .rearrange("p (q t d) -> p q t d", q=SLOTS - 1, t=GT)
        xn = [sb("xn", [P, GT, ROW])] + [rows_X2[:, k] for k in range(SLOTS - 1)]
        xT = sb("xT", [P, GT * P])
        G_sq = sb("G_sq", [P, 3, GT * K2, D])
        G = G_sq[:, 0:2]
        sq = G_sq[:, 1:3].rearrange("p q (j a) d -> p q j (a d)", j=E // 2)
        ss, sc = sb("ss", [P, GT, E]), sb("sc", [P, GT, E])
        nt1, nt2 = sb("nt1", [P, GT * E]), sb("nt2", [P, GT * E])
        mx, mi = sb("mx", [P, GT, 8]), sb("mi", [P, GT, 8], U32)
        mif = sb("mif", [P, GT, K2])
        pre = sb("pre", [P, GT, E])
        pick = sb("pick", [P, GT * K2, E])
        slot_u = [sb(f"slot_u{q}", [P, GT * K2], U32) for q in range(SLOTS)]
        ediff, eexp, den = sb("ediff", [P, GT]), sb("eexp", [P, GT]), sb("den", [P, GT])
        st = sb("st", [P, GT, 6])
        lnv = sb("lnv", [P, GT])
        norms = {n: (sb(f"mv_{n}", [P, GT, 2]), sb(f"rstd_{n}", [P, GT]), sb(f"shift_{n}", [P, GT]))
                 for n in ("x1", "rows", "y", "o")}
        cnt, cnt_i, ntl, tend = sb("cnt", [P, E]), sb("cnt_i", [P, E], I32), sb("ntl", [P, E]), sb("tend", [P, E])
        tadj = sb("tadj", [P, E])
        GW = sb("GW", [P, 2, GT * P])
        below = GW[:, :, :].rearrange("p k n -> p (k n)")[:, 0:ETILES * E].rearrange("p (j e) -> p j e", e=E)
        Gm, Wb = GW[:, 0].rearrange("p (t k) -> p t k", k=P), GW[:, 1].bitcast(BF16).rearrange("p (t n) -> p t n", n=INNER)
        yT = GW[:, :, :].rearrange("p k (t j) -> p k t j", j=P)
        row_f, exp_f = sb("row_f", [P, ETILES]), sb("exp_f", [P, ETILES])
        tab_row = sb("tab_row", [P, ETILES], I32)
        tab_expert = sb("tab_expert", [P, ETILES], I32)
        zidx = sb("zidx", [P, E], I32)
        ex = wide[:, E * (F + D):]

        def ex_part(at, *shape):
            n = int(np.prod(shape))
            names = "abc"[:len(shape)]
            return ex[:, at:at + n].rearrange(f"p ({' '.join(names)}) -> p {' '.join(names)}", **dict(zip(names, shape)))
        xr, yo = ex_part(0, 4, ROW), ex_part(4 * ROW, 4, D)
        at = 4 * (ROW + D)
        xrT, hT = ex_part(at, 2, P), ex_part(at + 2 * D, 2, 2, P)
        sg, hh = ex_part(at + 6 * D, 2, F), ex_part(at + 6 * D + 2 * F, 2, F)
        is_2nd, w_row, y_row = sb("is_2nd", [P, 8]), sb("w_row", [P, 8]), sb("y_row", [P, 8], I32)
        fin = work[:, 0:2].rearrange("p k t n -> p (k t n)").rearrange("p (q t d) -> p q t d", q=4, d=D)[:, 0:2]
        xh, xhT = sb("xh", [P, GT, D]), sb("xhT", [P, GT, P])
        ob = sb("ob", [P, GT, D])
        row_last = sb("row_last", [P, GT, ROW])
        BTs, CTs = sb("BTs", [STATE, GT, P]), sb("CTs", [STATE, GT, P])
        Bt, Binf = sb("Bt", [P, GT, STATE]), sb("Binf", [P, GT])
        dt_e, dt_z, dt_q, dt_p, decay = [sb(n, [P, GT, HEADS]) for n in ("dt_e", "dt_z", "dt_q", "dt_p", "decay")]
        e_cum, e_neg, e_end, h_cum = [sb(n, [P, GT, HEADS]) for n in ("e_cum", "e_neg", "e_end", "h_cum")]
        th, xd, xw = [work[:, k] for k in range(3)]
        zs, yb = th, xw
        S = sb("S", [STATE, SQ, 2, INNER])
        kmax, bnd = sb("kmax", [P, SQ, HEADS]), sb("bnd", [P, GT, HEADS])
        ok_state, ok_decay = sb("ok_state", [P, GT, HEADS]), sb("ok_decay", [P, GT, HEADS])
        state_u = sb("state_u", [P, 2, 2, STATE])
        state, step_u = state_u[:, 0], state_u[:, 1]
        ok_all, flag = sb("ok_all", [P, 1]), sb("flag", [P, 1], I32)
        X_, X2_ = X[:, :, :].rearrange("p n d -> p (n d)"), X2[:, :, :].rearrange("p n d -> p (n d)")
        OH_ = OH[:, :, :].rearrange("p n e -> p (n e)")
        WUG_ = WUG[:, :, :].rearrange("p e f -> p (e f)")
        WDT_ = WDT[:, :, :, :].rearrange("p e c d -> p (e c d)")

        B = [ps(f"bank{n}") for n in range(8)]

        v, pe, act, pool, sp = nc.vector, nc.tensor, nc.scalar, nc.gpsimd, nc.sync

        loaded, loaded_first = sem("loaded"), sem("loaded_first")
        loaded_x = [sem(f"loaded_x{k}") for k in range(4)]
        wab_ready, wab_kept = sem("wab_ready"), sem("wab_kept")
        zeroed, swept = [sem(f"zeroed{n}") for n in range(2)], [sem(f"swept{n}") for n in range(2)]
        A_exp, masks_ready = sem("A_exp"), sem("masks_ready")
        dve_own = sem("dve_own")

        block = ctx.enter_context(nc.Block())

        passed = sem("passed")

        def wait_on(eng, semaphore, value):
            eng.wait_ge(semaphore, value)
            eng.sem_inc(passed, 1)

        def after(eng, semaphore, value):
            if not isinstance(value, int) or value > 0:
                eng.wait_ge(semaphore, value)

        def rsqrt(ch, dst, src, tmp):
            k = 3 / 8
            ch(v.tensor_scalar(dst.bitcast(I32), src.bitcast(I32), -0.5, MAGIC, ALU.mult, ALU.add))
            ch.sync()
            ch(v.tensor_tensor(tmp, dst, dst, ALU.mult))
            ch.sync()
            ch(v.tensor_tensor(tmp, tmp, src, ALU.mult))
            ch.sync()
            ch(v.scalar_tensor_tensor(out=tmp, in0=tmp, scalar=-10 / 3, in1=tmp, op0=ALU.add, op1=ALU.mult))
            ch.sync()
            ch(v.scalar_tensor_tensor(out=dst, in0=tmp, scalar=5.0, in1=dst, op0=ALU.add, op1=ALU.mult))
            ch.sync()
            ch(v.tensor_tensor(tmp, dst, dst, ALU.mult))
            ch.sync()
            ch(v.scalar_tensor_tensor(out=tmp, in0=tmp, scalar=-0.5 * k ** 3, in1=src, op0=ALU.mult, op1=ALU.mult))
            ch.sync()
            ch(v.scalar_tensor_tensor(out=dst, in0=tmp, scalar=1.5 * k, in1=dst, op0=ALU.add, op1=ALU.mult))
            ch.sync()

        def norm_stats(ch, name, srcs, scale=1.0, eps=EPS, order=range(GT), before={}):
            mv, rstd, shift = norms[name]
            for n, t in enumerate(order):
                if n in before:
                    before[n]()
                ch(v.bn_stats(st[:, t, :], srcs[t]))
            ch.sync()
            for t in range(len(srcs)):
                ch(v.bn_aggr(mv[:, t, :], st[:, t, :]))
            ch.sync()
            ch(v.tensor_scalar(lnv[:, :], mv[:, :, 1], scale, eps, ALU.mult, ALU.add))
            ch.sync()
            rsqrt(ch, rstd[:, :], lnv[:, :], nt1[:, 0:GT])
            ch(v.scalar_tensor_tensor(out=shift[:, :], in0=mv[:, :, 0], scalar=-1.0, in1=rstd[:, :], op0=ALU.mult, op1=ALU.mult))
            ch.sync()

        def normalise(name, t, dst, src):
            _, rstd, shift = norms[name]
            return act.activation(dst, src, ACT.Identity, scale=rstd[:, t:t + 1], bias=shift[:, t:t + 1])

        def tiles_of(arr, g):
            return [arr[:, bass.ds((g * GT + t) * D, D)] for t in range(GT)]

        def route_sems(n, slots, T, rows):
            names = ("norm_ready", "rows_ready", "rowsT_made", "rowsT_ready", "gate_made", "squared", "summed",
                     "chosen", "ranked", "diff_ready", "diff_exp", "placed")
            sems = {k: sem(f"gate{n}_{k}") for k in names}
            sems["n"] = min(n, 2) - 1
            sems["T"], sems["rows"] = T, rows
            sems["scattered"] = [sem(f"gate{n}_scattered{q}") for q in range(slots)]
            return sems

        def start_counts(ch):
            ch(v.tensor_copy(base[:, :], cst[:, C_REG:C_REG + E]))
            ch(v.tensor_copy(tokens[:, :], cst[:, C_TOK:C_TOK + GT]))

        def route_norm(ch, r, g, srcs):
            if not isinstance(g, int) or g > 0:
                wait_on(v, r["rows_ready"], g * GT)
            norm_stats(ch, "rows", srcs)
            v.sem_inc(r["norm_ready"], 1)

        def route_choose(ch, r, g):
            scores = ss[:, :, :].rearrange("p t e -> p (t e)")
            for t in range(GT):
                v.wait_ge(r["squared"], g * E + (t + 1))
                ch(v.tensor_reduce(ss[:, t, :], sq[:, t // 4, t % 4, :].rearrange("p (e r) -> p e r", r=R), AX.X, ALU.add))
            ch.sync()
            v.sem_inc(r["summed"], 1)
            c_ = sc[:, :, :].rearrange("p t e -> p (t e)")
            ch(v.tensor_scalar(nt2[:, :], scores, 1e-30, None, ALU.add))
            ch.sync()
            rsqrt(ch, c_, nt2[:, :], nt1[:, :])
            ch(v.tensor_tensor(c_, c_, scores, ALU.mult))
            ch.sync()
            for t in range(GT):
                ch(v.max(mx[:, t, :], sc[:, t, :]))
            ch.sync()
            v.tensor_tensor(ediff[:, :], mx[:, :, 1], mx[:, :, 0], ALU.subtract).then_inc(r["diff_ready"], 1)
            for t in range(GT):
                ch(v.max_index(mi[:, t, :], mx[:, t, :], sc[:, t, :]))
            ch.sync()
            ch(v.tensor_copy(mif[:, :, :], mi[:, :, 0:K2]))
            ch.sync()
            iota = cst[:, C_IOTA:C_IOTA + E].unsqueeze(1).broadcast_to([P, GT * K2, E])
            v.tensor_tensor(OH_[:, bass.ds(g * (GT * K2 * E), GT * K2 * E)].rearrange("p (n e) -> p n e", e=E), iota,
                            mif[:, :, :].rearrange("p t c -> p (t c)").unsqueeze(2).broadcast_to([P, GT * K2, E]),
                            ALU.is_equal).then_inc(r["chosen"], 1)

        def route_place(ch, r, g, q, turn):
            ranks = B[1]
            v.wait_ge(r["diff_exp"], g + 1)
            ch(v.tensor_scalar(den[:, :], eexp[:, :], 2.0, 2.0, ALU.mult, ALU.add))
            ch.sync()
            ch(v.reciprocal(den[:, :], den[:, :]))
            ch.sync()
            if not isinstance(turn, int) or turn > 0:
                wait_on(v, r["scattered"][q], turn * (16 * GT * K2))
            row = r["rows"][q]
            ch(v.tensor_copy(row[:, :, C_W:C_W + 1], den[:, :].unsqueeze(2)))
            ch(v.scalar_tensor_tensor(out=row[:, :, C_DW:C_DW + 1], in0=eexp[:, :].unsqueeze(2), scalar=-1.0,
                                      in1=den[:, :].unsqueeze(2), op0=ALU.add, op1=ALU.mult))
            ch(v.tensor_copy(row[:, :, C_E2:C_E2 + 1], mif[:, :, 1:2]))
            ch(v.tensor_copy(row[:, :, C_TOKEN:C_TOKEN + 1], tokens[:, :].unsqueeze(2)))
            ch.sync()
            ch(v.tensor_scalar(tokens[:, :], tokens[:, :], float(GT * P), None, ALU.add))
            v.wait_ge(r["ranked"], g + 1)
            ch(v.tensor_tensor(pre[:, :, :], ranks[:, 0:GT * E].rearrange("p (t e) -> p t e", e=E),
                               base[:, :].unsqueeze(1).broadcast_to([P, GT, E]), ALU.add))
            ch.sync()
            ch(v.tensor_tensor(base[:, :], ranks[:, GT * E:(GT + 1) * E], base[:, :], ALU.add))
            for c in range(K2):
                oh = OH_[:, bass.ds(g * (GT * K2 * E), GT * K2 * E)].rearrange("p (t c e) -> p t c e", c=K2, e=E)
                ch(v.tensor_tensor(pick[:, :, :].rearrange("p (t c) e -> p t c e", c=K2)[:, :, c, :], oh[:, :, c, :],
                                   pre[:, :, :], ALU.mult))
            ch.sync()
            ch(v.tensor_reduce(slot_f[:, :], pick[:, :, :], AX.X, ALU.add))
            ch.sync()
            v.tensor_copy(slot_u[q][:, :], slot_f[:, :]).then_inc(r["placed"], 1)

        def route_pe_transpose(r, g, q):
            after(pe, r["rowsT_ready"], g * 2)
            for t in range(GT):
                pe.wait_ge(r["rows_ready"], g * GT + (t + 1))
                at = (t % 4) * P
                last = pe.transpose(B[r["T"][t // 4]][:, at:at + P], r["rows"][q][:, t, 0:D], ident)
                if t % 4 == 3:
                    last.then_inc(r["rowsT_made"], 1)

        def route_pe_gate(r, g, t):
            halves = 2 if r["T"] == (6, 7) else t // 4 + 1
            pe.wait_ge(r["rowsT_ready"], g * 2 + halves)
            after(pe, r["squared"], g * E + (t - 1))
            pe.matmul(B[6 + t % 2][:, :], xT[:, t * P:(t + 1) * P], WAT[:, :], start=True, stop=True)\
                .then_inc(r["gate_made"], 1)

        def route_pe_all(r, g):
            for t in range(GT):
                route_pe_gate(r, g, t)

        def route_pe_rank(r, g):
            pe.wait_ge(r["chosen"], g + 1)
            after(pe, r["placed"], g)
            oh = OH_[:, bass.ds(g * (GT * K2 * E), GT * K2 * E)].rearrange("p (t c e) -> p t c e", c=K2, e=E)
            pe.matmul(B[1][:, 0:(GT + 1) * E], zeros_bf[:, :], tri_bf[:, 0:(GT + 1) * E], start=True, stop=False)
            for c in range(K2):
                pe.matmul(B[1][:, 0:GT * E], strict_bf[:, :], oh[:, :, c, :], start=False, stop=False)
            for before in range(1, GT + 1):
                for c in range(K2):
                    last = pe.matmul(B[1][:, before * E:(GT + 1) * E], ones_bf[:, :], oh[:, 0:GT + 1 - before, c, :],
                                     start=False, stop=before == GT and c == K2 - 1)
            last.then_inc(r["ranked"], 1)

        def route_act_rows(r, g, q, turn, srcs, tiles=range(GT)):
            if tiles[0] == 0:
                act.wait_ge(r["norm_ready"], g + 1)
                after(act, r["scattered"][q], turn * (16 * GT * K2))
            for t in tiles:
                normalise("rows", t, r["rows"][q][:, t, 0:D], srcs[t]).then_inc(r["rows_ready"], 1)

        def route_act_T(r, g):
            after(act, r["gate_made"], g * E)
            for half in range(2):
                act.wait_ge(r["rowsT_made"], g * 2 + (half + 1))
                act.activation(xT[:, half * 4 * P:(half + 1) * 4 * P], B[r["T"][half]][:, :], ACT.Copy)\
                    .then_inc(r["rowsT_ready"], 1)

        def route_act_square(r, g, k):
            if k == 0:
                after(act, r["summed"], g)
            act.wait_ge(r["gate_made"], g * E + (k + 1))
            act.activation(sq[:, k // (E // 2), k % (E // 2), :], B[6 + k % 2][:, :], ACT.Square)\
                .then_inc(r["squared"], 1)

        def route_act_exp(r, g):
            act.wait_ge(r["diff_ready"], g + 1)
            act.activation(eexp[:, :], ediff[:, :], ACT.Exp).then_inc(r["diff_exp"], 1)

        def scattered_all(eng, r):
            groups = (GROUPS - 1, 1) if len(r["scattered"]) == 2 else [GROUPS // SLOTS] * SLOTS
            for scattered, n in zip(r["scattered"], groups):
                eng.wait_ge(scattered, 16 * GT * K2 * n)

        def route_pool(r, n, g, q):
            wait_on(pool, r["placed"], g + 1)
            for t in range(GT):
                for c in range(K2):
                    i = t * K2 + c
                    pool.indirect_dma_start(xg[n], bass.IndirectOffsetOnAxis(ap=slot_u[q][:, i:i + 1], axis=0),
                                            r["rows"][q][:, t, :], None).then_inc(r["scattered"][q], 16)

        def tables(ch, tab_ready, zidx_ready):
            reg = cst[:, C_REG:C_REG + E]
            ch(v.tensor_copy(zidx[:, :], base[:, :]))
            ch(v.tensor_tensor(cnt[:, :], base[:, :], reg, ALU.subtract))
            ch.sync()
            v.sem_inc(zidx_ready, 1)
            ch(v.tensor_scalar(cnt_i[:, :], cnt[:, :], float(P - 1), None, ALU.add))
            ch.sync()
            ch(v.tensor_scalar(cnt_i[:, :], cnt_i[:, :], 7, None, ALU.arith_shift_right))
            ch.sync()
            ch(v.tensor_copy(ntl[:, :], cnt_i[:, :]))
            ch.sync()
            ch(v.tensor_copy(tend[:, 0:1], ntl[:, 0:1]))
            ch.sync()
            for e in range(1, E):
                ch(v.tensor_tensor(tend[:, e:e + 1], tend[:, e - 1:e], ntl[:, e:e + 1], ALU.add))
                ch.sync()
            ch(v.tensor_scalar(tadj[:, :], ntl[:, :], -float(P), float(REG), ALU.mult, ALU.add))
            ch.sync()
            rows = cst[:, C_ROW:C_ROW + ETILES]
            ch(v.tensor_scalar(row_f[:, :], rows, 1.0 / P, None, ALU.mult))
            ch.sync()
            ch(v.tensor_tensor(below[:, :, :], row_f[:, :].unsqueeze(2).broadcast_to([P, ETILES, E]),
                               tend[:, :].unsqueeze(1).broadcast_to([P, ETILES, E]), ALU.is_ge))
            ch.sync()
            ch(v.tensor_reduce(exp_f[:, :], below[:, :, :], AX.X, ALU.add))
            ch.sync()
            ch(v.tensor_tensor(below[:, :, :], below[:, :, :], tadj[:, :].unsqueeze(1).broadcast_to([P, ETILES, E]), ALU.mult))
            ch.sync()
            ch(v.tensor_reduce(row_f[:, :], below[:, :, :], AX.X, ALU.add))
            ch(v.tensor_scalar(tab_expert[:, :], exp_f[:, :], float(E - 1), None, ALU.min))
            ch.sync()
            ch(v.tensor_tensor(tab_row[:, :], row_f[:, :], rows, ALU.add))
            ch.sync()
            v.sem_inc(tab_ready, 1)

        def sweep(n, zidx_ready, swept):
            sp.wait_ge(zidx_ready, 1)
            for e in range(E):
                row = sp.value_load(zidx[0:1, e:e + 1], min_val=0, max_val=E * REG - P)
                sp.dma_start(xg[n][bass.ds(row, P), :], no_rows[e * P:(e + 1) * P, :]).then_inc(swept, 16)

        def expert_sems(n):
            names = ("rowsT_made", "rowsT_ready", "ug_made", "silu_ready", "h_ready", "hT_made", "hT_ready",
                     "y_made", "y_ready", "told")
            sems = {k: sem(f"ex{n}_{k}") for k in names}
            sems["n"] = n
            sems["in"] = [sem(f"ex{n}_in{u}") for u in range(4)]
            sems["stored"] = [sem(f"ex{n}_stored{u}") for u in range(4)]
            return sems

        def turns_of_tiles(eng, step):
            turns = ETILES // 8
            for u in range(8):
                step(u, u, 0)
            with eng.Fori(1, turns - 1) as turn:
                for u in range(8):
                    step(turn * 8 + u, u, turn)
            for u in range(8):
                step((turns - 1) * 8 + u, u, turns - 1)

        def exists(j, ahead):
            return not isinstance(j, int) or 0 <= j + ahead < ETILES

        def used(eng, semaphore, j, ahead):
            if not isinstance(j, int) or j + ahead >= 2:
                eng.wait_ge(semaphore, j + (ahead - 1))

        def experts_pe(s, tab_ready):
            regs = [pe.alloc_register(f"expert{s['n']}_{w}") for w in range(8)]

            def rows_T(j, u, turn, ahead):
                at = (u + ahead) % 4
                pe.wait_ge(s["in"][at], turn * 32 + ((u + ahead) // 4) * 16 + 16)
                used(pe, s["rowsT_ready"], j, ahead)
                pe.transpose(B[at % 2][:, 0:P], xr[:, at, 0:D], ident).then_inc(s["rowsT_made"], 1)

            def up(j, u, ahead, expert):
                at = (u + ahead) % 2
                pe.wait_ge(s["rowsT_ready"], j + (ahead + 1))
                used(pe, s["h_ready"], j, ahead)
                pe.matmul(B[2 + at][:, :], xrT[:, at, :], WUG_[:, bass.ds(expert * (2 * F), 2 * F)], start=True, stop=True)\
                    .then_inc(s["ug_made"], 1)

            def hidden_T(j, u):
                pe.wait_ge(s["h_ready"], j + 1)
                used(pe, s["hT_ready"], j, 0)
                for k in range(2):
                    last = pe.transpose(B[4 + u % 2][:, k * P:(k + 1) * P], hh[:, u % 2, k * P:(k + 1) * P], ident)
                last.then_inc(s["hT_made"], 1)

            def down(j, u, behind, expert):
                at = (u - behind) % 2
                pe.wait_ge(s["hT_ready"], j + (1 - behind))
                used(pe, s["y_ready"], j, -behind)
                for k in range(2):
                    last = pe.matmul(B[6 + at][:, 0:D], hT[:, at, k, :],
                                     WDT_[:, bass.ds(expert * (2 * D) + k * D, D)], start=k == 0, stop=k == 1)
                last.then_inc(s["y_made"], 1)

            def expert_of(u):
                return pe.snap(regs[u % 8], min_val=0, max_val=E - 1)

            def step(j, u, turn):
                if isinstance(j, int) and j == 0:
                    pe.reg_load(regs[0:4], tab_expert[0:1, 0:4])
                    rows_T(0, 0, 0, 0)
                    rows_T(0, 0, 0, 1)
                    up(0, 0, 0, expert_of(0))
                if exists(j, 2):
                    rows_T(j, u, turn, 2)
                if exists(j, 1):
                    up(j, u, 1, expert_of(u + 1))
                hidden_T(j, u)
                if exists(j, -1):
                    down(j, u, 1, expert_of(u - 1))
                if u % 4 == 1 and exists(j, 3):
                    at = (u + 3) % 8
                    pe.reg_load(regs[at:at + 4], tab_expert[0:1, bass.ds(j + 3, 4)])
                if isinstance(j, int) and j == ETILES - 1:
                    down(j, u, 0, expert_of(u))
            pe.wait_ge(tab_ready, 1)
            turns_of_tiles(pe, step)

        def experts_act(s):
            def silu(j, u, ahead):
                at = (u + ahead) % 2
                act.wait_ge(s["ug_made"], j + (ahead + 1))
                used(act, s["h_ready"], j, ahead)
                act.activation(sg[:, at, :], B[2 + at][:, F:2 * F], ACT.Silu).then_inc(s["silu_ready"], 1)

            def keep_y(j, u, turn, behind):
                at = (u - behind) % 4
                act.wait_ge(s["y_made"], j + (1 - behind))
                if not isinstance(j, int) or j - behind >= 4:
                    act.wait_ge(s["stored"][at], turn * 32 + ((u - behind) // 4) * 16)
                w = w_row[:, (u - behind) % 8:(u - behind) % 8 + 1]
                act.activation(yo[:, at, :], B[6 + at % 2][:, 0:D], ACT.Copy, scale=w).then_inc(s["y_ready"], 1)

            def step(j, u, turn):
                if isinstance(j, int) and j == 0:
                    silu(0, 0, 0)
                if exists(j, 1):
                    silu(j, u, 1)
                if exists(j, -1):
                    keep_y(j, u, turn, 1)
                if isinstance(j, int) and j == ETILES - 1:
                    keep_y(j, u, turn, 0)
            turns_of_tiles(act, step)

        def experts_dve(s):
            def keep_rows_T(j, u, turn, ahead):
                at, at4, at8 = (u + ahead) % 2, (u + ahead) % 4, (u + ahead) % 8
                if not isinstance(j, int) or j + ahead >= 8:
                    v.wait_ge(s["stored"][at4], turn * 32 + ((u + ahead) // 4 - 1) * 16)
                v.wait_ge(s["in"][at4], turn * 32 + ((u + ahead) // 4) * 16 + 16)
                flag_, col = is_2nd[:, at8:at8 + 1], lambda c: xr[:, at4, c:c + 1]
                v.tensor_scalar(flag_, col(C_E2), exp_f[:, bass.ds(j + ahead, 1)], None, ALU.is_equal).then_inc(s["told"], 1)
                v.wait_ge(s["told"], j + (ahead + 1))
                v.tensor_scalar(w_row[:, at8:at8 + 1], flag_, col(C_DW), col(C_W), ALU.mult, ALU.add)
                v.tensor_scalar(y_row[:, at8:at8 + 1], flag_, float(TOK), col(C_TOKEN), ALU.mult, ALU.add)
                v.wait_ge(s["rowsT_made"], j + (ahead + 1))
                used(v, s["ug_made"], j, ahead)
                v.tensor_copy(xrT[:, at, :], B[at][:, 0:P]).then_inc(s["rowsT_ready"], 1)

            def hidden(j, u, ahead):
                at = (u + ahead) % 2
                v.wait_ge(s["silu_ready"], j + (ahead + 1))
                used(v, s["hT_made"], j, ahead)
                v.tensor_tensor(hh[:, at, :], sg[:, at, :], B[2 + at][:, 0:F], ALU.mult).then_inc(s["h_ready"], 1)

            def step(j, u, turn):
                if isinstance(j, int) and j == 0:
                    keep_rows_T(0, 0, 0, 0)
                    keep_rows_T(0, 0, 0, 1)
                    hidden(0, 0, 0)
                if exists(j, 2):
                    keep_rows_T(j, u, turn, 2)
                if exists(j, 1):
                    hidden(j, u, 1)
                v.wait_ge(s["hT_made"], j + 1)
                used(v, s["y_made"], j, 0)
                v.tensor_copy(hT[:, u % 2, :, :].rearrange("p c k -> p (c k)"), B[4 + u % 2][:, 0:2 * P])\
                    .then_inc(s["hT_ready"], 1)
            turns_of_tiles(v, step)

        def experts_sp(s, n, r, tab_ready, swept):
            scattered_all(sp, r)
            sp.wait_ge(swept, 16 * E)
            sp.wait_ge(zeroed[n], 16)
            sp.wait_ge(tab_ready, 1)

            def step(j, u, turn):
                row = sp.value_load(tab_row[0:1, bass.ds(j, 1)], min_val=0, max_val=E * REG + SPARE - P)
                if not isinstance(j, int) or j >= 4:
                    sp.wait_ge(s["rowsT_ready"], j - 3)
                sp.dma_start(xr[:, u % 4, :], xg[n][bass.ds(row, P), :]).then_inc(s["in"][u % 4], 16)
            turns_of_tiles(sp, step)

        def experts_pool(s, n):
            def step(j, u, turn):
                wait_on(pool, s["y_ready"], j + 1)
                pool.indirect_dma_start(yg[n], bass.IndirectOffsetOnAxis(ap=y_row[:, u:u + 1], axis=0),
                                        yo[:, u % 4, :], None).then_inc(s["stored"][u % 4], 16)
            turns_of_tiles(pool, step)

        def all_stored(eng, s):
            for u in range(4):
                eng.wait_ge(s["stored"][u], 16 * (ETILES // 4))

        def load_results(n, g, q, arrived):
            for c in range(K2):
                sp.dma_start(G[:, q, c * GT:(c + 1) * GT, :],
                             yg[n][bass.ds(g * (GT * P) + c * TOK, GT * P), :].rearrange("(t p) d -> p t d", p=P)).then_inc(arrived, 16)

        def combine(ch, q, src, dst):
            for c in range(K2):
                ch(v.tensor_tensor(dst, src if c == 0 else dst, G[:, q, c * GT:(c + 1) * GT, :].rearrange("p t d -> p (t d)"), ALU.add))
                ch.sync()

        def per_head(a):
            return a.unsqueeze(2).broadcast_to([a.shape[0], HEADS, HD])

        def heads(a):
            return a.rearrange("p (h c) -> p h c", c=HD)

        m = {k: sem(f"mix_{k}") for k in (
            "combined", "norm_ready", "xh_ready", "xhT_made", "xhT_ready", "dt_made", "bcT_made", "Bt_ready",
            "bcT_ready", "dt_in", "dt_exp", "decay_ready", "cum_made", "exps_ready", "zx_made", "tanh_ready", "xw_ready",
            "cb_made", "Gm_ready", "Binf_ready", "wb_ready", "state_made", "S_ready", "y_made", "bound_ready",
            "y_scaled", "skip_ready", "skipped", "y_gated", "y_norm_ready", "yn_ready", "ynT_made", "yT_ready", "o_made", "o_used", "o_norm_ready", "on_ready", "x1_kept")}
        arrived_m = sem("arrived_m")

        def mix_dve(ch, r, g, c, general=False):
            if not general:
                wait_on(v, m["combined"], (c + 1) * K2)
            norm_stats(ch, "x1", tiles_of(X_, g), 1.0 + EPS, EPS * EPS)
            v.sem_inc(m["norm_ready"], 1)
            first, second = isinstance(g, int) and g == 0, isinstance(g, int) and g <= 1
            if not second and not general:
                route_choose(ch, r, g - 2)
            if not first:
                finish_norm(ch, c - 1)
            if not second:
                route_place(ch, r, g - 2, 0, g - 2)
            v.wait_ge(m["dt_made"], c + 1)
            for half in range(2):
                ch(v.tensor_tensor(dt_e[:, half * 4:(half + 1) * 4, :],
                                   B[6 + half][:, 0:4 * NDB].rearrange("p (t n) -> p t n", n=NDB)[:, :, 0:HEADS],
                                   dtb[:, :].unsqueeze(1).broadcast_to([P, 4, HEADS]), ALU.add))
            ch.sync()
            ch(v.tensor_scalar(dt_e[:, :, :], dt_e[:, :, :], 20.0, None, ALU.min))
            ch.sync()
            v.sem_inc(m["dt_in"], 1)
            v.wait_ge(m["dt_exp"], c + 1)
            ch(v.tensor_scalar(dt_e[:, :, :], dt_p[:, :, :], 0.12, None, ALU.min))
            ch.sync()
            ch(v.tensor_scalar(dt_q[:, :, :], dt_e[:, :, :], 2.0, None, ALU.add))
            ch.sync()
            ch(v.reciprocal(dt_q[:, :, :], dt_q[:, :, :]))
            ch.sync()
            ch(v.tensor_tensor(dt_z[:, :, :], dt_e[:, :, :], dt_q[:, :, :], ALU.mult))
            ch.sync()
            ch(v.tensor_tensor(dt_q[:, :, :], dt_z[:, :, :], dt_z[:, :, :], ALU.mult))
            ch.sync()
            ch(v.tensor_scalar(dt_p[:, :, :], dt_q[:, :, :], 2 / 7, 2 / 5, ALU.mult, ALU.add))
            ch.sync()
            ch(v.tensor_tensor(dt_p[:, :, :], dt_p[:, :, :], dt_q[:, :, :], ALU.mult))
            ch.sync()
            ch(v.scalar_tensor_tensor(out=dt_p[:, :, :], in0=dt_p[:, :, :], scalar=2 / 3, in1=dt_q[:, :, :], op0=ALU.add, op1=ALU.mult))
            ch.sync()
            ch(v.scalar_tensor_tensor(out=dt_p[:, :, :], in0=dt_p[:, :, :], scalar=2.0, in1=dt_z[:, :, :], op0=ALU.add, op1=ALU.mult))
            ch.sync()
            ch(v.tensor_scalar(dt_p[:, :, :], dt_p[:, :, :], 0.001, 0.1, ALU.max, ALU.min))
            ch.sync()
            ch(v.tensor_tensor(dt_p[:, :, :], dt_p[:, :, :], nAb[:, :].unsqueeze(1).broadcast_to([P, GT, HEADS]), ALU.mult))
            ch.sync()
            if not general:
                ch(v.scalar_tensor_tensor(out=ok_decay[:, :, :], in0=dt_p[:, :, :], scalar=DECAY_MIN, in1=ok_decay[:, :, :], op0=ALU.is_ge, op1=ALU.mult))
                ch(v.tensor_scalar(decay[:, :, :], dt_p[:, :, :], LOG_CAP, DECAY_MIN, ALU.min, ALU.max))
                ch.sync()
                v.sem_inc(m["decay_ready"], 1)
            if not first:
                finish_add(ch, g - 1, c - 1)

            def norm_last():
                if not first:
                    route_norm(ch, r, g - 1, tiles_of(X2_, g - 1))
            if general:
                norm_last()
                if not first:
                    route_choose(ch, r, g - 1)
                general_dve(ch, g, c)
            else:
                chunks_dve(ch, c, norm_last)
            gated = {} if general else {
                n: (lambda n=n: wait_on(v, m["y_gated"], c * GT + (n + 2))) for n in range(0, GT, 2)}
            norm_stats(ch, "y", [yb[:, t, :] for t in range(GT)], order=TILE, before=gated)
            v.sem_inc(m["y_norm_ready"], 1)

        def finish_norm(ch, c):
            v.wait_ge(m["o_made"], c + 1)
            for half in range(2):
                at = slice(half * 4, (half + 1) * 4)
                ch(v.tensor_scalar(ob[:, at, :].rearrange("p t d -> p (t d)"), B[6 + half][:, :], 10.0, -10.0, ALU.min, ALU.max))
            ch.sync()
            v.sem_inc(m["o_used"], 1)
            norm_stats(ch, "o", [ob[:, t, :] for t in range(GT)])
            v.sem_inc(m["o_norm_ready"], 1)

        def finish_add(ch, g, c):
            v.wait_ge(m["on_ready"], (c + 1) * GT)
            ch(v.tensor_tensor(ob[:, :, :], ob[:, :, :], now[:, :].unsqueeze(1).broadcast_to([P, GT, D]), ALU.mult))
            v.wait_ge(m["x1_kept"], c + 1)
            ch.sync()
            x2 = X2_[:, bass.ds(g * (GT * D), GT * D)]
            ch(v.tensor_tensor(x2, ob[:, :, :].rearrange("p t d -> p (t d)"), x2, ALU.add))
            ch.sync()

        def finish_act(c):
            act.wait_ge(m["o_norm_ready"], c + 1)
            for t in range(GT):
                normalise("o", t, ob[:, t, :], ob[:, t, :]).then_inc(m["on_ready"], 1)

        def chunks_dve(ch, c, meanwhile):
            v.wait_ge(m["Bt_ready"], c + 1)
            ch(v.tensor_reduce(Binf[:, :], Bt[:, :, :], AX.X, ALU.max, apply_absolute_value=True))
            ch.sync()
            v.sem_inc(m["Binf_ready"], 1)
            v.wait_ge(m["exps_ready"], c + 1)
            for n in range(2):
                gate(ch, c, n, TILE[n])
                weigh(n)
            v.wait_ge(m["cb_made"], c + 1)
            for half in range(2):
                at = slice(half * 4, (half + 1) * 4)
                v.tensor_tensor(Gm[:, at, :], B[6 + half][:, :].rearrange("p (t k) -> p t k", k=P),
                                tri.unsqueeze(1).broadcast_to([P, 4, P]), ALU.mult).then_inc(m["Gm_ready"], 1)
            ch(v.tensor_scalar(h_cum[:, :, :], e_cum[:, :, :], 0.5, None, ALU.mult))
            ch.sync()
            meanwhile()
            for n in range(GT):
                chunk(ch, c, n)
            v.wait_ge(m["bound_ready"], (c + 1) * GT)
            ch(v.scalar_tensor_tensor(out=ok_state[:, :, :], in0=decay[:, :, :], scalar=STATE_MAX, in1=ok_state[:, :, :],
                                      op0=ALU.is_le, op1=ALU.mult))

        def gate(ch, c, n, i):
            v.wait_ge(m["tanh_ready"], c * GT + (n + 1))
            ch(v.scalar_tensor_tensor(out=zs[:, i, :], in0=th[:, i, :], scalar=1.0, in1=B[2 + n % 2][:, 0:INNER], op0=ALU.add, op1=ALU.mult))

        def weigh(n):
            v.tensor_tensor(heads(xw[:, TILE[n], :]), heads(B[2 + n % 2][:, INNER:NZX]), per_head(e_neg[:, TILE[n], :]), ALU.mult)\
                .then_inc(m["xw_ready"], 1)

        def chunk(ch, c, n):
            (t, q), i = ITEMS[n], TILE[n]
            carried, y, k = B[q], B[4 + q], kmax[:, q]
            if n >= 2:
                v.wait_ge(m["bound_ready"], c * GT + (n - 1))
            if t < CHUNKS - 1:
                v.wait_ge(m["state_made"], c * CARRIED + (n + 1))
                new, S_t = carried[0:STATE, 0:INNER], S[:, q, t % 2, :]
                if t > 0:
                    ch(v.tensor_tensor(S_t, S[:, q, (t + 1) % 2, :], new, ALU.add))
                    new = S_t
            summed = ch.n
            v.wait_ge(m["y_made"], c * GT + (n + 1))
            ch(v.tensor_reduce(k, heads(y[:, INNER:2 * INNER]), AX.X, ALU.max))
            maximum = ch.n
            if t < CHUNKS - 1:
                ch.sync(summed)
                v.tensor_tensor(heads(S_t), heads(new), per_head(e_end[0:STATE, i, :]), ALU.mult).then_inc(m["S_ready"], 1)
            v.tensor_tensor(heads(yb[:, i, :]), heads(y[:, 0:INNER]), per_head(h_cum[:, i, :]), ALU.mult).then_inc(m["y_scaled"], 1)
            ch.sync(maximum)
            if t > 0:
                ch(v.tensor_tensor(k, k, carried[:, CARRY:CARRY + HEADS], ALU.add))
            with_carry = ch.n
            if n < GT - 2:
                gate(ch, c, n + 2, TILE[n + 2])
            ch.sync(with_carry)
            v.tensor_tensor(decay[:, i, :], k, e_cum[:, i, :], ALU.mult).then_inc(m["bound_ready"], 1)
            if n < GT - 2:
                weigh(n + 2)

        def skip_and_gate(c):
            def skip(n):
                pool.wait_ge(m["tanh_ready"], c * GT + (n + 1))
                pool.tensor_tensor(xd[:, TILE[n], :], xd[:, TILE[n], :], Dbc[:, :], ALU.mult).then_inc(m["skip_ready"], 1)
            skip(0)
            for n in range(GT):
                y = yb[:, TILE[n], :]
                pool.wait_ge(m["y_scaled"], c * GT + (n + 1))
                pool.wait_ge(m["skip_ready"], c * GT + (n + 1))
                pool.tensor_tensor(y, y, xd[:, TILE[n], :], ALU.add).then_inc(m["skipped"], 1)
                if n < GT - 1:
                    skip(n + 1)
                pool.wait_ge(m["skipped"], c * GT + (n + 1))
                pool.tensor_tensor(y, y, zs[:, TILE[n], :], ALU.mult).then_inc(m["y_gated"], 1)

        def mix_pe(r, g, c, general=False):
            first, second = isinstance(g, int) and g == 0, isinstance(g, int) and g <= 1
            for t in range(GT):
                pe.wait_ge(m["xh_ready"], c * GT + (t + 1))
                last = pe.transpose(B[2 + t // 4][:, (t % 4) * P:(t % 4 + 1) * P], xh[:, t, :], ident)
                if t % 4 == 3:
                    last.then_inc(m["xhT_made"], 1)
            pe.wait_ge(m["xhT_ready"], c * 2 + 2)
            after(pe, m["o_used"], c)
            for t in range(GT):
                last = pe.matmul(B[6 + t // 4][:, (t % 4) * NDB:(t % 4 + 1) * NDB], xhT[:, t, :], WIN[:, C_DT:C_DT + NDB],
                                 start=True, stop=True)
            last.then_inc(m["dt_made"], 1)
            if not second:
                route_pe_rank(r, g - 2)
            for half in range(2):
                pe.matmul(B[4 + half][:, :], WIN[:, C_BC:C_BC + 2 * STATE], xhT[:, half * 4:(half + 1) * 4, :].rearrange("p t k -> p (t k)"),
                          start=True, stop=True).then_inc(m["bcT_made"], 1)
            order = range(GT) if general else TILE
            for n in range(2):
                project(n, order[n])
            if general:
                pe.wait_ge(m["bcT_ready"], c + 1)
                pe.wait_ge(m["Bt_ready"], c + 1)
                if not first:
                    route_pe_transpose(r, g - 1, 0)
                    route_pe_all(r, g - 1)
                    pe.wait_ge(r["squared"], g * E)
                general_pe(c)
            else:
                pe.wait_ge(m["decay_ready"], c + 1)
                a = decay[:, :, :].rearrange("p t h -> p (t h)")
                pe.matmul(B[0][:, M_CUM:M_CUM + GT * HEADS], tri, a, start=True, stop=True)
                pe.matmul(B[0][:, M_TOT:M_TOT + GT * HEADS], ones[:, :], a, start=True, stop=True).then_inc(m["cum_made"], 1)
                pe.wait_ge(m["bcT_ready"], c + 1)
                pe.wait_ge(m["Bt_ready"], c + 1)
                for i in range(GT):
                    last = pe.matmul(B[6 + i // 4][:, (i % 4) * P:(i % 4 + 1) * P], BTs[:, i, :], CTs[:, i, :], start=True, stop=True)
                last.then_inc(m["cb_made"], 1)
                for n in range(GT):
                    chunk_pe(c, n)
                    if not first:
                        if n == T_AT:
                            route_pe_transpose(r, g - 1, 0)
                        for k in GATE_AT[n]:
                            route_pe_gate(r, g - 1, k)
            for i in range(GT):
                pe.wait_ge(m["yn_ready"], c * GT + (i + 1))
                for k in range(2):
                    last = pe.transpose(B[2 + 2 * (i // 4) + k][:, (i % 4) * P:(i % 4 + 1) * P], yb[:, i, k * P:(k + 1) * P], ident)
                if i % 4 == 3:
                    last.then_inc(m["ynT_made"], 1)
            for i in range(GT):
                pe.wait_ge(m["yT_ready"], c * 2 + (i // 4 + 1))
                for k in range(2):
                    last = pe.matmul(B[6 + i // 4][:, (i % 4) * P:(i % 4 + 1) * P], yT[:, k, i, :], WOUT[:, k, :], start=k == 0, stop=k == 1)
            last.then_inc(m["o_made"], 1)

        def chunk_pe(c, n):
            (t, q), i = ITEMS[n], TILE[n]
            if n >= 2:
                pe.wait_ge(m["bound_ready"], c * GT + (n - 1))
                pe.matmul(B[q][:, CARRY:CARRY + HEADS], lastrow, decay[:, TILE[n - 2], :], start=True, stop=True)
            pe.wait_ge(m["xw_ready"], c * GT + (n + 1))
            if t < CHUNKS - 1:
                pe.matmul(B[q][0:STATE, 0:INNER], Bt[:, i, :], xw[:, i, :], start=True, stop=True).then_inc(m["state_made"], 1)
            if n < 2:
                pe.wait_ge(m["Gm_ready"], c * 2 + (n + 1))
            pe.matmul(B[4 + q][:, 0:INNER], Gm[:, i, :], xw[:, i, :], start=True, stop=t == 0)
            if t > 0:
                pe.wait_ge(m["S_ready"], c * CARRIED + (n - 1))
                pe.matmul(B[4 + q][:, 0:INNER], CTs[:, i, :], S[:, q, (t - 1) % 2, :], start=False, stop=True)
            pe.wait_ge(m["wb_ready"], c * GT + (n + 1))
            pe.matmul(B[4 + q][:, INNER:2 * INNER], tri_bf[:, :], Wb[:, i, :], start=True, stop=True).then_inc(m["y_made"], 1)
            if n < GT - 2:
                project(n + 2, TILE[n + 2])

        def project(n, i):
            pe.matmul(B[2 + n % 2][:, :], xhT[:, i, :], WIN[:, 0:NZX], start=True, stop=True).then_inc(m["zx_made"], 1)

        def mix_act(r, g, c, general=False):
            first, second = isinstance(g, int) and g == 0, isinstance(g, int) and g <= 1
            act.wait_ge(m["norm_ready"], c + 1)
            for t in range(GT):
                normalise("x1", t, xh[:, t, :], tiles_of(X_, g)[t]).then_inc(m["xh_ready"], 1)
            for half in range(2):
                act.wait_ge(m["xhT_made"], c * 2 + (half + 1))
                act.activation(xhT[:, half * 4:(half + 1) * 4, :].rearrange("p t k -> p (t k)"), B[2 + half][:, :], ACT.Identity,
                               scale=vec[:, 0:1], bias=vec[:, 1:2]).then_inc(m["xhT_ready"], 1)
            if not second:
                route_act_exp(r, g - 2)
            if not first:
                finish_act(c - 1)
            act.wait_ge(m["dt_in"], c + 1)
            act.activation(dt_p[:, :, :], dt_e[:, :, :], ACT.Exp).then_inc(m["dt_exp"], 1)
            for half in range(2):
                last = act.activation(Bt[:, half * 4:(half + 1) * 4, :],
                                      B[6 + half][:, 0:4 * NDB].rearrange("p (t n) -> p t n", n=NDB)[:, :, HEADS:NDB], ACT.Copy)
            last.then_inc(m["Bt_ready"], 1)
            for half in range(2):
                act.wait_ge(m["bcT_made"], c * 2 + (half + 1))
                at = slice(half * 4, (half + 1) * 4)
                act.activation(BTs[:, at, :].rearrange("p t k -> p (t k)"), B[4 + half][0:STATE, :], ACT.Copy)
                last = act.activation(CTs[:, at, :].rearrange("p t k -> p (t k)"), B[4 + half][STATE:2 * STATE, :], ACT.Copy)
            last.then_inc(m["bcT_ready"], 1)
            if not general:
                for n in range(2):
                    tanh_z(c, n, TILE[n])
            if general:
                if not first:
                    route_act_rows(r, g - 1, 0, g - 1, tiles_of(X2_, g - 1))
                    route_act_T(r, g - 1)
                    for k in range(E):
                        route_act_square(r, g - 1, k)
                general_act(c)
            else:
                act.wait_ge(m["cum_made"], c + 1)
                cum = B[0][:, M_CUM:M_CUM + 2 * GT * HEADS].rearrange("p (k t h) -> p k t h", k=2, h=HEADS)
                act.activation(e_neg[:, :, :], cum[:, 0], ACT.Exp, scale=-1.0)
                act.activation(e_cum[:, :, :], cum[:, 0], ACT.Exp)
                act.activation(e_end[:, :, :], cum[:, 1], ACT.Exp).then_inc(m["exps_ready"], 1)
                act.wait_ge(m["Binf_ready"], c + 1)
                for n in range(GT):
                    act.wait_ge(m["xw_ready"], c * GT + (n + 1))
                    act.activation(Wb[:, TILE[n], :], xw[:, TILE[n], :], ACT.Abs, scale=Binf[:, TILE[n]:TILE[n] + 1])\
                        .then_inc(m["wb_ready"], 1)
                    if n < GT - 2:
                        tanh_z(c, n + 2, TILE[n + 2])
                    if not first:
                        if n in ROWS_AT:
                            route_act_rows(r, g - 1, 0, g - 1, tiles_of(X2_, g - 1), ROWS_AT[n])
                        if n == T_AT:
                            route_act_T(r, g - 1)
                        for k in GATE_AT[n]:
                            route_act_square(r, g - 1, k)
            act.wait_ge(m["y_norm_ready"], c + 1)
            for i in range(GT):
                normalise("y", i, yb[:, i, :], yb[:, i, :]).then_inc(m["yn_ready"], 1)
            for half in range(2):
                act.wait_ge(m["ynT_made"], c * 2 + (half + 1))
                for k in range(2):
                    last = act.activation(yT[:, k, half * 4:(half + 1) * 4, :].rearrange("p t j -> p (t j)"), B[2 + 2 * half + k][:, :],
                                          ACT.Identity, scale=vec[:, 2 + k:3 + k], bias=vec[:, 4 + k:5 + k])
                last.then_inc(m["yT_ready"], 1)

        def tanh_z(c, n, i):
            act.wait_ge(m["zx_made"], c * GT + (n + 1))
            act.activation(th[:, i, :], B[2 + n % 2][:, 0:INNER], ACT.Tanh, scale=0.5)
            act.activation(xd[:, i, :], B[2 + n % 2][:, INNER:NZX], ACT.Copy).then_inc(m["tanh_ready"], 1)

        def make_x1(g):
            wait_on(pool, arrived_m, (g + 1) * (16 * K2))
            x1 = X_[:, bass.ds(g * (GT * D), GT * D)]
            for c in range(K2):
                pool.tensor_tensor(x1, x1, G[:, 0, c * GT:(c + 1) * GT, :].rearrange("p t d -> p (t d)"), ALU.add)\
                    .then_inc(m["combined"], 1)
                if c == 0:
                    wait_on(pool, m["combined"], g * K2 + 1)

        def keep_x1(g, c):
            pool.wait_ge(m["xh_ready"], (c + 1) * GT)
            pool.tensor_tensor(X2_[:, bass.ds(g * (GT * D), GT * D)].rearrange("p (t d) -> p t d", d=D),
                               X_[:, bass.ds(g * (GT * D), GT * D)].rearrange("p (t d) -> p t d", d=D),
                               nob[:, :].unsqueeze(1).broadcast_to([P, GT, D]), ALU.add).then_inc(m["x1_kept"], 1)

        def last_pe(r, g):
            route_pe_rank(r, g - 1)
            route_pe_transpose(r, g, 1)
            for t in range(GT):
                route_pe_gate(r, g, t)
            route_pe_rank(r, g)

        def last_act(r, g, c):
            route_act_exp(r, g - 1)
            finish_act(c)
            route_act_rows(r, g, 1, 0, tiles_of(X2_, g))
            route_act_T(r, g)
            for k in range(E):
                route_act_square(r, g, k)
            route_act_exp(r, g)

        def last_dve(ch, r, g, c):
            if c < GROUPS:
                route_choose(ch, r, g - 1)
            finish_norm(ch, c)
            route_place(ch, r, g - 1, 0, g - 1)
            finish_add(ch, g, c)
            route_norm(ch, r, g, tiles_of(X2_, g))
            route_choose(ch, r, g)
            route_place(ch, r, g, 1, 0)

        gen = {k: sem(f"general_{k}") for k in (
            "log_ready", "decay_made", "tile_ready", "T_made", "c_made", "bc_ready", "bc_stored", "block_in", "block_used",
            "scanned", "y_made", "flag_sum", "flag_ready")}
        bc_rows = nc.dram_tensor("bc_rows", (1, SQ * SEQ * 2 * STATE), F32).ap()
        xs_T = G[:, 1, 0:GT].rearrange("p (c a) d -> p c (a d)", c=2)
        da_T = G[:, 1, GT:2 * GT].rearrange("p (c a) d -> p c (a d)", c=2)
        ys_T = xT[:, :].rearrange("p (c n) -> p c n", c=2)
        decay_w = G[:, 0].rearrange("p (t a) d -> p t (a d)", a=2)
        bc = ob
        bc_all = sq[:, 1].rearrange("p j n -> p (j n)")

        def general_dve(ch, g, c):
            ch(v.tensor_scalar(decay[:, :, :], dt_p[:, :, :], LOG_CAP, None, ALU.min))
            ch.sync()
            v.sem_inc(gen["log_ready"], 1)
            v.wait_ge(gen["c_made"], g + 1)
            v.wait_ge(m["Bt_ready"], c + 1)
            ch(v.tensor_copy(bc[:, :, 0:STATE], Bt[:, :, :]))
            ch(v.tensor_copy(bc[:, :, STATE:2 * STATE], B[6][:, 0:GT * STATE].rearrange("p (t n) -> p t n", n=STATE)))
            ch.sync()
            v.sem_inc(gen["bc_ready"], 1)
            v.wait_ge(gen["decay_made"], g + 1)
            for q in range(SQ):
                general_sequence(ch, g, c, q)

        def general_sequence(ch, g, c, q):
            seq, blocks = g * SQ + q, SEQ // BLOCK
            for i in range(q * CHUNKS, (q + 1) * CHUNKS):
                gate(ch, c, i, i)
                ch(v.tensor_tensor(xd[:, i, :], xd[:, i, :], Dbc[:, :], ALU.mult))
                ch.sync()
                ch(v.tensor_copy(heads(decay_w[:, i, :]), per_head(e_cum[:, i, :])))
                ch(v.tensor_copy(xw[:, i, :], B[2 + i % 2][:, INNER:NZX]))
                ch.sync()
                v.sem_inc(m["xw_ready"], 1)
            v.wait_ge(gen["T_made"], seq + 1)
            for k in range(2):
                ch(v.tensor_copy(xs_T[:, k, :], B[4 + k][:, :]))
                ch(v.tensor_copy(da_T[:, k, :], B[7 * k][:, :]))
            ch(v.memset(state, 0.0))
            ch.restart()
            with v.Fori(0, blocks) as blk:
                wait_on(v, gen["block_in"], seq * (16 * blocks) + (blk * 16 + 16))
                with v.Fori(0, BLOCK) as tt:
                    def over_n(a):
                        return a[:, :, bass.ds(blk * BLOCK + tt, 1)].broadcast_to([P, 2, STATE])

                    def over_c(at):
                        return bc_all[:, bass.ds(tt * (2 * STATE) + at, STATE)].unsqueeze(1).broadcast_to([P, 2, STATE])
                    ch(v.tensor_tensor(step_u, over_c(0), over_n(xs_T), ALU.mult))
                    ch(v.tensor_tensor(state, state, over_n(da_T), ALU.mult))
                    ch.sync()
                    ch(v.tensor_tensor(state, state, step_u, ALU.add))
                    ch.sync()
                    ch(v.tensor_scalar(state, state, 10.0, -10.0, ALU.min, ALU.max))
                    ch.sync()
                    ch(v.tensor_tensor(step_u, state, over_c(STATE), ALU.mult))
                    ch.sync()
                    ch(v.tensor_reduce(ys_T[:, :, bass.ds(blk * BLOCK + tt, 1)], step_u, AX.X, ALU.add))
                    ch.restart()
                v.sem_inc(gen["block_used"], 1)
            v.sem_inc(gen["scanned"], 1)
            v.wait_ge(gen["y_made"], seq + 1)
            for t in range(CHUNKS):
                i = q * CHUNKS + t
                ch(v.tensor_scalar(yb[:, i, :], B[4 + t // 2][:, (t % 2) * INNER:(t % 2 + 1) * INNER], 0.5, None, ALU.mult))
                ch.sync()
                ch(v.tensor_tensor(yb[:, i, :], yb[:, i, :], xd[:, i, :], ALU.add))
                ch.sync()
                ch(v.tensor_tensor(yb[:, i, :], yb[:, i, :], zs[:, i, :], ALU.mult))
            ch.sync()

        def general_pe(c):
            g = c - GROUPS
            pe.wait_ge(gen["log_ready"], g + 1)
            for i in range(GT):
                last = pe.matmul(B[6][:, i * STATE:(i + 1) * STATE], xhT[:, i, :],
                                 WIN[:, C_BC + STATE:C_BC + 2 * STATE], start=True, stop=True)
            last.then_inc(gen["c_made"], 1)
            for q in range(SQ):
                seq = g * SQ + q
                if q > 0:
                    pe.wait_ge(m["xw_ready"], c * GT + (q * CHUNKS + 1))
                for t in range(CHUNKS):
                    i = q * CHUNKS + t
                    pe.wait_ge(m["xw_ready"], c * GT + (i + 1))
                    if i < GT - 2:
                        project(i + 2, i + 2)
                    for k in range(2):
                        part = slice(k * P, (k + 1) * P)
                        pe.transpose(B[4 + k][:, t * P:(t + 1) * P], xw[:, i, part], ident)
                        last = pe.transpose(B[7 * k][:, t * P:(t + 1) * P], decay_w[:, i, part], ident)
                last.then_inc(gen["T_made"], 1)
                pe.wait_ge(gen["scanned"], seq + 1)
                for t in range(CHUNKS):
                    for k in range(2):
                        at = (t % 2) * INNER + k * P
                        last = pe.transpose(B[4 + t // 2][:, at:at + P], ys_T[:, k, t * P:(t + 1) * P], ident)
                last.then_inc(gen["y_made"], 1)

        def general_act(c):
            g = c - GROUPS
            act.wait_ge(gen["log_ready"], g + 1)
            act.activation(e_cum[:, :, :], decay[:, :, :], ACT.Exp).then_inc(gen["decay_made"], 1)
            for i in range(GT):
                tanh_z(c, i, i)

        def general_sp(g):
            blocks = SQ * SEQ // BLOCK
            wait_on(sp, gen["bc_ready"], g + 1)
            sp.dma_start(bc_rows.rearrange("o (t p n) -> (o p) t n", p=P, n=2 * STATE), bc[:, :, :]).then_inc(gen["bc_stored"], 16)
            wait_on(sp, gen["bc_stored"], g * 16 + 16)

            def block_in(blk):
                sp.dma_start(bc_all, bc_rows[:, bass.ds(blk * (BLOCK * 2 * STATE), BLOCK * 2 * STATE)]
                             .broadcast_to([P, BLOCK * 2 * STATE])).then_inc(gen["block_in"], 16)
            block_in(0)
            with sp.Fori(1, blocks) as blk:
                sp.wait_ge(gen["block_used"], g * blocks + blk)
                block_in(blk)

        def flagged(eng):
            eng.wait_ge(gen["flag_ready"], 1)
            return eng.value_load(flag[0:1, 0:1], min_val=0, max_val=1) > 0

        r1, e1 = route_sems(1, SLOTS, (4, 5), xn), expert_sems(1)
        tab1, zidx1 = sem("tab1_ready"), sem("zidx1_ready")
        (r2, r3), e2 = [route_sems(n, 2, (6, 7), (xn[0], row_last)) for n in (2, 3)], expert_sems(2)
        tab2, zidx2 = sem("tab2_ready"), sem("zidx2_ready")
        arrived_f = [sem(f"arrived_f{q}") for q in range(2)]
        combined_f, stored_f = sem("combined_f"), [sem(f"stored_f{q}") for q in range(2)]

        @block.sync
        def _(_e):
            part = [slice(k * TILES // 4, (k + 1) * TILES // 4) for k in range(4)]
            x_tiles = x.rearrange("(n p) d -> p n d", p=P)
            sp.dma_start(cst[:, :], consts).then_inc(loaded_first, 16)
            sp.dma_start(X[:, part[0], :], x_tiles[:, part[0], :]).then_inc(loaded_x[0], 16)
            sp.dma_start(WAT[:, :], wA_T).then_inc(loaded_first, 16)
            for k in range(1, 4):
                sp.dma_start(X[:, part[k], :], x_tiles[:, part[k], :]).then_inc(loaded_x[k], 16)
            sp.dma_start(WA, wA).then_inc(loaded, 16)
            sp.dma_start(WBT, wB_T).then_inc(loaded, 16)
            sp.dma_start(WUG[:, :, 0:F], wUp_T).then_inc(loaded, 16)
            sp.dma_start(WDT[:, :, :, :], wDn_T).then_inc(loaded, 16)
            sp.dma_start(vec[:, :], vecs).then_inc(loaded, 16)
            for dst, src in ((nAb, A_log), (dtb, dt_bias), (Dh, Dparam), (now, no_w), (nob, no_b)):
                sp.dma_start(dst[:, :], src.broadcast_to([P, src.shape[1]])).then_inc(loaded, 16)
            sp.dma_start(WIN[:, :], in_T).then_inc(loaded, 16)
            sp.dma_start(WOUT[:, :, :], out_T).then_inc(loaded, 16)
            for n in range(2):
                sp.dma_start(xg[n][E * REG:E * REG + SPARE, :], no_rows[SPARE:2 * SPARE, :])\
                    .then_inc(zeroed[n], 16)
            sweep(0, zidx1, swept[0])
            experts_sp(e1, 0, r1, tab1, swept[0])
            all_stored(sp, e1)
            load_results(0, 0, 0, arrived_m)
            with sp.Fori(1, GROUPS) as g:
                sp.wait_ge(m["combined"], g * K2)
                load_results(0, g, 0, arrived_m)
            with sp.If(flagged(sp)):
                with sp.Fori(0, GROUPS) as g:
                    general_sp(g)
            sweep(1, zidx2, swept[1])
            experts_sp(e2, 1, r2, tab2, swept[1])

            all_stored(sp, e2)
            for q in range(2):
                load_results(1, q, q, arrived_f[q])
            with sp.Fori(1, GROUPS // 2) as turn:
                for q in range(2):
                    sp.wait_ge(combined_f, turn * 2 + (q - 1))
                    load_results(1, turn * 2 + q, q, arrived_f[q])

        @block.vector
        def _(_e):
            ch = Chain(v, dve_own)
            ch(v.memset(ones_bf[:, :], 1.0))
            ch(v.memset(zeros_bf[:, :], 0.0))
            ch(v.memset(ones[:, :], 1.0))
            ch(v.memset(ok_state[:, :, :], 1.0))
            ch(v.memset(ok_decay[:, :, :], 1.0))
            v.wait_ge(loaded_first, 16 * 2)
            ch(v.tensor_copy(strict_bf[:, :], cst[:, C_STRICT:C_STRICT + P]))
            ch(v.tensor_copy(tri_bf[:, :], tri))
            start_counts(ch)
            ch.restart()
            v.sem_inc(masks_ready, 1)

            def norm_in(g):
                if g % 2 == 0:
                    v.wait_ge(loaded_x[g // 2], 16)
                route_norm(ch, r1, g, tiles_of(X_, g))
            norm_in(0)
            for g in range(GROUPS):
                if g < GROUPS - 1:
                    norm_in(g + 1)
                route_choose(ch, r1, g)
                route_place(ch, r1, g, g % SLOTS, g // SLOTS)
                ch.restart()
            tables(ch, tab1, zidx1)
            v.wait_ge(A_exp, 1)
            ch(v.tensor_scalar(nAb[:, :], nAb[:, :], -1.0, None, ALU.mult))
            ch(v.tensor_scalar(Dh[:, :], Dh[:, :], 0.5, None, ALU.mult))
            ch.sync()
            ch(v.tensor_copy(heads(Dbc[:, :]), per_head(Dh[:, :])))
            ch.restart()
            experts_dve(e1)
            start_counts(ch)
            ch.sync()
            for g in range(3):
                mix_dve(ch, r2, g, g)
                ch.restart()
            with v.Fori(3, GROUPS) as g:
                mix_dve(ch, r2, g, g)
                ch.restart()
            last_dve(ch, r2, GROUPS - 1, GROUPS - 1)
            ch(v.tensor_tensor(bnd[:, :, :], ok_state[:, :, :], ok_decay[:, :, :], ALU.mult))
            ch.sync()
            ch(v.tensor_reduce(ok_all[:, :], bnd[:, :, :].rearrange("p t h -> p (t h)"), AX.X, ALU.min))
            ch.sync()
            v.sem_inc(gen["flag_sum"], 1)
            v.wait_ge(gen["flag_sum"], 2)
            ch(v.tensor_scalar(flag[:, :], B[7][:, 0:1], P - 0.5, None, ALU.is_lt))
            ch.restart()
            v.sem_inc(gen["flag_ready"], 1)
            with v.If(flagged(v)):
                scattered_all(v, r2)
                again = Chain(v, dve_own)
                start_counts(again)
                again.restart()
                for g in range(3):
                    mix_dve(again, r3, g, g + GROUPS, True)
                    again.restart()
                with v.Fori(3, GROUPS) as g:
                    mix_dve(again, r3, g, g + GROUPS, True)
                    again.restart()
                last_dve(again, r3, GROUPS - 1, 2 * GROUPS - 1)
                again.restart()
            tables(ch, tab2, zidx2)
            ch.restart()
            experts_dve(e2)

            def combine_last(turn):
                for q in range(2):
                    g = turn * 2 + q
                    v.wait_ge(arrived_f[q], (turn + 1) * (16 * K2))
                    after(v, stored_f[q], turn * 16)
                    combine(ch, q, X2_[:, bass.ds(g * (GT * D), GT * D)], fin[:, q, :, :].rearrange("p t d -> p (t d)"))
                    v.sem_inc(combined_f, 1)
                ch.restart()
            combine_last(0)
            with v.Fori(1, GROUPS // 2) as turn:
                combine_last(turn)

        @block.tensor
        def _(_e):
            pe.wait_ge(loaded_first, 16 * 2)
            pe.wait_ge(masks_ready, 1)

            for g in range(GROUPS + 1):
                if g < GROUPS:
                    route_pe_transpose(r1, g, g % SLOTS)
                for t in range(GT):
                    if t == 5 and g > 0:
                        route_pe_rank(r1, g - 1)
                    if g < GROUPS:
                        route_pe_gate(r1, g, t)
            pe.wait_ge(loaded, 16 * LOADS)
            for e in range(E):
                if e >= 4:
                    pe.wait_ge(wab_kept, e - 3)
                pe.matmul(B[2 + e % 4][:, 0:F], WA[:, e * D:(e + 1) * D], WBT[:, e * F:(e + 1) * F], start=True, stop=True)\
                    .then_inc(wab_ready, 1)
            pe.wait_ge(wab_kept, E)
            experts_pe(e1, tab1)
            for g in range(3):
                mix_pe(r2, g, g)
            with pe.Fori(3, GROUPS) as g:
                mix_pe(r2, g, g)
            last_pe(r2, GROUPS - 1)
            pe.wait_ge(gen["flag_sum"], 1)
            pe.matmul(B[7][:, 0:1], ones[:, :], ok_all[:, :], start=True, stop=True).then_inc(gen["flag_sum"], 1)
            with pe.If(flagged(pe)):
                for g in range(3):
                    mix_pe(r3, g, g + GROUPS, True)
                with pe.Fori(3, GROUPS) as g:
                    mix_pe(r3, g, g + GROUPS, True)
                last_pe(r3, GROUPS - 1)
            experts_pe(e2, tab2)

        @block.scalar
        def _(_e):
            for g in range(GROUPS + 1):
                if g < GROUPS:
                    route_act_rows(r1, g, g % SLOTS, g // SLOTS, tiles_of(X_, g))
                    route_act_T(r1, g)
                for k in range(E):
                    if k == 2 and g > 0:
                        route_act_exp(r1, g - 1)
                    if g < GROUPS:
                        route_act_square(r1, g, k)
            act.wait_ge(loaded, 16 * LOADS)
            act.activation(nAb[:, :], nAb[:, :], ACT.Exp).then_inc(A_exp, 1)
            for e in range(E):
                act.wait_ge(wab_ready, e + 1)
                act.activation(WUG[:, e, F:2 * F], B[2 + e % 4][:, 0:F], ACT.Copy).then_inc(wab_kept, 1)
            experts_act(e1)
            for g in range(3):
                mix_act(r2, g, g)
            with act.Fori(3, GROUPS) as g:
                mix_act(r2, g, g)
            last_act(r2, GROUPS - 1, GROUPS - 1)
            with act.If(flagged(act)):
                scattered_all(act, r2)
                for g in range(3):
                    mix_act(r3, g, g + GROUPS, True)
                with act.Fori(3, GROUPS) as g:
                    mix_act(r3, g, g + GROUPS, True)
                last_act(r3, GROUPS - 1, 2 * GROUPS - 1)
            experts_act(e2)

        @block.gpsimd
        def _(_e):
            for g in range(GROUPS):
                route_pool(r1, 0, g, g % SLOTS)
            experts_pool(e1, 0)
            make_x1(0)

            def turn_of_mixer(g):
                if not (isinstance(g, int) and g == GROUPS - 1):
                    make_x1(g + 1)
                if not isinstance(g, int) or g >= 2:
                    route_pool(r2, 1, g - 2, 0)
                skip_and_gate(g)
                keep_x1(g, g)
            for g in range(2):
                turn_of_mixer(g)
            with pool.Fori(2, GROUPS - 1) as g:
                turn_of_mixer(g)
            turn_of_mixer(GROUPS - 1)
            route_pool(r2, 1, GROUPS - 2, 0)
            route_pool(r2, 1, GROUPS - 1, 1)
            with pool.If(flagged(pool)):
                for g in range(2):
                    keep_x1(g, g + GROUPS)
                with pool.Fori(2, GROUPS) as g:
                    keep_x1(g, g + GROUPS)
                    route_pool(r3, 1, g - 2, 0)
                route_pool(r3, 1, GROUPS - 2, 0)
                route_pool(r3, 1, GROUPS - 1, 1)
                scattered_all(pool, r3)
            experts_pool(e2, 1)

            def store(g, q):
                pool.wait_ge(combined_f, g + 1)
                pool.dma_start(out[bass.ds(g * (GT * P), GT * P), :].rearrange("(t p) d -> p t d", p=P), fin[:, q, :, :])\
                    .then_inc(stored_f[q], 16)
            with pool.Fori(0, GROUPS // 2) as turn:
                for q in range(2):
                    store(turn * 2 + q, q)
            for q in range(2):
                pool.wait_ge(stored_f[q], 16 * (GROUPS // 2))


def kernel(**inputs):
    import numpy as np
    import concourse.bacc as bacc
    from concourse.bass_utils import run_bass_kernel_spmd

    a = {k.replace("L0_", ""): np.asarray(i) for k, i in inputs.items()}
    cc = np.ascontiguousarray
    k, m = np.arange(P)[:, None], np.arange(P)[None, :]
    consts = np.zeros((P, C_N), np.float32)
    consts[:, C_ID:C_ID + P] = k == m
    consts[:, C_TRI:C_TRI + P] = k <= m
    consts[:, C_STRICT:C_STRICT + P] = k < m
    consts[P - 1, C_LAST:C_LAST + P] = 1
    consts[:, C_IOTA:C_IOTA + E] = np.arange(E)
    consts[:, C_REG:C_REG + E] = np.arange(E) * REG
    consts[:, C_TOK:C_TOK + GT] = np.arange(GT) * P + k
    consts[:, C_ROW:C_ROW + ETILES] = np.arange(ETILES) * P
    no_rows = np.zeros((2 * SPARE, ROW), np.float32)
    no_rows[:, C_E2] = -1
    no_rows[:, C_TOKEN] = K2 * TOK + np.arange(2 * SPARE)
    win = a["attn_in_proj_w"].T
    o = 2 * INNER
    win = np.concatenate([win[:, 0:o], win[:, o + 2 * STATE:], win[:, o:o + 2 * STATE]], axis=1)
    halves = lambda w: w.reshape(2, P).T
    arrays = {
        "x": cc(a["attn_x"].reshape(TOK, D)),
        "consts": consts,
        "no_rows": no_rows,
        "wA_T": cc(a["ffn_W_A"].transpose(2, 0, 1).reshape(D, E * R)),
        "wA": cc(a["ffn_W_A"].transpose(1, 0, 2).reshape(R, E * D)),
        "wB_T": cc(a["ffn_W_B"].transpose(2, 0, 1).reshape(R, E * F)),
        "wUp_T": cc(a["ffn_W_up"].transpose(2, 0, 1)),
        "wDn_T": cc(a["ffn_W_down"].transpose(2, 0, 1).reshape(2, P, E, D).transpose(1, 2, 0, 3)),
        "in_T": cc(win),
        "out_T": cc(a["attn_out_proj_w"].T.reshape(2, P, D).transpose(1, 0, 2)),
        "vecs": cc(np.concatenate([a["attn_ni_w"][:, None], a["attn_ni_b"][:, None],
                                   halves(a["attn_ln_w"]), halves(a["attn_ln_b"])], axis=1)),
        "dt_bias": cc(a["attn_dt_bias"].reshape(1, HEADS)),
        "A_log": cc(a["attn_A_log"].reshape(1, HEADS)),
        "Dparam": cc(a["attn_Dparam"].reshape(1, HEADS)),
        "no_w": cc(a["attn_no_w"].reshape(1, D)),
        "no_b": cc(a["attn_no_b"].reshape(1, D)),
    }
    nc = bacc.Bacc("TRN2", target_bir_lowering=False, num_devices=1)
    args = [nc.dram_tensor(n, v.shape, F32, kind="ExternalInput").ap() for n, v in arrays.items()]
    args.append(nc.dram_tensor("out", (TOK, D), F32, kind="ExternalOutput").ap())
    macaron(nc, *args)
    res = run_bass_kernel_spmd(nc, [arrays], core_ids=[0])
    return res.results[0]["out"].reshape(BATCH, SEQ, D)
```
